# Optimizing a Trainium2 kernel written in Bass

```python
import numpy as np
import jax
import jax.numpy as jnp

def _softmax(x, axis=-1):
    return jax.nn.softmax(x, axis=axis)

def _gelu(x):
    return jax.nn.gelu(x, approximate=True)

def _silu(x):
    return jax.nn.silu(x)

def _sigmoid(x):
    return jax.nn.sigmoid(x)

def _layernorm(x, axis=-1, eps=1e-05):
    m = jnp.mean(x, axis=axis, keepdims=True)
    v = jnp.var(x, axis=axis, keepdims=True)
    return (x - m) / jnp.sqrt(v + eps)

def _scatter_add(tgt, idx, src, axis=0):
    return tgt.at[idx].add(src)

def _segment_sum(src, seg, n):
    return jax.ops.segment_sum(src, seg, n)
kernel_name = 'mk_perceiver_d1_seqx_r8_0be8db'

def setup_inputs(seed: int=0):
    np.random.seed(seed)
    _w = jnp.asarray

    def _rec_inputs():
        import jax
        import jax.numpy as jnp
        _rk = jax.random.key(seed)
        x = -0.0003929 + 0.9999 * jax.random.normal(jax.random.fold_in(_rk, 1), (1, 64, 512), jnp.float32)
        _lenS = 64 - jax.random.randint(jax.random.fold_in(_rk, 7), (1,), 0, max(1, 64 // 4) + 1, jnp.int32)
        _lenS2 = 6272 - jax.random.randint(jax.random.fold_in(_rk, 8), (1,), 0, max(1, 6272 // 4) + 1, jnp.int32)
        _ctx_4096P = jax.random.normal(jax.random.fold_in(_rk, 11), (1, 16, 512), jnp.float32)
        _ctx_4096c = jax.random.dirichlet(jax.random.fold_in(_rk, 511), 0.3 * jnp.ones((16,), jnp.float32), (1, 6272))
        _ctx_4096t = jnp.einsum('bsk,bkd->bsd', _ctx_4096c, _ctx_4096P)
        _ctx_4096t = _ctx_4096t * jax.lax.rsqrt(jnp.mean(jnp.square(_ctx_4096t)) + 1e-12) * 0.953939
        ctx_4096 = 2.81802e-05 + 1.00001 * (_ctx_4096t + 0.3 * jax.random.normal(jax.random.fold_in(_rk, 611), (1, 6272, 512), jnp.float32))
        return (x, ctx_4096)
    x, ctx_4096 = _rec_inputs()

    def _L0_xattn_setup():
        import jax, jax.numpy as jnp
        import numpy as np
        HID = 512
        NHEAD = 32
        NKV = 8
        HDIM = 128
        G = NHEAD // NKV
        key = jax.random.key(seed)
        ks = jax.random.split(key, 6)
        s = 0.02
        B, L = (2, 256)
        return {'query': jax.random.normal(ks[0], (B, L, HID), jnp.float32), 'kv': jax.random.normal(ks[1], (B, L, HID), jnp.float32), 'Wq': jax.random.normal(ks[2], (HID, NHEAD * HDIM), jnp.float32) * s, 'bq': jnp.zeros((NHEAD * HDIM,), jnp.float32), 'Wkv': jax.random.normal(ks[3], (HID, 2 * NKV * HDIM), jnp.float32) * s, 'bkv': jnp.zeros((2 * NKV * HDIM,), jnp.float32), 'Wo': jax.random.normal(ks[4], (NHEAD * HDIM, HID), jnp.float32) * s, 'bo': jnp.zeros((HID,), jnp.float32)}
    _L0_xattn_all = _L0_xattn_setup()
    _L0_xattn_in = {k: v for k, v in _L0_xattn_all.items() if k in ('Wq', 'bq', 'Wkv', 'bkv', 'Wo', 'bo')}
    del _L0_xattn_all

    def _L0_attn_setup():
        import jax, jax.numpy as jnp
        import numpy as np
        NF4 = jnp.array([-1.0, -0.6961928009986877, -0.5250730514526367, -0.39491748809814453, -0.28444138169288635, -0.18477343022823334, -0.09105003625154495, 0.0, 0.07958029955625534, 0.16093020141124725, 0.24611230194568634, 0.33791524171829224, 0.44070982933044434, 0.5626170039176941, 0.7229568362236023, 1.0], dtype=jnp.float32)
        BLOCK = 64

        def _dequant(codes, scales):
            w = NF4[codes]
            O, I = w.shape
            w = w.reshape(O, I // BLOCK, BLOCK) * scales[:, :, None]
            return w.reshape(O, I)

        def _lin_lora(x, W, A, B):
            base = jnp.einsum('bsh,oh->bso', x, W)
            lora = jnp.einsum('bsr,or->bso', jnp.einsum('bsh,rh->bsr', x, A), B)
            return base + lora
        H, I, R, BT, S = (512, 1792, 16, 2, 256)
        key = jax.random.key(seed)
        ks = jax.random.split(key, 12)
        x = jax.random.normal(ks[0], (BT, S, H), jnp.float32)
        codes_attn = jax.random.randint(ks[1], (4, H, H), 0, 16, jnp.int32)
        scales_attn = jax.random.uniform(ks[2], (4, H, H // BLOCK), jnp.float32) * 0.02
        codes_gu = jax.random.randint(ks[3], (2, I, H), 0, 16, jnp.int32)
        scales_gu = jax.random.uniform(ks[4], (2, I, H // BLOCK), jnp.float32) * 0.02
        codes_down = jax.random.randint(ks[5], (H, I), 0, 16, jnp.int32)
        scales_down = jax.random.uniform(ks[6], (H, I // BLOCK), jnp.float32) * 0.02
        lora_A_h = jax.random.normal(ks[7], (6, R, H), jnp.float32) * 0.02
        lora_A_down = jax.random.normal(ks[8], (R, I), jnp.float32) * 0.02
        lora_B_attn = jax.random.normal(ks[9], (4, H, R), jnp.float32) * 0.02
        lora_B_gu = jax.random.normal(ks[10], (2, I, R), jnp.float32) * 0.02
        lora_B_down = jax.random.normal(ks[11], (H, R), jnp.float32) * 0.02
        return dict(x=x, codes_attn=codes_attn, scales_attn=scales_attn, codes_gu=codes_gu, scales_gu=scales_gu, codes_down=codes_down, scales_down=scales_down, lora_A_h=lora_A_h, lora_A_down=lora_A_down, lora_B_attn=lora_B_attn, lora_B_gu=lora_B_gu, lora_B_down=lora_B_down)
    _L0_attn_all = _L0_attn_setup()
    _L0_attn_in = {k: v for k, v in _L0_attn_all.items() if k in ('codes_attn', 'scales_attn', 'codes_gu', 'scales_gu', 'codes_down', 'scales_down', 'lora_A_h', 'lora_A_down', 'lora_B_attn', 'lora_B_gu', 'lora_B_down')}
    del _L0_attn_all

    def _L0_ffn_setup():
        import math
        import jax, jax.numpy as jnp
        import numpy as np
        SCALING = 16.0 / 32.0

        def real_fourier_orthogonal_multiply(c):
            n = c.shape[-1]
            sqrt_n = math.sqrt(n)
            pair_scale = math.sqrt(n / 2.0)
            max_f = (n - 1) // 2
            work = c.astype(jnp.float32)
            dc = (work[..., 0] * sqrt_n)[..., None].astype(jnp.complex64)
            cos = work[..., 1:1 + 2 * max_f:2] * pair_scale
            sin = work[..., 2:2 + 2 * max_f:2] * pair_scale
            mid = (cos - 1j * sin).astype(jnp.complex64)
            parts = [dc, mid]
            if n % 2 == 0:
                parts.append((work[..., -1] * sqrt_n)[..., None].astype(jnp.complex64))
            spectrum = jnp.concatenate(parts, axis=-1)
            return jnp.fft.irfft(spectrum, n=n, axis=-1).astype(c.dtype)
        key = jax.random.key(seed)
        ks = jax.random.split(key, 9)
        B, S, D_in, D_out, R0, R1, E = (4, 256, 512, 512, 32, 8, 3)
        x = jax.random.normal(ks[0], (B, S, D_in), dtype=jnp.float32)
        W_base = jax.random.normal(ks[1], (D_out, D_in), dtype=jnp.float32) * 0.02
        b_base = jax.random.normal(ks[2], (D_out,), dtype=jnp.float32) * 0.02
        enc0 = jax.random.normal(ks[3], (R0, D_in), dtype=jnp.float32) * 0.02
        enc1 = jax.random.normal(ks[4], (R1, D_in), dtype=jnp.float32) * 0.02
        coefs0 = jax.random.normal(ks[5], (E, D_out, R0), dtype=jnp.float32) * 0.02
        coefs1 = jax.random.normal(ks[6], (E, D_out, R1), dtype=jnp.float32) * 0.02
        mask0 = jax.random.randint(ks[7], (E, D_out, R0), 0, 2).astype(bool)
        mask1 = jax.random.randint(ks[8], (E, D_out, R1), 0, 2).astype(bool)
        return dict(x=x, W_base=W_base, b_base=b_base, enc0=enc0, enc1=enc1, coefs0=coefs0, coefs1=coefs1, mask0=mask0, mask1=mask1)
    _L0_ffn_all = _L0_ffn_setup()
    _L0_ffn_in = {k: v for k, v in _L0_ffn_all.items() if k in ('W_base', 'b_base', 'enc0', 'enc1', 'coefs0', 'coefs1', 'mask0', 'mask1')}
    del _L0_ffn_all
    return {'x': x, 'ctx_4096': ctx_4096, 'L0_xattn_Wq': _L0_xattn_in['Wq'], 'L0_xattn_bq': _L0_xattn_in['bq'], 'L0_xattn_Wkv': _L0_xattn_in['Wkv'], 'L0_xattn_bkv': _L0_xattn_in['bkv'], 'L0_xattn_Wo': _L0_xattn_in['Wo'], 'L0_xattn_bo': _L0_xattn_in['bo'], 'L0_attn_codes_attn': _L0_attn_in['codes_attn'], 'L0_attn_scales_attn': _L0_attn_in['scales_attn'], 'L0_attn_codes_gu': _L0_attn_in['codes_gu'], 'L0_attn_scales_gu': _L0_attn_in['scales_gu'], 'L0_attn_codes_down': _L0_attn_in['codes_down'], 'L0_attn_scales_down': _L0_attn_in['scales_down'], 'L0_attn_lora_A_h': _L0_attn_in['lora_A_h'], 'L0_attn_lora_A_down': _L0_attn_in['lora_A_down'], 'L0_attn_lora_B_attn': _L0_attn_in['lora_B_attn'], 'L0_attn_lora_B_gu': _L0_attn_in['lora_B_gu'], 'L0_attn_lora_B_down': _L0_attn_in['lora_B_down'], 'L0_ffn_W_base': _L0_ffn_in['W_base'], 'L0_ffn_b_base': _L0_ffn_in['b_base'], 'L0_ffn_enc0': _L0_ffn_in['enc0'], 'L0_ffn_enc1': _L0_ffn_in['enc1'], 'L0_ffn_coefs0': _L0_ffn_in['coefs0'], 'L0_ffn_coefs1': _L0_ffn_in['coefs1'], 'L0_ffn_mask0': _L0_ffn_in['mask0'], 'L0_ffn_mask1': _L0_ffn_in['mask1']}

def reference(x, ctx_4096, L0_xattn_Wq, L0_xattn_bq, L0_xattn_Wkv, L0_xattn_bkv, L0_xattn_Wo, L0_xattn_bo, L0_attn_codes_attn, L0_attn_scales_attn, L0_attn_codes_gu, L0_attn_scales_gu, L0_attn_codes_down, L0_attn_scales_down, L0_attn_lora_A_h, L0_attn_lora_A_down, L0_attn_lora_B_attn, L0_attn_lora_B_gu, L0_attn_lora_B_down, L0_ffn_W_base, L0_ffn_b_base, L0_ffn_enc0, L0_ffn_enc1, L0_ffn_coefs0, L0_ffn_coefs1, L0_ffn_mask0, L0_ffn_mask1):
    import jax
    import jax.numpy as jnp

    def _L0_xattn_ref(query, kv, Wq, bq, Wkv, bkv, Wo, bo):
        import jax, jax.numpy as jnp
        import numpy as np
        HID = 512
        NHEAD = 32
        NKV = 8
        HDIM = 128
        G = NHEAD // NKV
        B, L, _ = query.shape
        Lk = kv.shape[1]
        scale = jnp.asarray(1.0 / np.sqrt(HDIM), query.dtype)
        q = (query @ Wq + bq).reshape(B, L, NKV, G, HDIM)
        k_, v_ = jnp.split(kv @ Wkv + bkv, 2, axis=-1)
        k = k_.reshape(B, Lk, NKV, HDIM)
        v = v_.reshape(B, Lk, NKV, HDIM)
        scores = jnp.einsum('blkgd,bmkd->bkglm', q, k) * scale
        attn = jax.nn.softmax(scores, axis=-1)
        o = jnp.einsum('bkglm,bmkd->blkgd', attn, v).reshape(B, L, NHEAD * HDIM)
        return o @ Wo + bo

    def _L0_attn_ref(x, codes_attn, scales_attn, codes_gu, scales_gu, codes_down, scales_down, lora_A_h, lora_A_down, lora_B_attn, lora_B_gu, lora_B_down):
        import jax, jax.numpy as jnp
        import numpy as np
        NF4 = jnp.array([-1.0, -0.6961928009986877, -0.5250730514526367, -0.39491748809814453, -0.28444138169288635, -0.18477343022823334, -0.09105003625154495, 0.0, 0.07958029955625534, 0.16093020141124725, 0.24611230194568634, 0.33791524171829224, 0.44070982933044434, 0.5626170039176941, 0.7229568362236023, 1.0], dtype=jnp.float32)
        BLOCK = 64

        def _dequant(codes, scales):
            w = NF4[codes]
            O, I = w.shape
            w = w.reshape(O, I // BLOCK, BLOCK) * scales[:, :, None]
            return w.reshape(O, I)

        def _lin_lora(x, W, A, B):
            base = jnp.einsum('bsh,oh->bso', x, W)
            lora = jnp.einsum('bsr,or->bso', jnp.einsum('bsh,rh->bsr', x, A), B)
            return base + lora
        q = _lin_lora(x, _dequant(codes_attn[0], scales_attn[0]), lora_A_h[0], lora_B_attn[0])
        k = _lin_lora(x, _dequant(codes_attn[1], scales_attn[1]), lora_A_h[1], lora_B_attn[1])
        v = _lin_lora(x, _dequant(codes_attn[2], scales_attn[2]), lora_A_h[2], lora_B_attn[2])
        attn = (q + k + v) / 3.0
        o = _lin_lora(attn, _dequant(codes_attn[3], scales_attn[3]), lora_A_h[3], lora_B_attn[3])
        x1 = x + o
        g = _lin_lora(x1, _dequant(codes_gu[0], scales_gu[0]), lora_A_h[4], lora_B_gu[0])
        u = _lin_lora(x1, _dequant(codes_gu[1], scales_gu[1]), lora_A_h[5], lora_B_gu[1])
        h = jax.nn.silu(g) * u
        d = _lin_lora(h, _dequant(codes_down, scales_down), lora_A_down, lora_B_down)
        return x1 + d

    def _L0_ffn_ref(x, W_base, b_base, enc0, enc1, coefs0, coefs1, mask0, mask1):
        import math
        import jax, jax.numpy as jnp
        import numpy as np
        SCALING = 16.0 / 32.0

        def real_fourier_orthogonal_multiply(c):
            n = c.shape[-1]
            sqrt_n = math.sqrt(n)
            pair_scale = math.sqrt(n / 2.0)
            max_f = (n - 1) // 2
            work = c.astype(jnp.float32)
            dc = (work[..., 0] * sqrt_n)[..., None].astype(jnp.complex64)
            cos = work[..., 1:1 + 2 * max_f:2] * pair_scale
            sin = work[..., 2:2 + 2 * max_f:2] * pair_scale
            mid = (cos - 1j * sin).astype(jnp.complex64)
            parts = [dc, mid]
            if n % 2 == 0:
                parts.append((work[..., -1] * sqrt_n)[..., None].astype(jnp.complex64))
            spectrum = jnp.concatenate(parts, axis=-1)
            return jnp.fft.irfft(spectrum, n=n, axis=-1).astype(c.dtype)
        base = jnp.einsum('bsd,od->bso', x, W_base) + b_base
        e0 = jnp.einsum('bsd,rd->bsr', x, enc0)
        e1 = jnp.einsum('bsd,rd->bsr', x, enc1)
        w0 = coefs0 * mask0.astype(coefs0.dtype)
        w1 = coefs1 * mask1.astype(coefs1.dtype)
        decoded = jnp.einsum('bsr,eor->ebso', e0, w0) + jnp.einsum('bsr,eor->ebso', e1, w1)
        transformed = real_fourier_orthogonal_multiply(decoded)
        update = transformed.sum(axis=0)
        return base + update * SCALING
    x = x + _L0_xattn_ref(_layernorm(x, axis=-1), ctx_4096, L0_xattn_Wq, L0_xattn_bq, L0_xattn_Wkv, L0_xattn_bkv, L0_xattn_Wo, L0_xattn_bo)
    x = x + _L0_attn_ref(_layernorm(x, axis=-1), L0_attn_codes_attn, L0_attn_scales_attn, L0_attn_codes_gu, L0_attn_scales_gu, L0_attn_codes_down, L0_attn_scales_down, L0_attn_lora_A_h, L0_attn_lora_A_down, L0_attn_lora_B_attn, L0_attn_lora_B_gu, L0_attn_lora_B_down)
    x = x + _L0_ffn_ref(_layernorm(x, axis=-1), L0_ffn_W_base, L0_ffn_b_base, L0_ffn_enc0, L0_ffn_enc1, L0_ffn_coefs0, L0_ffn_coefs1, L0_ffn_mask0, L0_ffn_mask1)
    return x

_drawn_inputs = setup_inputs


def setup_inputs(seed=0):
    import zlib

    import numpy as np

    out = dict(_drawn_inputs(seed))
    spreads = {'L0_xattn_bq': (0.0, 0.8), 'L0_xattn_bkv': (0.0, 0.1), 'L0_xattn_bo': (0.0, 0.1)}
    factors = {'L0_xattn_Wq': 2.996,
     'L0_attn_scales_attn': 8.0,
     'L0_attn_scales_gu': 8.0,
     'L0_attn_scales_down': 8.0,
     'L0_attn_lora_A_h': 8.0,
     'L0_attn_lora_A_down': 8.0,
     'L0_attn_lora_B_attn': 8.0,
     'L0_attn_lora_B_gu': 8.0,
     'L0_attn_lora_B_down': 8.0,
     'L0_ffn_b_base': 200.0,
     'L0_ffn_enc0': 30.92,
     'L0_ffn_enc1': 62.312,
     'L0_ffn_coefs0': 30.048,
     'L0_ffn_coefs1': 63.744,
     'L0_ffn_W_base': 47.227}
    for name, (base, spread) in spreads.items():
        noise = np.random.default_rng([zlib.crc32(name.encode()), seed]).standard_normal(out[name].shape)
        drawn = base * np.exp(spread * noise) if base else spread * noise
        out[name] = jnp.asarray(drawn.astype(out[name].dtype))
    for name, factor in factors.items():
        out[name] = (out[name] * factor).astype(out[name].dtype)
    return out
```

```python
from contextlib import ExitStack

import numpy as np

import concourse.bass as bass
from concourse import mybir

ALU = mybir.AluOpType
ACT = mybir.ActivationFunctionType
AX_X = mybir.AxisListType.X
F32 = mybir.dt.float32
F32R = mybir.dt.float32r
I32 = mybir.dt.int32
U16 = mybir.dt.uint16
U8 = mybir.dt.uint8

P = 128
HID = 512
KT = HID // P
TOK = 64
KEYS = 6272
D = 128
NKV = 8
G = 4
NH = NKV * G
ROWS = G * TOK
RT = ROWS // P
CT = 7
CHUNK = CT * P
NCH = KEYS // CHUNK
HALF = CHUNK // 2
SCALE = float(1.0 / np.sqrt(D))
FFN = 1792
FT = FFN // P
RANK = 16
R0, R1, NEXP = 32, 8, 3
RR = R0 + R1
QBLK = 64
NF4 = [-1.0, -0.6961928009986877, -0.5250730514526367, -0.39491748809814453, -0.28444138169288635,
       -0.18477343022823334, -0.09105003625154495, 0.0, 0.07958029955625534, 0.16093020141124725,
       0.24611230194568634, 0.33791524171829224, 0.44070982933044434, 0.5626170039176941,
       0.7229568362236023, 1.0]
TW = 512
ATT_TILES = 4 * KT
GU_COLS = 2 * FFN // TW
GU_TILES = KT * GU_COLS
NT = ATT_TILES + GU_TILES + FT
EXTRA = NT - NCH * NKV
EPS = 1e-5
LOWEST = -3.0e38


def split_matmuls(nc, out, hi, lo, rhi, rlo, start=True, stop=True):
    nc.tensor.matmul(out, hi, rhi, start=start, stop=False)
    nc.tensor.matmul(out, hi, rlo, start=False, stop=False)
    return nc.tensor.matmul(out, lo, rhi, start=False, stop=stop)


def wait_apart(eng, sem, value, passed):
    eng.wait_ge(sem, value)
    eng.sem_inc(passed, 1)


def perceiver_block(nc, x, ctx_t, wq, bq, wkv, bk, bv, wo, bo, codes, scales, lora_a, lora_a_down, lora_b,
                    lora_b_down, w_base, b_base, enc, coefs, mask, fourier, ident_in, out):
    with ExitStack() as top:
        def sem(name):
            return top.enter_context(nc.semaphore(name))

        def sb(stack, name, shape, dt):
            return stack.enter_context(nc.sbuf_tensor(name, shape, dt))

        def psum(stack, name, shape):
            return stack.enter_context(nc.psum_tensor(name, shape, F32))

        weights = nc.dram_tensor("expanded_weights", [NT, P, TW], F32).ap()
        four_dram = nc.dram_tensor("folded_fourier", [RR, HID], F32).ap()

        ident = sb(top, "ident", [P, P], F32)
        acc = sb(top, "acc", [P, NKV, RT, D], F32)
        denom = sb(top, "denom", [P, NKV, RT], F32)
        maxes = sb(top, "maxes", [P, NKV, RT, 3], F32)
        bv_sb = sb(top, "bv_sb", [P, NKV], F32)

        phase1 = ExitStack()
        wkv_hi = sb(phase1, "wkv_hi", [P, KT, 2 * NKV * D], F32R)
        wkv_lo = sb(phase1, "wkv_lo", [P, KT, 2 * NKV * D], F32R)
        q_hi = sb(phase1, "q_hi", [P, NKV, ROWS], F32R)
        q_lo = sb(phase1, "q_lo", [P, NKV, ROWS], F32R)
        bk_sb = sb(phase1, "bk_sb", [P, NKV], F32)

        prologue(nc, top, x, wq, bq, wkv, bk, bv, coefs, mask, fourier, ident_in,
                 ident, acc, denom, maxes, bv_sb, bk_sb, four_dram, wkv_hi, wkv_lo, q_hi, q_lo, sem, sb, psum)
        attention(nc, ctx_t, codes, scales, weights, ident, acc, denom, maxes, bk_sb,
                  wkv_hi, wkv_lo, q_hi, q_lo, sem, sb, psum)
        phase1.close()
        tail(nc, wo, bo, weights, lora_a, lora_a_down, lora_b, lora_b_down, w_base, b_base, enc, out,
             ident, x, acc, denom, bv_sb, four_dram, sem, sb, psum)


def prologue(nc, top, x, wq, bq, wkv, bk, bv, coefs, mask, fourier, ident_in, ident, acc, denom, maxes,
             bv_sb, bk_sb, four_dram, wkv_hi, wkv_lo, q_hi, q_lo, sem, sb, psum):
    with ExitStack() as st:
        x_sb = sb(st, "x_in_sb", [TOK, HID], F32)
        w_four = sb(st, "w_four_out", [RR, HID], F32)
        xhat = sb(st, "xhat0", [TOK, HID], F32)
        stats = sb(st, "stats0", [TOK, 6], F32)
        mv = sb(st, "mv0", [TOK, 4], F32)
        xt = sb(st, "xt0", [P, KT, TOK], F32)
        bq_sb = sb(st, "bq_sb", [P, NH], F32)
        wq_sb = sb(st, "wq_sb", [P, 2, KT, TW], F32)
        wkv_st = sb(st, "wkv_st", [P, 2, 2 * NKV * D], F32)
        q_f = sb(st, "q_f", [P, 2, 8 * TOK], F32)
        co = sb(st, "co", [P, KT, NEXP, RR], F32)
        mk = sb(st, "mk", [P, KT, NEXP, RR], U8)
        cm = sb(st, "cm", [P, KT, NEXP, RR], F32)
        ws = sb(st, "ws", [P, KT, RR], F32)
        four = sb(st, "four", [P, KT, HID], F32)
        p_x = psum(st, "p_x", [P, KT, TOK])
        p_q = psum(st, "p_q", [P, 2, 8 * TOK])
        p_w = psum(st, "p_w", [RR, HID])

        x_in, vecs_in = sem("x_in"), sem("vecs_in")
        wq_in = [sem(f"wq_in{i}") for i in range(2)]
        wkv_in = [sem(f"wkv_in{i}") for i in range(2)]
        coef_in = sem("coef_in")
        ln_step, var_ready, std_ready, xhat_ready = sem("ln_step0"), sem("var_ready0"), sem("std_ready0"), sem("xhat_ready0")
        xt_psum, xt_ready = sem("xt_psum0"), sem("xt_ready0")
        q_psum, q_biased, q_rounded = sem("q_psum"), sem("q_biased"), sem("q_rounded")
        wkv_rounded, wkv_split = sem("wkv_rounded"), sem("wkv_split")
        masked, summed, folded, folded_out, four_stored = sem("masked"), sem("summed"), sem("folded"), sem("folded_out"), sem("four_stored")
        NG = NH // 8

        block = st.enter_context(nc.Block())

        @block.sync
        def _(sp):
            sp.dma_start(x_sb[:], x).then_inc(x_in, 16)
            sp.dma_start(ident[:], ident_in).then_inc(x_in, 16)
            for dst, src in ((bq_sb, bq), (bk_sb, bk), (bv_sb, bv)):
                sp.dma_start(dst[:], src).then_inc(vecs_in, 16)
            for g in range(NG * 2):
                if g >= 2:
                    sp.wait_ge(q_psum, g - 1)
                sp.dma_start(wq_sb[:, g % 2], wq[:, :, g * TW:(g + 1) * TW]).then_inc(wq_in[g % 2], 16)
            sp.wait_ge(folded_out, 1)
            sp.dma_start(four_dram, w_four[:]).then_inc(four_stored, 16)
            sp.wait_ge(four_stored, 16)

        @block.scalar
        def _(act):
            for k in range(KT):
                if k >= 2:
                    act.wait_ge(wkv_split, k - 1)
                act.dma_start(wkv_st[:, k % 2], wkv[:, k]).then_inc(wkv_in[k % 2], 16)
                if k == 1:
                    act.dma_start(co[:], coefs).then_inc(coef_in, 16)
                    act.dma_start(mk[:], mask).then_inc(coef_in, 16)
                    act.dma_start(four[:], fourier).then_inc(coef_in, 16)
                if k == 1:
                    act.wait_ge(var_ready, 1)
                    nc.scalar.activation(mv[:, 3:4], mv[:, 2:3], ACT.Sqrt).then_inc(std_ready, 1)

        @block.gpsimd
        def _(pool):
            nc.gpsimd.memset(acc[:], 0.0)
            nc.gpsimd.memset(denom[:], 0.0)
            nc.gpsimd.memset(maxes[:], LOWEST)
            pool.wait_ge(coef_in, 48)
            nc.gpsimd.tensor_copy(cm[:], mk[:]).then_inc(masked, 1)
            pool.wait_ge(masked, 1)
            nc.gpsimd.tensor_tensor(cm[:], cm[:], co[:], ALU.mult).then_inc(masked, 1)
            pool.wait_ge(masked, 2)
            nc.gpsimd.tensor_tensor(ws[:], cm[:, :, 0, :], cm[:, :, 1, :], ALU.add).then_inc(masked, 1)
            pool.wait_ge(masked, 3)
            nc.gpsimd.tensor_tensor(ws[:], ws[:], cm[:, :, 2, :], ALU.add).then_inc(summed, 1)

        @block.vector
        def _(dve):
            dve.wait_ge(x_in, 32)
            nc.vector.bn_stats(stats[:], x_sb[:]).then_inc(ln_step, 1)
            dve.wait_ge(ln_step, 1)
            nc.vector.bn_aggr(mv[:, 0:2], stats[:]).then_inc(ln_step, 1)
            dve.wait_ge(ln_step, 2)
            nc.vector.tensor_scalar(mv[:, 2:3], mv[:, 1:2], EPS, None, ALU.add).then_inc(var_ready, 1)
            dve.wait_ge(std_ready, 1)
            nc.vector.reciprocal(mv[:, 2:3], mv[:, 3:4]).then_inc(ln_step, 1)
            dve.wait_ge(ln_step, 3)
            nc.vector.tensor_scalar(xhat[:], x_sb[:], mv[:, 0:1], mv[:, 2:3], ALU.subtract,
                                    ALU.mult).then_inc(xhat_ready, 1)
            dve.wait_ge(xt_psum, 1)
            nc.vector.tensor_copy(xt[:], p_x[:]).then_inc(xt_ready, 1)
            dve.wait_ge(vecs_in, 48)
            for k in range(KT):
                dve.wait_ge(wkv_in[k % 2], 16 * (k // 2 + 1))
                nc.vector.tensor_copy(wkv_hi[:, k], wkv_st[:, k % 2]).then_inc(wkv_rounded, 1)
                dve.wait_ge(wkv_rounded, k + 1)
                nc.vector.tensor_tensor(wkv_lo[:, k], wkv_st[:, k % 2], wkv_hi[:, k].bitcast(F32),
                                        ALU.subtract).then_inc(wkv_split, 1)
            for g in range(NG):
                dve.wait_ge(q_psum, 2 * g + 2)
                heads = q_f[:, g % 2].rearrange("p (h t) -> p h t", h=8)
                nc.vector.tensor_tensor(heads, p_q[:, g % 2].rearrange("p (h t) -> p h t", h=8),
                                        bq_sb[:, 8 * g:8 * g + 8].unsqueeze(2).broadcast_to([P, 8, TOK]),
                                        ALU.add).then_inc(q_biased, 1)
                dve.wait_ge(q_biased, g + 1)
                two = slice(2 * g, 2 * g + 2)
                q3 = q_f[:, g % 2].rearrange("p (h r) -> p h r", h=2)
                nc.vector.tensor_copy(q_hi[:, two], q3).then_inc(q_rounded, 1)
                dve.wait_ge(q_rounded, g + 1)
                nc.vector.tensor_tensor(q_lo[:, two], q3, q_hi[:, two].bitcast(F32), ALU.subtract)
            dve.wait_ge(folded, 1)
            nc.vector.tensor_scalar(w_four[:], p_w[:], 0.5, None, ALU.mult).then_inc(folded_out, 1)

        @block.tensor
        def _(pe):
            pe.wait_ge(xhat_ready, 1)
            for k in range(KT):
                t = nc.tensor.transpose(p_x[:, k, :], xhat[:, k * P:(k + 1) * P], ident[0:TOK, 0:TOK])
            t.then_inc(xt_psum, 1)
            pe.wait_ge(xt_ready, 1)
            for g in range(2 * NG):
                pe.wait_ge(wq_in[g % 2], 16 * (g // 2 + 1))
                if g >= 4 and g % 2 == 0:
                    pe.wait_ge(q_biased, g // 2 - 1)
                for h in range(4):
                    col = (g % 2) * 4 * TOK + h * TOK
                    for k in range(KT):
                        m = nc.tensor.matmul(p_q[:, (g // 2) % 2, col:col + TOK],
                                             wq_sb[:, g % 2, k, h * D:(h + 1) * D], xt[:, k, :],
                                             start=(k == 0), stop=(k == KT - 1))
                m.then_inc(q_psum, 1)
            pe.wait_ge(summed, 1)
            for k in range(KT):
                m = nc.tensor.matmul(p_w[:], ws[:, k, :], four[:, k, :], start=(k == 0), stop=(k == KT - 1))
            m.then_inc(folded, 1)


def attention(nc, ctx_t, codes, scales, weights, ident, acc, denom, maxes, bk_sb,
              wkv_hi, wkv_lo, q_hi, q_lo, sem, sb, psum):
    with ExitStack() as st:
        ctx_st = sb(st, "ctx_st", [P, CHUNK], F32)
        ctx_hi = sb(st, "ctx_hi", [P, 2, KT, CHUNK], F32R)
        ctx_lo = sb(st, "ctx_lo", [P, 2, KT, CHUNK], F32R)
        v_hi = sb(st, "v_hi", [P, CT, 2 * D], F32R)
        v_lo = sb(st, "v_lo", [P, CT, 2 * D], F32R)
        k_hi = sb(st, "k_hi", [P, CHUNK], F32R)
        k_lo = sb(st, "k_lo", [P, CHUNK], F32R)
        probs = sb(st, "probs", [P, RT, CHUNK], F32)
        pt_hi = sb(st, "pt_hi", [P, CT, ROWS], F32R)
        pt_lo = sb(st, "pt_lo", [P, CT, ROWS], F32R)
        o_t = sb(st, "o_t", [P, ROWS], F32)
        newmax = sb(st, "newmax", [P, RT], F32)
        negmax = sb(st, "negmax", [P, RT], F32)
        drop = sb(st, "drop", [P, RT], F32)
        alpha = sb(st, "alpha", [P, 2, RT], F32)
        rowsum = sb(st, "rowsum", [P, 2, RT], F32)
        scale = sb(st, "scale", [P, TW], F32)
        bit0 = sb(st, "bit0", [P, TW], U16)
        bit1 = sb(st, "bit1", [P, TW], U16)
        bit2 = sb(st, "bit2", [P, TW], U16)
        bit3 = sb(st, "bit3", [P, TW], U16)
        leaf = sb(st, "leaf", [P, 5, TW], F32)
        code = leaf[:, 4, :].bitcast(I32)

        p_kv = psum(st, "p_kv", [P, 2, 512])
        p_s = psum(st, "p_s", [P, 2, 512])
        p_t = psum(st, "p_t", [P, 2, 512])
        p_o = psum(st, "p_o", [P, 512])
        p_ot = psum(st, "p_ot", [P, 512])

        ctx_in, ctx_rounded, ctx_split = sem("ctx_in"), sem("ctx_rounded"), sem("ctx_split")
        kv_psum, kv_rounded, kv_split = sem("kv_psum"), sem("kv_rounded"), sem("kv_split")
        scores_psum, scores_out = sem("scores_psum"), sem("scores_out")
        stat_step, max_ready = sem("stat_step"), sem("max_ready")
        alpha_ready, exp_ready = sem("alpha_ready"), sem("exp_ready")
        pt_psum, pt_rounded, pt_split = sem("pt_psum"), sem("pt_rounded"), sem("pt_split")
        o_psum, o_out, ot_psum, ot_added = sem("o_psum"), sem("o_out"), sem("ot_psum"), sem("ot_added")
        code_in, scale_in = sem("code_in"), sem("scale_in")
        code_narrow, bits_ready = sem("code_narrow"), sem("bits_ready")
        leaves_ready, chosen, choice = sem("leaves_ready"), sem("chosen"), sem("choice")
        scaled, weight_out = sem("scaled"), sem("weight_out")
        pool_passed, dve_passed = sem("pool_passed"), sem("dve_passed")

        NB = NCH * NKV
        KV_USES = CT + 4

        def v_use(s, h, t):
            return 2 + KV_USES * (4 * s + h // 2) + t

        def k_use(s, h, c):
            return 2 + KV_USES * (4 * s + h // 2) + CT + 2 * (h % 2) + c

        def v_bank(h, t):
            return (h // 2 + t) % 2

        def k_bank(h, c):
            return (h // 2 + 1 + c) % 2

        block = st.enter_context(nc.Block())

        @block.sync
        def _(sp):
            def load_ctx(s, k, first):
                if not first:
                    sp.wait_ge(ctx_split, KT * s + k)
                sp.dma_start(ctx_st[:], ctx_t[s, k]).then_inc(ctx_in, 16)

            def tile_in(n, tile, first=False):
                if not first:
                    sp.wait_ge(chosen, 2 * n)
                sp.dma_start(code, codes[tile]).then_inc(code_in, 16)
                if not first:
                    sp.wait_ge(scaled, n)
                for b in range(2):
                    sp.dma_start(scale[b * QBLK:(b + 1) * QBLK, :],
                                 scales[tile, b].partition_broadcast(QBLK)).then_inc(scale_in, 16)

            def tile_out(n, tile):
                sp.wait_ge(scaled, n + 1)
                sp.dma_start(weights[tile], leaf[:, 0, :]).then_inc(weight_out, 16)

            for k in range(KT):
                load_ctx(0, k, k == 0)
            for e in range(EXTRA):
                tile_in(e, NB + e, e == 0)
                tile_out(e, NB + e)

            def chunk(s, last):
                for h in range(NKV):
                    i = NKV * s + h
                    if not last and h < KT:
                        load_ctx(s + 1, h, False)
                    tile_in(i + EXTRA, i)
                    tile_out(i + EXTRA, i)

            with sp.Fori(0, NCH - 1) as s:
                chunk(s, False)
            chunk(NCH - 1, True)
            sp.wait_ge(weight_out, 16 * NT)

        @block.gpsimd
        def _(pool):
            def split_ctx(s, k, half):
                wait_apart(pool, ctx_in, 16 * (KT * s + k + 1), pool_passed)
                nc.gpsimd.tensor_copy(ctx_hi[:, half, k], ctx_st[:]).then_inc(ctx_rounded, 1)
                wait_apart(pool, ctx_rounded, KT * s + k + 1, pool_passed)
                nc.gpsimd.tensor_tensor(ctx_lo[:, half, k], ctx_st[:], ctx_hi[:, half, k].bitcast(F32),
                                        ALU.subtract).then_inc(ctx_split, 1)

            def leaves(first, slots):
                for j, slot in slots:
                    m = nc.gpsimd.tensor_scalar(leaf[:, slot, :], bit0[:], NF4[2 * j + 1] - NF4[2 * j], NF4[2 * j],
                                                ALU.mult, ALU.add)
                m.then_inc(leaves_ready, 1)

            def expand(n, first=False):
                wait_apart(pool, code_in, 16 * (n + 1), pool_passed)
                nc.gpsimd.tensor_copy(bit3[:], code).then_inc(code_narrow, 1)
                if not first:
                    wait_apart(pool, weight_out, 16 * n, pool_passed)
                wait_apart(pool, bits_ready, n + 1, pool_passed)
                leaves(True, ((0, 0), (1, 1), (2, 2), (3, 3)))
                wait_apart(pool, chosen, 2 * n + 1, pool_passed)
                leaves(False, ((4, 1), (5, 2), (6, 3), (7, 4)))
                wait_apart(pool, scale_in, 32 * (n + 1), pool_passed)
                wait_apart(pool, chosen, 2 * n + 2, pool_passed)
                nc.gpsimd.tensor_tensor(leaf[:, 0, :], leaf[:, 0, :], scale[:], ALU.mult).then_inc(scaled, 1)

            for k in range(KT):
                split_ctx(0, k, 0)
            for e in range(EXTRA):
                expand(e, e == 0)

            def chunk(s, par, last):
                for h in range(NKV):
                    i = NKV * s + h
                    if not last and h < KT:
                        split_ctx(s + 1, h, 1 - par)
                    expand(i + EXTRA)

            with pool.Fori(0, NCH // 2) as s2:
                chunk(2 * s2, 0, False)
                chunk(2 * s2 + 1, 1, False)
            chunk(NCH - 1, 0, True)

        @block.tensor
        def _(pe):
            def project_keys(use, bank, half, h, c, k):
                cols = slice(h * D, (h + 1) * D)
                keys = slice(c * HALF, (c + 1) * HALF)
                m = split_matmuls(nc, p_kv[:, bank, 0:HALF], wkv_hi[:, k, cols], wkv_lo[:, k, cols],
                                  ctx_hi[:, half, k, keys], ctx_lo[:, half, k, keys],
                                  start=(k == 0), stop=(k == KT - 1))
                if k == KT - 1:
                    m.then_inc(kv_psum, 1)

            def weighted_values(i, h):
                pe.wait_ge(pt_split, 4 * i + 4)
                pe.wait_ge(kv_split, v_use_of(i, h) + CT)
                if not static_first(i):
                    pe.wait_ge(o_out, i)
                d = slice((h % 2) * D, (h % 2 + 1) * D)
                for t in range(CT):
                    m = split_matmuls(nc, p_o[:, 0:ROWS], v_hi[:, t, d], v_lo[:, t, d], pt_hi[:, t], pt_lo[:, t],
                                      start=(t == 0), stop=(t == CT - 1))
                m.then_inc(o_psum, 1)

            def v_use_of(i, h):
                return 2 + ((i - (h % 2)) * KV_USES) // 2 if isinstance(i, int) else None

            def static_first(i):
                return isinstance(i, int) and i == 0

            def turn_output(i):
                pe.wait_ge(o_out, i + 1)
                if not static_first(i):
                    pe.wait_ge(ot_added, i)
                for r in range(RT):
                    m = nc.tensor.transpose(p_ot[:, r * D:(r + 1) * D], o_t[:, r * P:(r + 1) * P], ident[:])
                m.then_inc(ot_psum, 1)

            def turn_probs(i, c, skip):
                if c == 0:
                    pe.wait_ge(exp_ready, 2 * i + 2)
                if not skip:
                    pe.wait_ge(pt_split, 4 * i + c - 1)
                for t in range(2 * c, min(2 * c + 2, CT)):
                    for r in range(RT):
                        col = (t % 2) * ROWS + r * P
                        m = nc.tensor.transpose(p_t[:, c % 2, col:col + P], probs[:, r, t * P:(t + 1) * P], ident[:])
                m.then_inc(pt_psum, 1)

            def scores(i, h, kuse, static):
                for c in range(2):
                    pe.wait_ge(kv_split, kuse + c + 1)
                    for r in range(RT):
                        j = 2 * c + r
                        if not (static and j < 2):
                            pe.wait_ge(scores_out, 4 * i + j - 1)
                        m = split_matmuls(nc, p_s[:, j % 2, 0:HALF], q_hi[:, h, r * P:(r + 1) * P],
                                          q_lo[:, h, r * P:(r + 1) * P], k_hi[:, c * HALF:(c + 1) * HALF],
                                          k_lo[:, c * HALF:(c + 1) * HALF])
                        m.then_inc(scores_psum, 1)

            def values(s, h, half):
                for t in range(CT):
                    pe.wait_ge(kv_split, v_use(s, h, t) - 1)
                    cols = slice((NKV + h) * D, (NKV + h + 2) * D)
                    for k in range(KT):
                        keys = slice(t * P, (t + 1) * P)
                        m = split_matmuls(nc, p_kv[:, v_bank(h, t), 0:2 * D], ctx_hi[:, half, k, keys],
                                          ctx_lo[:, half, k, keys], wkv_hi[:, k, cols], wkv_lo[:, k, cols],
                                          start=(k == 0), stop=(k == KT - 1))
                    m.then_inc(kv_psum, 1)

            def prev_values(s, h):
                i = NKV * s + h - 1
                hp = (h - 1) % NKV
                pair = 4 * s + h // 2 - (1 if h % 2 == 0 else 0)
                pe.wait_ge(pt_split, 4 * i + 4)
                pe.wait_ge(kv_split, 2 + KV_USES * pair + CT)
                if not static_first(i):
                    pe.wait_ge(o_out, i)
                d = slice((hp % 2) * D, (hp % 2 + 1) * D)
                for t in range(CT):
                    m = split_matmuls(nc, p_o[:, 0:ROWS], v_hi[:, t, d], v_lo[:, t, d], pt_hi[:, t], pt_lo[:, t],
                                      start=(t == 0), stop=(t == CT - 1))
                m.then_inc(o_psum, 1)

            def block_work(s, h, half, first, last):
                i = NKV * s + h
                first = first and h == 0
                last = last and h == NKV - 1
                kuse = 0 if first else k_use(s, h, 0) - 2 - (CT if h % 2 == 0 else 0)
                scores(i, h, kuse, first)
                if not first:
                    prev_values(s, h)
                if h % 2 == 0:
                    values(s, h, half)
                nh, nhalf = ((h + 1), half) if h + 1 < NKV else (0, 1 - half)
                if not last:
                    if nh == 0:
                        pe.wait_ge(ctx_split, KT * (s + 2))
                    pe.wait_ge(kv_split, k_use(s, h, 0) - 1)
                    for k in range(KT):
                        project_keys(None, k_bank(h, 0), nhalf, nh, 0, k)
                    if not first:
                        turn_output(i - 1)
                    turn_probs(i, 0, first)
                    pe.wait_ge(kv_split, k_use(s, h, 1) - 1)
                    project_keys(None, k_bank(h, 1), nhalf, nh, 1, 0)
                    turn_probs(i, 1, first)
                    project_keys(None, k_bank(h, 1), nhalf, nh, 1, 1)
                    project_keys(None, k_bank(h, 1), nhalf, nh, 1, 2)
                    turn_probs(i, 2, False)
                    project_keys(None, k_bank(h, 1), nhalf, nh, 1, 3)
                    turn_probs(i, 3, False)
                else:
                    turn_output(i - 1)
                    for c in range(4):
                        turn_probs(i, c, False)

            pe.wait_ge(ctx_split, KT)
            for c in range(2):
                for k in range(KT):
                    project_keys(None, c, 0, 0, c, k)
            for h in range(NKV):
                block_work(0, h, 0, True, False)
            with pe.Fori(0, NCH // 2 - 1) as s2:
                for h in range(NKV):
                    block_work(2 * s2 + 1, h, 1, False, False)
                for h in range(NKV):
                    block_work(2 * s2 + 2, h, 0, False, False)
            for h in range(NKV):
                block_work(NCH - 2, h, 1, False, False)
            for h in range(NKV):
                block_work(NCH - 1, h, 0, False, True)
            prev_values(NCH, 0)
            turn_output(NB - 1)

        @block.scalar
        def _(act):
            def round_kv(use, dst, src, bias=None):
                act.wait_ge(kv_psum, use + 1)
                nc.scalar.activation(dst, src, ACT.Identity, bias=0.0 if bias is None else bias).then_inc(kv_rounded, 1)

            def round_keys(use, bank, nh, c):
                round_kv(use, k_hi[:, c * HALF:(c + 1) * HALF], p_kv[:, bank, 0:HALF], bk_sb[:, nh:nh + 1])

            def round_probs(i, c):
                act.wait_ge(pt_psum, 4 * i + c + 1)
                n = min(2, CT - 2 * c)
                nc.scalar.activation(pt_hi[:, 2 * c:2 * c + n, :].rearrange("p t q -> p (t q)"),
                                     p_t[:, c % 2, 0:n * ROWS], ACT.Copy).then_inc(pt_rounded, 1)

            def output_out(i):
                act.wait_ge(o_psum, i + 1)
                nc.scalar.activation(o_t[:], p_o[:, 0:ROWS], ACT.Copy).then_inc(o_out, 1)

            def block_work(s, h, first, last):
                i = NKV * s + h
                par = h % 2
                act.wait_ge(max_ready, i + 1)
                nc.scalar.activation(alpha[:, par, :], drop[:], ACT.Exp).then_inc(alpha_ready, 1)
                for r in range(RT):
                    nc.scalar.activation(probs[:, r, :], probs[:, r, :], ACT.Exp, bias=negmax[:, r:r + 1],
                                         accum_out=rowsum[:, par, r:r + 1]).then_inc(exp_ready, 1)
                if not (first and h == 0):
                    output_out(i - 1)
                if h % 2 == 0:
                    for t in range(CT):
                        round_kv(v_use(s, h, t), v_hi[:, t], p_kv[:, v_bank(h, t), 0:2 * D])
                if last and h == NKV - 1:
                    for c in range(4):
                        round_probs(i, c)
                    return
                nh = (h + 1) % NKV
                round_keys(k_use(s, h, 0), k_bank(h, 0), nh, 0)
                for c in range(3):
                    round_probs(i, c)
                round_keys(k_use(s, h, 1), k_bank(h, 1), nh, 1)
                round_probs(i, 3)

            for c in range(2):
                round_keys(c, c, 0, c)
            for h in range(NKV):
                block_work(0, h, True, False)
            with act.Fori(1, NCH - 1) as s:
                for h in range(NKV):
                    block_work(s, h, False, False)
            for h in range(NKV):
                block_work(NCH - 1, h, False, True)
            output_out(NB - 1)

        @block.vector
        def _(dve):
            def split_kv(use, dst, src, hi, bias=None):
                dve.wait_ge(kv_rounded, use + 1)
                if bias is None:
                    nc.vector.tensor_tensor(dst, src, hi.bitcast(F32), ALU.subtract).then_inc(kv_split, 1)
                else:
                    nc.vector.scalar_tensor_tensor(dst, src, bias, hi.bitcast(F32), ALU.add,
                                                   ALU.subtract).then_inc(kv_split, 1)

            def split_keys(use, bank, nh, c):
                keys = slice(c * HALF, (c + 1) * HALF)
                split_kv(use, k_lo[:, keys], p_kv[:, bank, 0:HALF], k_hi[:, keys], bk_sb[:, nh:nh + 1])

            def split_probs(i, c):
                dve.wait_ge(pt_rounded, 4 * i + c + 1)
                n = min(2, CT - 2 * c)
                nc.vector.tensor_tensor(pt_lo[:, 2 * c:2 * c + n, :].rearrange("p t q -> p (t q)"),
                                        p_t[:, c % 2, 0:n * ROWS],
                                        pt_hi[:, 2 * c:2 * c + n, :].rearrange("p t q -> p (t q)").bitcast(F32),
                                        ALU.subtract).then_inc(pt_split, 1)

            def add_output(i, h):
                dve.wait_ge(alpha_ready, i + 1)
                dve.wait_ge(ot_psum, i + 1)
                par = h % 2
                for r in range(RT):
                    nc.vector.scalar_tensor_tensor(denom[:, h, r:r + 1], denom[:, h, r:r + 1], alpha[:, par, r:r + 1],
                                                   rowsum[:, par, r:r + 1], ALU.mult, ALU.add)
                for r in range(RT):
                    m = nc.vector.scalar_tensor_tensor(acc[:, h, r, :], acc[:, h, r, :], alpha[:, par, r:r + 1],
                                                       p_ot[:, r * D:(r + 1) * D], ALU.mult, ALU.add)
                m.then_inc(ot_added, 1)

            def score_stats(i, h):
                for c in range(2):
                    for r in range(RT):
                        dve.wait_ge(scores_psum, 4 * i + 2 * c + r + 1)
                        nc.vector.tensor_scalar(probs[:, r, c * HALF:(c + 1) * HALF], p_s[:, r, 0:HALF], SCALE, None,
                                                ALU.mult, ALU.max,
                                                accum_out=maxes[:, h, r, 1 + c:2 + c]).then_inc(scores_out, 1)
                dve.wait_ge(scores_out, 4 * i + 4)
                nc.vector.tensor_reduce(newmax[:], maxes[:, h], AX_X, ALU.max).then_inc(stat_step, 1)
                dve.wait_ge(stat_step, 2 * i + 1)
                nc.vector.tensor_scalar(negmax[:], newmax[:], -1.0, None, ALU.mult)
                nc.vector.tensor_tensor(drop[:], maxes[:, h, :, 0], newmax[:], ALU.subtract).then_inc(max_ready, 1)
                dve.wait_ge(max_ready, i + 1)
                nc.vector.tensor_copy(maxes[:, h, :, 0], newmax[:]).then_inc(stat_step, 1)

            def take_bits(n):
                dve.wait_ge(code_narrow, n + 1)
                for bit, dst in ((0, bit0), (1, bit1), (2, bit2), (3, bit3)):
                    m = nc.vector.tensor_scalar(dst[:], bit3[:], 1 << bit, None, ALU.bitwise_and)
                m.then_inc(bits_ready, 1)

            def choose_low(n):
                wait_apart(dve, leaves_ready, 2 * n + 1, dve_passed)
                nc.vector.copy_predicated(leaf[:, 0, :], bit1[:], leaf[:, 1, :])
                nc.vector.copy_predicated(leaf[:, 2, :], bit1[:], leaf[:, 3, :]).then_inc(choice, 1)
                wait_apart(dve, choice, 3 * n + 1, dve_passed)
                nc.vector.copy_predicated(leaf[:, 0, :], bit2[:], leaf[:, 2, :]).then_inc(chosen, 1)

            def choose_high(n):
                wait_apart(dve, leaves_ready, 2 * n + 2, dve_passed)
                nc.vector.copy_predicated(leaf[:, 1, :], bit1[:], leaf[:, 2, :])
                nc.vector.copy_predicated(leaf[:, 3, :], bit1[:], leaf[:, 4, :]).then_inc(choice, 1)
                wait_apart(dve, choice, 3 * n + 2, dve_passed)
                nc.vector.copy_predicated(leaf[:, 1, :], bit2[:], leaf[:, 3, :]).then_inc(choice, 1)
                wait_apart(dve, choice, 3 * n + 3, dve_passed)
                nc.vector.copy_predicated(leaf[:, 0, :], bit3[:], leaf[:, 1, :]).then_inc(chosen, 1)

            def block_work(s, h, first, last):
                i = NKV * s + h
                score_stats(i, h)
                take_bits(i + EXTRA)
                if h % 2 == 0:
                    for t in range(CT):
                        split_kv(v_use(s, h, t), v_lo[:, t], p_kv[:, v_bank(h, t), 0:2 * D], v_hi[:, t])
                if last and h == NKV - 1:
                    add_output(i - 1, (h - 1) % NKV)
                    for c in range(4):
                        split_probs(i, c)
                    choose_low(i + EXTRA)
                    choose_high(i + EXTRA)
                    return
                nh = (h + 1) % NKV
                split_keys(k_use(s, h, 0), k_bank(h, 0), nh, 0)
                choose_low(i + EXTRA)
                if not (first and h == 0):
                    add_output(i - 1, (h - 1) % NKV)
                for c in range(3):
                    split_probs(i, c)
                split_keys(k_use(s, h, 1), k_bank(h, 1), nh, 1)
                split_probs(i, 3)
                choose_high(i + EXTRA)

            for c in range(2):
                split_keys(c, c, 0, c)
            for e in range(EXTRA):
                take_bits(e)
                choose_low(e)
                choose_high(e)
            for h in range(NKV):
                block_work(0, h, True, False)
            with dve.Fori(1, NCH - 1) as s:
                for h in range(NKV):
                    block_work(s, h, False, False)
            for h in range(NKV):
                block_work(NCH - 1, h, False, True)
            add_output(NB - 1, NKV - 1)


def tail(nc, wo, bo, weights, lora_a, lora_a_down, lora_b, lora_b_down, w_base, b_base, enc, out,
         ident, x, acc, denom, bv_sb, four_dram, sem, sb, psum):
    WB = 10
    with ExitStack() as st:
        wring = sb(st, "wring", [P, WB, TW], F32)
        o_n = sb(st, "o_n", [P, NKV, RT, D], F32)
        rden = sb(st, "rden", [P, NKV, RT], F32)
        ot = sb(st, "ot", [P, NKV, ROWS], F32)
        x_sb = sb(st, "x_sb", [TOK, HID], F32)
        w_four = sb(st, "w_four", [RR, HID], F32)
        bo_sb = sb(st, "bo_sb", [TOK, HID], F32)
        bb_sb = sb(st, "bb_sb", [TOK, HID], F32)
        la = sb(st, "la", [P, KT, 6 * RANK], F32)
        lad = sb(st, "lad", [P, FT, RANK], F32)
        lb_qkv = sb(st, "lb_qkv", [3 * RANK, HID], F32)
        lb_o = sb(st, "lb_o", [RANK, HID], F32)
        lb_gu = sb(st, "lb_gu", [RANK, 2 * FFN], F32)
        lb_d = sb(st, "lb_d", [RANK, HID], F32)
        wb = sb(st, "wb", [P, KT, HID], F32)
        en = sb(st, "en", [P, KT, RR], F32)
        xa = sb(st, "xa", [TOK, HID], F32)
        z = sb(st, "z", [TOK, HID], F32)
        y = sb(st, "y", [TOK, HID], F32)
        xb = sb(st, "xb", [TOK, HID], F32)
        z2 = sb(st, "z2", [TOK, HID], F32)
        av = sb(st, "av", [TOK, HID], F32)
        fin = sb(st, "fin", [TOK, HID], F32)
        res = sb(st, "res", [TOK, HID], F32)
        sums = sb(st, "sums", [TOK, HID], F32)
        zt = sb(st, "zt", [P, KT, TOK], F32)
        at = sb(st, "at", [P, KT, TOK], F32)
        yt = sb(st, "yt", [P, KT, TOK], F32)
        z2t = sb(st, "z2t", [P, KT, TOK], F32)
        gu = sb(st, "gu", [TOK, 2 * FFN], F32)
        eg = sb(st, "eg", [TOK, FFN], F32)
        rg = sb(st, "rg", [TOK, FFN], F32)
        ht = sb(st, "ht", [P, FT, TOK], F32)
        e_qkv = sb(st, "e_qkv", [3 * RANK, TOK], F32)
        e_small = sb(st, "e_small", [RANK, 4, TOK], F32)
        e_f = sb(st, "e_f", [RR, TOK], F32)
        stats = sb(st, "stats", [TOK, 2, 6], F32)
        mv = sb(st, "mv", [TOK, 2, 4], F32)

        pb = [psum(st, f"pb{i}", [P, 512]) for i in range(8)]

        small_in = sem("small_in")
        w_in = [sem(f"w_in{i}") for i in range(WB)]
        w_used = sem("w_used")
        PARTS = NH + NT
        block = st.enter_context(nc.Block())
        order = list(range(0, ATT_TILES))
        order += [ATT_TILES + k * GU_COLS + c for c in range(GU_COLS) for k in range(KT)]
        order += [ATT_TILES + GU_TILES + j for j in range(FT)]
        smalls = [(bo_sb[:], bo.partition_broadcast(TOK)), (bb_sb[:], b_base.partition_broadcast(TOK)),
                  (la[:], lora_a), (lad[:], lora_a_down), (lb_qkv[:], lora_b[0:3 * RANK, 0:HID]),
                  (lb_o[:], lora_b[3 * RANK:4 * RANK, 0:HID]), (lb_gu[:, 0:FFN], lora_b[4 * RANK:5 * RANK, :]),
                  (lb_gu[:, FFN:2 * FFN], lora_b[5 * RANK:6 * RANK, :]), (lb_d[:], lora_b_down),
                  (wb[:], w_base), (en[:], enc), (x_sb[:], x), (w_four[:], four_dram)]

        names = {}

        def step(name):
            if name not in names:
                names[name] = sem(name)
            return names[name]

        @block.scalar
        def _(act):
            for dst, src in smalls:
                act.dma_start(dst, src).then_inc(small_in, 16)

            def root(n):
                act.wait_ge(step(f"variance{n}"), 1)
                nc.scalar.activation(mv[:, n, 3:4], mv[:, n, 2:3], ACT.Sqrt).then_inc(step(f"deviation{n}"), 1)

            root(0)
            act.wait_ge(step("gu_out"), 1)
            nc.scalar.activation(eg[:], gu[:, 0:FFN], ACT.Exp, scale=-1.0).then_inc(step("exp_gate"), 1)
            root(1)

        @block.sync
        def _(sp):
            for n in range(PARTS):
                if n >= WB:
                    sp.wait_ge(w_used, n - WB + 1)
                src = wo[n] if n < NH else weights[order[n - NH]]
                sp.dma_start(wring[:, n % WB, :], src).then_inc(w_in[n % WB], 16)
            sp.wait_ge(step("final"), 1)
            sp.dma_start(out, res[:]).then_inc(step("stored"), 16)
            sp.wait_ge(step("stored"), 16)

        @block.vector
        def _(dve):
            nc.vector.reciprocal(rden[:], denom[:]).then_inc(step("reciprocals"), 1)
            dve.wait_ge(step("reciprocals"), 1)
            for h in range(NKV):
                for r in range(RT):
                    m = nc.vector.tensor_scalar(o_n[:, h, r, :], acc[:, h, r, :], rden[:, h, r:r + 1], None, ALU.mult)
                m.then_inc(step("divided"), 1)
            for h in range(NKV):
                dve.wait_ge(step("attn_turned"), h + 1)
                nc.vector.tensor_scalar(ot[:, h, :], pb[h % 2][:, 0:ROWS], bv_sb[:, h:h + 1], None,
                                        ALU.add).then_inc(step("attn_t"), 1)
            dve.wait_ge(step("attn_psum"), 1)
            dve.wait_ge(small_in, 16 * len(smalls))
            nc.vector.tensor_tensor(sums[:], pb[2][0:TOK, :], bo_sb[:], ALU.add).then_inc(step("with_bo"), 1)
            dve.wait_ge(step("with_bo"), 1)
            nc.vector.tensor_tensor(xa[:], sums[:], x_sb[:], ALU.add).then_inc(step("xa_ready"), 1)

            def norm(n, src, dst, ready):
                dve.wait_ge(step(ready), 1)
                nc.vector.bn_stats(stats[:, n], src[:]).then_inc(step(f"moments{n}"), 1)
                dve.wait_ge(step(f"moments{n}"), 1)
                nc.vector.bn_aggr(mv[:, n, 0:2], stats[:, n]).then_inc(step(f"mean{n}"), 1)
                dve.wait_ge(step(f"mean{n}"), 1)
                nc.vector.tensor_scalar(mv[:, n, 2:3], mv[:, n, 1:2], EPS, None, ALU.add).then_inc(step(f"variance{n}"), 1)
                dve.wait_ge(step(f"deviation{n}"), 1)
                nc.vector.reciprocal(mv[:, n, 2:3], mv[:, n, 3:4]).then_inc(step(f"inverse{n}"), 1)
                dve.wait_ge(step(f"inverse{n}"), 1)
                nc.vector.tensor_scalar(dst[:], src[:], mv[:, n, 0:1], mv[:, n, 2:3], ALU.subtract,
                                        ALU.mult).then_inc(step(f"normed{n}"), 1)

            def turned(name, dst, bank):
                dve.wait_ge(step(f"{name}_turned"), 1)
                nc.vector.tensor_copy(dst[:], bank[:, 0:KT * TOK].rearrange("p (k t) -> p k t", k=KT)).then_inc(
                    step(f"{name}_t"), 1)

            norm(0, xa, z, "xa_ready")
            turned("z", zt, pb[0])
            dve.wait_ge(step("low_qkv"), 1)
            nc.vector.tensor_copy(e_qkv[:], pb[3][0:3 * RANK, 0:TOK]).then_inc(step("e_qkv"), 1)
            dve.wait_ge(step("qkv_psum"), 1)
            nc.vector.tensor_scalar(av[:], pb[2][0:TOK, :], 1.0 / 3.0, None, ALU.mult).then_inc(step("av_ready"), 1)
            turned("a", at, pb[0])
            dve.wait_ge(step("low_o"), 1)
            nc.vector.tensor_copy(e_small[:, 0], pb[3][0:RANK, 0:TOK]).then_inc(step("e_o"), 1)
            dve.wait_ge(step("o_psum_t"), 1)
            nc.vector.tensor_tensor(y[:], pb[2][0:TOK, :], z[:], ALU.add).then_inc(step("y_ready"), 1)
            turned("y", yt, pb[0])
            for j in range(2):
                dve.wait_ge(step(f"low_gu{j}"), 1)
                nc.vector.tensor_copy(e_small[:, 1 + j], pb[0][0:RANK, 256 + j * TOK:256 + (j + 1) * TOK]).then_inc(
                    step(f"e_gu{j}"), 1)
            for c in range(GU_COLS):
                dve.wait_ge(step("gu_psum"), c + 1)
                m = nc.vector.tensor_copy(gu[:, c * TW:(c + 1) * TW], pb[1 + c][0:TOK, :])
            m.then_inc(step("gu_out"), 1)
            dve.wait_ge(step("exp_gate"), 1)
            nc.vector.tensor_scalar(rg[:], eg[:], 1.0, None, ALU.add).then_inc(step("one_plus"), 1)
            dve.wait_ge(step("one_plus"), 1)
            nc.vector.reciprocal(eg[:], rg[:]).then_inc(step("gate"), 1)
            dve.wait_ge(step("gate"), 1)
            nc.vector.tensor_tensor(rg[:], eg[:], gu[:, 0:FFN], ALU.mult).then_inc(step("silu"), 1)
            dve.wait_ge(step("silu"), 1)
            nc.vector.tensor_tensor(eg[:], rg[:], gu[:, FFN:2 * FFN], ALU.mult).then_inc(step("h_ready"), 1)
            for half in range(2):
                dve.wait_ge(step("h_turned"), half + 1)
                nc.vector.tensor_copy(ht[:, 7 * half:7 * half + 7, :],
                                      pb[half][:, 0:7 * TOK].rearrange("p (k t) -> p k t", k=7)).then_inc(step("h_t"), 1)
            dve.wait_ge(step("low_d"), 1)
            nc.vector.tensor_copy(e_small[:, 3], pb[3][0:RANK, 0:TOK]).then_inc(step("e_d"), 1)
            nc.vector.tensor_tensor(fin[:], y[:], xa[:], ALU.add).then_inc(step("y_plus_xa"), 1)
            dve.wait_ge(step("y_plus_xa"), 1)
            dve.wait_ge(step("d_psum"), 1)
            nc.vector.tensor_tensor(xb[:], pb[2][0:TOK, :], fin[:], ALU.add).then_inc(step("xb_ready"), 1)
            norm(1, xb, z2, "xb_ready")
            nc.vector.tensor_tensor(sums[:], xb[:], bb_sb[:], ALU.add).then_inc(step("with_bb"), 1)
            turned("z2", z2t, pb[0])
            dve.wait_ge(step("low_f"), 1)
            nc.vector.tensor_copy(e_f[:], pb[3][0:RR, 0:TOK]).then_inc(step("e_f"), 1)
            dve.wait_ge(step("f_psum"), 1)
            dve.wait_ge(step("with_bb"), 1)
            nc.vector.tensor_tensor(res[:], pb[4][0:TOK, :], sums[:], ALU.add).then_inc(step("final"), 1)

        @block.tensor
        def _(pe):
            used = [0]

            def product(dst, lhs, start, stop=False):
                n = used[0]
                pe.wait_ge(w_in[n % WB], 16 * (n // WB + 1))
                used[0] += 1
                return nc.tensor.matmul(dst, lhs, wring[:, n % WB, :], start=start, stop=stop)

            def turn(name, src, dst):
                for k in range(KT):
                    m = nc.tensor.transpose(dst[:, k * TOK:(k + 1) * TOK], src[:, k * P:(k + 1) * P],
                                            ident[0:TOK, 0:TOK])
                m.then_inc(step(f"{name}_turned"), 1)

            for h in range(NKV):
                pe.wait_ge(step("divided"), h + 1)
                if h >= 2:
                    pe.wait_ge(step("attn_t"), h - 1)
                for r in range(RT):
                    m = nc.tensor.transpose(pb[h % 2][:, r * P:(r + 1) * P], o_n[:, h, r, :], ident[:])
                m.then_inc(step("attn_turned"), 1)
            for h in range(NH):
                pe.wait_ge(step("attn_t"), h // G + 1)
                m = product(pb[2][0:TOK, :], ot[:, h // G, (h % G) * TOK:(h % G + 1) * TOK], h == 0, h == NH - 1)
                m.then_inc(w_used, 1)
            nc.tensor.matmul(pb[3][0:TOK, 0:2], ident[:, 0:TOK], ident[:, 0:2], start=True, stop=True).then_inc(
                step("attn_psum"), 1)

            pe.wait_ge(small_in, 16 * len(smalls))
            pe.wait_ge(step("normed0"), 1)
            pe.wait_ge(step("attn_t"), NKV)
            turn("z", z, pb[0])
            pe.wait_ge(step("z_t"), 1)
            for k in range(KT):
                m = nc.tensor.matmul(pb[3][0:3 * RANK, 0:TOK], la[:, k, 0:3 * RANK], zt[:, k], start=(k == 0),
                                     stop=(k == KT - 1))
            m.then_inc(step("low_qkv"), 1)
            for n in range(3 * KT):
                product(pb[2][0:TOK, :], zt[:, n % KT], n == 0).then_inc(w_used, 1)
            pe.wait_ge(step("e_qkv"), 1)
            nc.tensor.matmul(pb[2][0:TOK, :], e_qkv[:], lb_qkv[:], start=False, stop=True).then_inc(step("qkv_psum"), 1)
            pe.wait_ge(step("av_ready"), 1)
            turn("a", av, pb[0])
            pe.wait_ge(step("a_t"), 1)
            for k in range(KT):
                m = nc.tensor.matmul(pb[3][0:RANK, 0:TOK], la[:, k, 3 * RANK:4 * RANK], at[:, k], start=(k == 0),
                                     stop=(k == KT - 1))
            m.then_inc(step("low_o"), 1)
            for k in range(KT):
                product(pb[2][0:TOK, :], at[:, k], k == 0).then_inc(w_used, 1)
            pe.wait_ge(step("e_o"), 1)
            nc.tensor.matmul(pb[2][0:TOK, :], e_small[:, 0], lb_o[:], start=False, stop=True).then_inc(
                step("o_psum_t"), 1)
            pe.wait_ge(step("y_ready"), 1)
            turn("y", y, pb[0])
            pe.wait_ge(step("y_t"), 1)
            for j in range(2):
                for k in range(KT):
                    m = nc.tensor.matmul(pb[0][0:RANK, 256 + j * TOK:256 + (j + 1) * TOK],
                                         la[:, k, (4 + j) * RANK:(5 + j) * RANK], yt[:, k], start=(k == 0),
                                         stop=(k == KT - 1))
                m.then_inc(step(f"low_gu{j}"), 1)
                pe.wait_ge(step(f"e_gu{j}"), 1)
            for c in range(GU_COLS):
                for k in range(KT):
                    product(pb[1 + c][0:TOK, :], yt[:, k], k == 0).then_inc(w_used, 1)
                lo, hi = c * TW, (c + 1) * TW
                parts = [(0, lo, min(hi, FFN))] * (lo < FFN) + [(1, max(lo, FFN), hi)] * (hi > FFN)
                for n, (j, a, b) in enumerate(parts):
                    m = nc.tensor.matmul(pb[1 + c][0:TOK, a - lo:b - lo], e_small[:, 1 + j], lb_gu[:, a:b],
                                         start=False, stop=(n == len(parts) - 1))
                m.then_inc(step("gu_psum"), 1)
            pe.wait_ge(step("h_ready"), 1)
            for t in range(FT):
                m = nc.tensor.transpose(pb[t // 7][:, (t % 7) * TOK:(t % 7 + 1) * TOK], eg[:, t * P:(t + 1) * P],
                                        ident[0:TOK, 0:TOK])
                if t % 7 == 6:
                    m.then_inc(step("h_turned"), 1)
            pe.wait_ge(step("h_t"), 2)
            for t in range(FT):
                m = nc.tensor.matmul(pb[3][0:RANK, 0:TOK], lad[:, t], ht[:, t], start=(t == 0), stop=(t == FT - 1))
            m.then_inc(step("low_d"), 1)
            for t in range(FT):
                product(pb[2][0:TOK, :], ht[:, t], t == 0).then_inc(w_used, 1)
            pe.wait_ge(step("e_d"), 1)
            nc.tensor.matmul(pb[2][0:TOK, :], e_small[:, 3], lb_d[:], start=False, stop=True).then_inc(step("d_psum"), 1)
            pe.wait_ge(step("normed1"), 1)
            turn("z2", z2, pb[0])
            pe.wait_ge(step("z2_t"), 1)
            for k in range(KT):
                m = nc.tensor.matmul(pb[3][0:RR, 0:TOK], en[:, k], z2t[:, k], start=(k == 0), stop=(k == KT - 1))
            m.then_inc(step("low_f"), 1)
            for k in range(KT):
                nc.tensor.matmul(pb[4][0:TOK, :], z2t[:, k], wb[:, k], start=(k == 0), stop=False)
            pe.wait_ge(step("e_f"), 1)
            nc.tensor.matmul(pb[4][0:TOK, :], e_f[:], w_four[:], start=False, stop=True).then_inc(step("f_psum"), 1)


def fourier_matrix(n):
    t = np.arange(n)
    rows = np.zeros((n, n))
    rows[0] = 1.0 / np.sqrt(n)
    for f in range(1, (n - 1) // 2 + 1):
        rows[2 * f - 1] = np.sqrt(2.0 / n) * np.cos(2 * np.pi * f * t / n)
        rows[2 * f] = np.sqrt(2.0 / n) * np.sin(2 * np.pi * f * t / n)
    rows[n - 1] = (1.0 - 2.0 * (t % 2)) / np.sqrt(n)
    return rows.astype(np.float32)


def kernel(**inputs):
    import numpy as _np
    import concourse.bacc as _bacc
    from concourse import mybir as _mybir
    from concourse.bass_utils import run_bass_kernel_spmd as _run

    a = {k: _np.asarray(v) for k, v in inputs.items()}

    def k_tiles(m):
        return m.reshape(-1, P, m.shape[1]).transpose(1, 0, 2)

    def weight_tiles(m):
        o, i = m.shape
        return m.T.reshape(i // P, P, o // TW, TW).transpose(0, 2, 1, 3).reshape(-1, P, TW)

    def scale_tiles(m):
        o, b = m.shape
        return m.T.reshape(b // 2, 2, o // TW, TW).transpose(0, 2, 1, 3).reshape(-1, 2, TW)

    def all_tiles(f, att, gate_up, down):
        return _np.concatenate([f(m) for m in att] + [f(_np.concatenate([gate_up[0], gate_up[1]], 0)), f(down)])

    lb_gu = a["L0_attn_lora_B_gu"]
    lb = _np.zeros((6 * RANK, FFN), _np.float32)
    for m in range(4):
        lb[m * RANK:(m + 1) * RANK, 0:HID] = a["L0_attn_lora_B_attn"][m].T
    for m in range(2):
        lb[(4 + m) * RANK:(5 + m) * RANK] = lb_gu[m].T
    coefs = _np.concatenate([a["L0_ffn_coefs0"], a["L0_ffn_coefs1"]], 2)
    mask = _np.concatenate([a["L0_ffn_mask0"], a["L0_ffn_mask1"]], 2)
    laid = {
        "x": a["x"].reshape(TOK, HID),
        "ctx_t": a["ctx_4096"].reshape(NCH, CHUNK, KT, P).transpose(0, 2, 3, 1),
        "wq": k_tiles(a["L0_xattn_Wq"]),
        "bq": a["L0_xattn_bq"].reshape(NH, D).T,
        "wkv": k_tiles(a["L0_xattn_Wkv"]),
        "bk": a["L0_xattn_bkv"][:NKV * D].reshape(NKV, D).T,
        "bv": a["L0_xattn_bkv"][NKV * D:].reshape(NKV, D).T,
        "wo": a["L0_xattn_Wo"].reshape(NH, D, HID),
        "bo": a["L0_xattn_bo"],
        "codes": all_tiles(weight_tiles, a["L0_attn_codes_attn"], a["L0_attn_codes_gu"], a["L0_attn_codes_down"]),
        "scales": all_tiles(scale_tiles, a["L0_attn_scales_attn"], a["L0_attn_scales_gu"], a["L0_attn_scales_down"]),
        "lora_a": k_tiles(a["L0_attn_lora_A_h"].reshape(6 * RANK, HID).T),
        "lora_a_down": k_tiles(a["L0_attn_lora_A_down"].T),
        "lora_b": lb,
        "lora_b_down": a["L0_attn_lora_B_down"].T,
        "w_base": k_tiles(a["L0_ffn_W_base"].T),
        "b_base": a["L0_ffn_b_base"],
        "enc": k_tiles(_np.concatenate([a["L0_ffn_enc0"], a["L0_ffn_enc1"]], 0).T),
        "coefs": coefs.transpose(1, 0, 2).reshape(KT, P, NEXP, RR).transpose(1, 0, 2, 3),
        "mask": mask.transpose(1, 0, 2).reshape(KT, P, NEXP, RR).transpose(1, 0, 2, 3),
        "fourier": k_tiles(fourier_matrix(HID)),
        "ident": _np.eye(P, dtype=_np.float32),
    }
    nc = _bacc.Bacc("TRN2", target_bir_lowering=False, num_devices=1)
    arrays, args = {}, []
    for name, m in laid.items():
        m = _np.ascontiguousarray(m)
        arrays[f"in_{name}"] = m
        args.append(nc.dram_tensor(f"in_{name}", m.shape, _mybir.dt.from_np(m.dtype), kind="ExternalInput").ap())
    args.append(nc.dram_tensor("out_x", (TOK, HID), _mybir.dt.float32, kind="ExternalOutput").ap())
    perceiver_block(nc, *args)
    r = _run(nc, [arrays], core_ids=[0])
    return r.results[0]["out_x"].reshape(1, TOK, HID)
```

```python
from contextlib import ExitStack

import numpy as np

import concourse.bass as bass
from concourse import mybir

ALU = mybir.AluOpType
ACT = mybir.ActivationFunctionType
AX_X = mybir.AxisListType.X
F32 = mybir.dt.float32
F32R = mybir.dt.float32r
I32 = mybir.dt.int32
U16 = mybir.dt.uint16
U8 = mybir.dt.uint8

P = 128
HID = 512
KT = HID // P
TOK = 64
KEYS = 6272
D = 128
NKV = 8
G = 4
NH = NKV * G
ROWS = G * TOK
RT = ROWS // P
CT = 7
CHUNK = CT * P
NCH = KEYS // CHUNK
HALF = CHUNK // 2
SCALE = float(1.0 / np.sqrt(D))
FFN = 1792
FT = FFN // P
RANK = 16
R0, R1, NEXP = 32, 8, 3
RR = R0 + R1
QBLK = 64
NF4 = [-1.0, -0.6961928009986877, -0.5250730514526367, -0.39491748809814453, -0.28444138169288635,
       -0.18477343022823334, -0.09105003625154495, 0.0, 0.07958029955625534, 0.16093020141124725,
       0.24611230194568634, 0.33791524171829224, 0.44070982933044434, 0.5626170039176941,
       0.7229568362236023, 1.0]
TW = 512
ATT_TILES = 4 * KT
GU_COLS = 2 * FFN // TW
GU_TILES = KT * GU_COLS
NT = ATT_TILES + GU_TILES + FT
EXTRA = NT - NCH * NKV
HW = TW // 2
PIECE = CHUNK // 4
PIECES = KT * (CHUNK // PIECE)
PAIR_PIECES = (5, 5, 5, 1)
EPS = 1e-5
LOWEST = -3.0e38


def split_matmuls(nc, out, hi, lo, rhi, rlo, start=True, stop=True):
    nc.tensor.matmul(out, hi, rhi, start=start, stop=False)
    nc.tensor.matmul(out, hi, rlo, start=False, stop=False)
    return nc.tensor.matmul(out, lo, rhi, start=False, stop=stop)


def wait_apart(eng, sem, value, passed):
    eng.wait_ge(sem, value)
    eng.sem_inc(passed, 1)


def perceiver_block(nc, x, ctx_t, wq, bq, wkv, bk, bv, wo, bo, codes, scales, lora_a, lora_a_down, lora_b,
                    lora_b_down, w_base, b_base, enc, coefs, mask, fourier, ident_in, out):
    with ExitStack() as top:
        def sem(name):
            return top.enter_context(nc.semaphore(name))

        def sb(stack, name, shape, dt):
            return stack.enter_context(nc.sbuf_tensor(name, shape, dt))

        def psum(stack, name, shape):
            return stack.enter_context(nc.psum_tensor(name, shape, F32))

        weights = nc.dram_tensor("expanded_weights", [NT, P, TW], F32).ap()
        four_dram = nc.dram_tensor("folded_fourier", [RR, HID], F32).ap()

        ident = sb(top, "ident", [P, P], F32)
        acc = sb(top, "acc", [P, NKV, RT, D], F32)
        denom = sb(top, "denom", [P, NKV, RT], F32)
        maxes = sb(top, "maxes", [P, NKV, RT, 3], F32)
        bv_sb = sb(top, "bv_sb", [P, NKV], F32)

        phase1 = ExitStack()
        wkv_hi = sb(phase1, "wkv_hi", [P, KT, 2 * NKV * D], F32R)
        wkv_lo = sb(phase1, "wkv_lo", [P, KT, 2 * NKV * D], F32R)
        q_hi = sb(phase1, "q_hi", [P, NKV, ROWS], F32R)
        q_lo = sb(phase1, "q_lo", [P, NKV, ROWS], F32R)
        bk_sb = sb(phase1, "bk_sb", [P, NKV], F32)

        prologue(nc, codes, scales, weights, x, wq, bq, wkv, bk, bv, coefs, mask, fourier, ident_in,
                 ident, acc, denom, maxes, bv_sb, bk_sb, four_dram, wkv_hi, wkv_lo, q_hi, q_lo, sem, sb, psum)
        attention(nc, ctx_t, codes, scales, weights, ident, acc, denom, maxes, bk_sb,
                  wkv_hi, wkv_lo, q_hi, q_lo, sem, sb, psum)
        phase1.close()
        tail(nc, wo, bo, weights, lora_a, lora_a_down, lora_b, lora_b_down, w_base, b_base, enc, out,
             ident, x, acc, denom, bv_sb, four_dram, sem, sb, psum)


def prologue(nc, codes, scales, weights, x, wq, bq, wkv, bk, bv, coefs, mask, fourier, ident_in, ident, acc, denom, maxes,
             bv_sb, bk_sb, four_dram, wkv_hi, wkv_lo, q_hi, q_lo, sem, sb, psum):
    with ExitStack() as st:
        x_sb = sb(st, "x_in_sb", [TOK, HID], F32)
        w_four = sb(st, "w_four_out", [RR, HID], F32)
        xhat = sb(st, "xhat0", [TOK, HID], F32)
        stats = sb(st, "stats0", [TOK, 6], F32)
        mv = sb(st, "mv0", [TOK, 4], F32)
        xt = sb(st, "xt0", [P, KT, TOK], F32)
        bq_sb = sb(st, "bq_sb", [P, NH], F32)
        wq_sb = sb(st, "wq_sb", [P, 2, KT, TW], F32)
        wkv_st = sb(st, "wkv_st", [P, 2, 2 * NKV * D], F32)
        q_f = sb(st, "q_f", [P, 2, 8 * TOK], F32)
        co = sb(st, "co", [P, KT, NEXP, RR], F32)
        mk = sb(st, "mk", [P, KT, NEXP, RR], U8)
        cm = sb(st, "cm", [P, KT, NEXP, RR], F32)
        ws = sb(st, "ws", [P, KT, RR], F32)
        four = sb(st, "four", [P, KT, HID], F32)
        p_x = psum(st, "p_x", [P, KT, TOK])
        p_q = psum(st, "p_q", [P, 2, 8 * TOK])
        p_w = psum(st, "p_w", [RR, HID])

        x_in, vecs_in = sem("x_in"), sem("vecs_in")
        wq_in = [sem(f"wq_in{i}") for i in range(2)]
        wkv_in = [sem(f"wkv_in{i}") for i in range(2)]
        coef_in = sem("coef_in")
        ln_step, var_ready, std_ready, xhat_ready = sem("ln_step0"), sem("var_ready0"), sem("std_ready0"), sem("xhat_ready0")
        xt_psum, xt_ready = sem("xt_psum0"), sem("xt_ready0")
        q_psum, q_biased, q_rounded = sem("q_psum"), sem("q_biased"), sem("q_rounded")
        wkv_rounded, wkv_split = sem("wkv_rounded"), sem("wkv_split")
        masked, summed, folded, folded_out, four_stored = sem("masked"), sem("summed"), sem("folded"), sem("folded_out"), sem("four_stored")
        NG = NH // 8
        e_code = sb(st, "e_code", [P, EXTRA * TW], I32)
        e_codef = sb(st, "e_codef", [P, EXTRA * TW], F32)
        e_scale = sb(st, "e_scale", [P, EXTRA * TW], F32)
        e_term = sb(st, "e_term", [P, 2, EXTRA * TW], F32)
        e_w = sb(st, "e_w", [P, EXTRA * TW], F32)
        e_in, e_step, e_added, e_done, e_stored = sem("e_in"), sem("e_step"), sem("e_added"), sem("e_done"), sem("e_stored")

        block = st.enter_context(nc.Block())

        @block.sync
        def _(sp):
            sp.dma_start(x_sb[:], x).then_inc(x_in, 16)
            sp.dma_start(ident[:], ident_in).then_inc(x_in, 16)
            for dst, src in ((bq_sb, bq), (bk_sb, bk), (bv_sb, bv)):
                sp.dma_start(dst[:], src).then_inc(vecs_in, 16)
            for e in range(EXTRA):
                tile = slice(e * TW, (e + 1) * TW)
                sp.dma_start(e_code[:, tile], codes[NCH * NKV + e]).then_inc(e_in, 16)
                for b in range(2):
                    sp.dma_start(e_scale[b * QBLK:(b + 1) * QBLK, tile],
                                 scales[NCH * NKV + e, b].partition_broadcast(QBLK)).then_inc(e_in, 16)
            for g in range(NG * 2):
                if g >= 2:
                    sp.wait_ge(q_psum, g - 1)
                sp.dma_start(wq_sb[:, g % 2], wq[:, :, g * TW:(g + 1) * TW]).then_inc(wq_in[g % 2], 16)
            sp.wait_ge(e_done, 1)
            for e in range(EXTRA):
                sp.dma_start(weights[NCH * NKV + e], e_w[:, e * TW:(e + 1) * TW]).then_inc(e_stored, 16)
            sp.wait_ge(e_stored, 16 * EXTRA)
            sp.wait_ge(folded_out, 1)
            sp.dma_start(four_dram, w_four[:]).then_inc(four_stored, 16)
            sp.wait_ge(four_stored, 16)

        @block.scalar
        def _(act):
            for k in range(KT):
                if k >= 2:
                    act.wait_ge(wkv_split, k - 1)
                act.dma_start(wkv_st[:, k % 2], wkv[:, k]).then_inc(wkv_in[k % 2], 16)
                if k == 1:
                    act.dma_start(co[:], coefs).then_inc(coef_in, 16)
                    act.dma_start(mk[:], mask).then_inc(coef_in, 16)
                    act.dma_start(four[:], fourier).then_inc(coef_in, 16)
                if k == 1:
                    act.wait_ge(var_ready, 1)
                    nc.scalar.activation(mv[:, 3:4], mv[:, 2:3], ACT.Sqrt).then_inc(std_ready, 1)

        @block.gpsimd
        def _(pool):
            pool.wait_ge(e_in, 48 * EXTRA)
            nc.gpsimd.tensor_copy(e_codef[:], e_code[:]).then_inc(e_step, 1)
            pool.wait_ge(e_step, 1)
            for c in range(16):
                if c >= 2:
                    pool.wait_ge(e_added, c - 1)
                nc.gpsimd.tensor_scalar(e_term[:, c % 2], e_codef[:], float(c), NF4[c], ALU.is_equal,
                                        ALU.mult).then_inc(e_step, 1)
            nc.gpsimd.memset(acc[:], 0.0)
            nc.gpsimd.memset(denom[:], 0.0)
            nc.gpsimd.memset(maxes[:], LOWEST)
            pool.wait_ge(coef_in, 48)
            nc.gpsimd.tensor_copy(cm[:], mk[:]).then_inc(masked, 1)
            pool.wait_ge(masked, 1)
            nc.gpsimd.tensor_tensor(cm[:], cm[:], co[:], ALU.mult).then_inc(masked, 1)
            pool.wait_ge(masked, 2)
            nc.gpsimd.tensor_tensor(ws[:], cm[:, :, 0, :], cm[:, :, 1, :], ALU.add).then_inc(masked, 1)
            pool.wait_ge(masked, 3)
            nc.gpsimd.tensor_tensor(ws[:], ws[:], cm[:, :, 2, :], ALU.add).then_inc(summed, 1)

        @block.vector
        def _(dve):
            dve.wait_ge(x_in, 32)
            nc.vector.bn_stats(stats[:], x_sb[:]).then_inc(ln_step, 1)
            dve.wait_ge(ln_step, 1)
            nc.vector.bn_aggr(mv[:, 0:2], stats[:]).then_inc(ln_step, 1)
            dve.wait_ge(ln_step, 2)
            nc.vector.tensor_scalar(mv[:, 2:3], mv[:, 1:2], EPS, None, ALU.add).then_inc(var_ready, 1)
            dve.wait_ge(std_ready, 1)
            nc.vector.reciprocal(mv[:, 2:3], mv[:, 3:4]).then_inc(ln_step, 1)
            dve.wait_ge(ln_step, 3)
            nc.vector.tensor_scalar(xhat[:], x_sb[:], mv[:, 0:1], mv[:, 2:3], ALU.subtract,
                                    ALU.mult).then_inc(xhat_ready, 1)
            dve.wait_ge(xt_psum, 1)
            nc.vector.tensor_copy(xt[:], p_x[:]).then_inc(xt_ready, 1)
            dve.wait_ge(vecs_in, 48)
            for k in range(KT):
                dve.wait_ge(wkv_in[k % 2], 16 * (k // 2 + 1))
                nc.vector.tensor_copy(wkv_hi[:, k], wkv_st[:, k % 2]).then_inc(wkv_rounded, 1)
                dve.wait_ge(wkv_rounded, k + 1)
                nc.vector.tensor_tensor(wkv_lo[:, k], wkv_st[:, k % 2], wkv_hi[:, k].bitcast(F32),
                                        ALU.subtract).then_inc(wkv_split, 1)
            for c in range(1, 16):
                dve.wait_ge(e_step, c + 2)
                if c >= 2:
                    dve.wait_ge(e_added, c - 1)
                nc.vector.tensor_tensor(e_w[:], e_w[:] if c > 1 else e_term[:, 0], e_term[:, c % 2],
                                        ALU.add).then_inc(e_added, 1)
            dve.wait_ge(e_added, 15)
            nc.vector.tensor_tensor(e_w[:], e_w[:], e_scale[:], ALU.mult).then_inc(e_done, 1)
            for g in range(NG):
                dve.wait_ge(q_psum, 2 * g + 2)
                heads = q_f[:, g % 2].rearrange("p (h t) -> p h t", h=8)
                nc.vector.tensor_tensor(heads, p_q[:, g % 2].rearrange("p (h t) -> p h t", h=8),
                                        bq_sb[:, 8 * g:8 * g + 8].unsqueeze(2).broadcast_to([P, 8, TOK]),
                                        ALU.add).then_inc(q_biased, 1)
                dve.wait_ge(q_biased, g + 1)
                two = slice(2 * g, 2 * g + 2)
                q3 = q_f[:, g % 2].rearrange("p (h r) -> p h r", h=2)
                nc.vector.tensor_copy(q_hi[:, two], q3).then_inc(q_rounded, 1)
                dve.wait_ge(q_rounded, g + 1)
                nc.vector.tensor_tensor(q_lo[:, two], q3, q_hi[:, two].bitcast(F32), ALU.subtract)
            dve.wait_ge(folded, 1)
            nc.vector.tensor_scalar(w_four[:], p_w[:], 0.5, None, ALU.mult).then_inc(folded_out, 1)

        @block.tensor
        def _(pe):
            pe.wait_ge(xhat_ready, 1)
            for k in range(KT):
                t = nc.tensor.transpose(p_x[:, k, :], xhat[:, k * P:(k + 1) * P], ident[0:TOK, 0:TOK])
            t.then_inc(xt_psum, 1)
            pe.wait_ge(xt_ready, 1)
            for g in range(2 * NG):
                pe.wait_ge(wq_in[g % 2], 16 * (g // 2 + 1))
                if g >= 4 and g % 2 == 0:
                    pe.wait_ge(q_biased, g // 2 - 1)
                for h in range(4):
                    col = (g % 2) * 4 * TOK + h * TOK
                    for k in range(KT):
                        m = nc.tensor.matmul(p_q[:, (g // 2) % 2, col:col + TOK],
                                             wq_sb[:, g % 2, k, h * D:(h + 1) * D], xt[:, k, :],
                                             start=(k == 0), stop=(k == KT - 1))
                m.then_inc(q_psum, 1)
            pe.wait_ge(summed, 1)
            for k in range(KT):
                m = nc.tensor.matmul(p_w[:], ws[:, k, :], four[:, k, :], start=(k == 0), stop=(k == KT - 1))
            m.then_inc(folded, 1)


def attention(nc, ctx_t, codes, scales, weights, ident, acc, denom, maxes, bk_sb,
              wkv_hi, wkv_lo, q_hi, q_lo, sem, sb, psum):
    with ExitStack() as st:
        ctx_st = sb(st, "ctx_st", [P, PIECE], F32)
        ctx_hi = sb(st, "ctx_hi", [P, 2, KT, CHUNK], F32R)
        ctx_lo = sb(st, "ctx_lo", [P, 2, KT, CHUNK], F32R)
        v_hi = sb(st, "v_hi", [P, CT, 2 * D], F32R)
        v_lo = sb(st, "v_lo", [P, CT, 2 * D], F32R)
        k_hi = sb(st, "k_hi", [P, CHUNK], F32R)
        k_lo = sb(st, "k_lo", [P, CHUNK], F32R)
        probs = sb(st, "probs", [P, RT, CHUNK], F32)
        pt_hi = sb(st, "pt_hi", [P, CT, ROWS], F32R)
        pt_lo = sb(st, "pt_lo", [P, CT, ROWS], F32R)
        o_t = sb(st, "o_t", [P, ROWS], F32)
        newmax = sb(st, "newmax", [P, RT], F32)
        negmax = sb(st, "negmax", [P, RT], F32)
        drop = sb(st, "drop", [P, RT], F32)
        alpha = sb(st, "alpha", [P, 4, RT], F32)
        rowsum = sb(st, "rowsum", [P, 4, RT], F32)
        scale = sb(st, "scale", [P, TW], F32)
        code = sb(st, "code", [P, TW], I32)
        bit0 = sb(st, "bit0", [P, TW], U16)
        bit1 = sb(st, "bit1", [P, TW], U16)
        bit2 = sb(st, "bit2", [P, TW], U16)
        bit3 = sb(st, "bit3", [P, TW], U16)
        code16 = sb(st, "code16", [P, TW], U16)
        leaf = sb(st, "leaf", [P, 2, 5, HW], F32)

        p_kv = psum(st, "p_kv", [P, 2, 512])
        p_s = psum(st, "p_s", [P, 2, 512])
        p_t = psum(st, "p_t", [P, 2, 512])
        p_o = psum(st, "p_o", [P, 512])
        p_ot = psum(st, "p_ot", [P, 512])

        ctx_in, ctx_rounded, ctx_split = sem("ctx_in"), sem("ctx_rounded"), sem("ctx_split")
        kv_psum, kv_rounded, kv_split = sem("kv_psum"), sem("kv_rounded"), sem("kv_split")
        scores_psum, scores_out = sem("scores_psum"), sem("scores_out")
        stat_step, max_ready = sem("stat_step"), sem("max_ready")
        alpha_ready, exp_ready = sem("alpha_ready"), sem("exp_ready")
        pt_psum, pt_rounded, pt_split = sem("pt_psum"), sem("pt_rounded"), sem("pt_split")
        o_psum, o_out, ot_psum, ot_added = sem("o_psum"), sem("o_out"), sem("ot_psum"), sem("ot_added")
        code_in, scale_in = sem("code_in"), sem("scale_in")
        code_narrow, bits_ready = sem("code_narrow"), sem("bits_ready")
        leaves_ready, chosen, choice = sem("leaves_ready"), sem("chosen"), sem("choice")
        scaled = sem("scaled")
        weight_out = [sem(f"weight_out{b}") for b in range(2)]
        pool_passed, dve_passed = sem("pool_passed"), sem("dve_passed")

        NB = NCH * NKV
        KV_USES = CT + 4

        def v_use(s, h, t):
            return 2 + KV_USES * (4 * s + h // 2) + t

        def k_use(s, h, c):
            return 2 + KV_USES * (4 * s + h // 2) + CT + 2 * (h % 2) + c

        def v_bank(h, t):
            return (h // 2 + t) % 2

        def k_bank(h, c):
            return (h // 2 + 1 + c) % 2

        block = st.enter_context(nc.Block())

        @block.sync
        def _(sp):
            def load_ctx(s, piece, first=False):
                if not first:
                    sp.wait_ge(ctx_split, PIECES * s + piece)
                k, q = piece // 4, piece % 4
                sp.dma_start(ctx_st[:], ctx_t[s, k, :, q * PIECE:(q + 1) * PIECE]).then_inc(ctx_in, 16)

            def codes_of(n, first=False):
                if not first:
                    sp.wait_ge(code_narrow, n)
                sp.dma_start(code[:], codes[n]).then_inc(code_in, 16)

            def scales_of(n, first=False):
                if not first:
                    sp.wait_ge(scaled, 2 * n)
                for b in range(2):
                    sp.dma_start(scale[b * QBLK:(b + 1) * QBLK, :],
                                 scales[n, b].partition_broadcast(QBLK)).then_inc(scale_in, 16)

            def tile_out(n):
                for b in range(2):
                    sp.wait_ge(scaled, 2 * n + b + 1)
                    sp.dma_start(weights[n, :, b * HW:(b + 1) * HW], leaf[:, b, 4, :]).then_inc(weight_out[b], 16)

            for piece in range(PIECES):
                load_ctx(0, piece, piece == 0)
            codes_of(0, True)
            scales_of(0, True)

            def chunk(s, last):
                piece = 0
                for pair in range(NKV // 2):
                    n = NKV * s + 2 * pair
                    start = isinstance(n, int) and n == 0
                    if not last:
                        load_ctx(s + 1, piece)
                    codes_of(n + 1)
                    if not start:
                        tile_out(n - 1)
                        scales_of(n)
                    if not (last and pair == NKV // 2 - 1):
                        codes_of(n + 2)
                    tile_out(n)
                    scales_of(n + 1)
                    for q in range(1, PAIR_PIECES[pair]):
                        if not last:
                            load_ctx(s + 1, piece + q)
                    piece += PAIR_PIECES[pair]

            chunk(0, False)
            with sp.Fori(1, NCH - 1) as s:
                chunk(s, False)
            chunk(NCH - 1, True)
            tile_out(NB - 1)
            for b in range(2):
                sp.wait_ge(weight_out[b], 16 * NB)

        @block.gpsimd
        def _(pool):
            def split_ctx(s, piece, half):
                n, k = PIECES * s + piece, piece // 4
                keys = slice(piece % 4 * PIECE, (piece % 4 + 1) * PIECE)
                wait_apart(pool, ctx_in, 16 * (n + 1), pool_passed)
                nc.gpsimd.tensor_copy(ctx_hi[:, half, k, keys], ctx_st[:]).then_inc(ctx_rounded, 1)
                wait_apart(pool, ctx_rounded, n + 1, pool_passed)
                nc.gpsimd.tensor_tensor(ctx_lo[:, half, k, keys], ctx_st[:], ctx_hi[:, half, k, keys].bitcast(F32),
                                        ALU.subtract).then_inc(ctx_split, 1)

            def narrow(n, first=False):
                wait_apart(pool, code_in, 16 * (n + 1), pool_passed)
                if not first:
                    wait_apart(pool, bits_ready, n, pool_passed)
                nc.gpsimd.tensor_copy(code16[:], code[:]).then_inc(code_narrow, 1)

            def leaves(b, first_leaf, slots):
                for k, slot in enumerate(slots):
                    j = first_leaf + k
                    m = nc.gpsimd.tensor_scalar(leaf[:, b, slot, :], bit0[:, b * HW:(b + 1) * HW],
                                                NF4[2 * j + 1] - NF4[2 * j], NF4[2 * j], ALU.mult, ALU.add)
                m.then_inc(leaves_ready, 1)

            def low_leaves(n):
                wait_apart(pool, bits_ready, n + 1, pool_passed)
                if not (isinstance(n, int) and n == 0):
                    wait_apart(pool, scaled, 2 * n, pool_passed)
                for b in range(2):
                    leaves(b, 0, (0, 1, 2, 3))

            def high_leaves(n):
                for b in range(2):
                    wait_apart(pool, chosen, 4 * n + 1 + b, pool_passed)
                    if not (isinstance(n, int) and n == 0):
                        wait_apart(pool, weight_out[b], 16 * n, pool_passed)
                    leaves(b, 4, (1, 2, 3, 4))

            def apply_scales(n):
                wait_apart(pool, scale_in, 32 * (n + 1), pool_passed)
                for b in range(2):
                    wait_apart(pool, chosen, 4 * n + 3 + b, pool_passed)
                    nc.gpsimd.tensor_tensor(leaf[:, b, 4, :], leaf[:, b, 0, :], scale[:, b * HW:(b + 1) * HW],
                                            ALU.mult).then_inc(scaled, 1)

            for piece in range(PIECES):
                split_ctx(0, piece, 0)
            narrow(0, True)

            def chunk(s, par, last):
                piece = 0
                for pair in range(NKV // 2):
                    n = NKV * s + 2 * pair
                    if not (isinstance(n, int) and n == 0):
                        apply_scales(n - 1)
                    low_leaves(n)
                    high_leaves(n)
                    narrow(n + 1)
                    apply_scales(n)
                    if not last:
                        split_ctx(s + 1, piece, 1 - par)
                    low_leaves(n + 1)
                    if not (last and pair == NKV // 2 - 1):
                        narrow(n + 2)
                    for q in range(1, max(2, PAIR_PIECES[pair])):
                        if not last and q < PAIR_PIECES[pair]:
                            split_ctx(s + 1, piece + q, 1 - par)
                        if q == 1:
                            high_leaves(n + 1)
                    piece += PAIR_PIECES[pair]

            chunk(0, 0, False)
            with pool.Fori(0, NCH // 2 - 1) as s2:
                chunk(2 * s2 + 1, 1, False)
                chunk(2 * s2 + 2, 0, False)
            chunk(NCH - 2, 1, False)
            chunk(NCH - 1, 0, True)
            apply_scales(NB - 1)

        @block.tensor
        def _(pe):
            def project_keys(use, bank, half, h, c, k):
                cols = slice(h * D, (h + 1) * D)
                keys = slice(c * HALF, (c + 1) * HALF)
                m = split_matmuls(nc, p_kv[:, bank, 0:HALF], wkv_hi[:, k, cols], wkv_lo[:, k, cols],
                                  ctx_hi[:, half, k, keys], ctx_lo[:, half, k, keys],
                                  start=(k == 0), stop=(k == KT - 1))
                if k == KT - 1:
                    m.then_inc(kv_psum, 1)

            def weighted_values(i, h):
                pe.wait_ge(pt_split, 4 * i + 4)
                pe.wait_ge(kv_split, v_use_of(i, h) + CT)
                if not static_first(i):
                    pe.wait_ge(o_out, i)
                d = slice((h % 2) * D, (h % 2 + 1) * D)
                for t in range(CT):
                    m = split_matmuls(nc, p_o[:, 0:ROWS], v_hi[:, t, d], v_lo[:, t, d], pt_hi[:, t], pt_lo[:, t],
                                      start=(t == 0), stop=(t == CT - 1))
                m.then_inc(o_psum, 1)

            def v_use_of(i, h):
                return 2 + ((i - (h % 2)) * KV_USES) // 2 if isinstance(i, int) else None

            def static_first(i):
                return isinstance(i, int) and i == 0

            def turn_output(i):
                pe.wait_ge(o_out, i + 1)
                if not static_first(i):
                    pe.wait_ge(ot_added, i)
                for r in range(RT):
                    m = nc.tensor.transpose(p_ot[:, r * D:(r + 1) * D], o_t[:, r * P:(r + 1) * P], ident[:])
                m.then_inc(ot_psum, 1)

            def turn_probs(i, c, skip):
                if c == 0:
                    pe.wait_ge(exp_ready, 2 * i + 2)
                if not skip:
                    pe.wait_ge(pt_split, 4 * i + c - 1)
                for t in range(2 * c, min(2 * c + 2, CT)):
                    for r in range(RT):
                        col = (t % 2) * ROWS + r * P
                        m = nc.tensor.transpose(p_t[:, c % 2, col:col + P], probs[:, r, t * P:(t + 1) * P], ident[:])
                m.then_inc(pt_psum, 1)

            def scores(i, h, kuse, static):
                for c in range(2):
                    pe.wait_ge(kv_split, kuse + c + 1)
                    for r in range(RT):
                        bank = p_s[:, r, 0:HALF] if c == 0 else p_kv[:, k_bank((h - 1) % NKV, r), 0:HALF]
                        if c == 0 and not static:
                            pe.wait_ge(scores_out, 4 * i - 3 + r)
                        m = split_matmuls(nc, bank, q_hi[:, h, r * P:(r + 1) * P],
                                          q_lo[:, h, r * P:(r + 1) * P], k_hi[:, c * HALF:(c + 1) * HALF],
                                          k_lo[:, c * HALF:(c + 1) * HALF])
                        m.then_inc(scores_psum, 1)

            def values(s, h, half):
                for t in range(CT):
                    if t < 2:
                        pe.wait_ge(scores_out, 4 * (NKV * s + h) + 4)
                    pe.wait_ge(kv_split, v_use(s, h, t) - 1)
                    cols = slice((NKV + h) * D, (NKV + h + 2) * D)
                    for k in range(KT):
                        keys = slice(t * P, (t + 1) * P)
                        m = split_matmuls(nc, p_kv[:, v_bank(h, t), 0:2 * D], ctx_hi[:, half, k, keys],
                                          ctx_lo[:, half, k, keys], wkv_hi[:, k, cols], wkv_lo[:, k, cols],
                                          start=(k == 0), stop=(k == KT - 1))
                    m.then_inc(kv_psum, 1)

            def prev_values(s, h):
                i = NKV * s + h - 1
                hp = (h - 1) % NKV
                pair = 4 * s + h // 2 - (1 if h % 2 == 0 else 0)
                pe.wait_ge(pt_split, 4 * i + 4)
                pe.wait_ge(kv_split, 2 + KV_USES * pair + CT)
                if not static_first(i):
                    pe.wait_ge(o_out, i)
                d = slice((hp % 2) * D, (hp % 2 + 1) * D)
                for t in range(CT):
                    m = split_matmuls(nc, p_o[:, 0:ROWS], v_hi[:, t, d], v_lo[:, t, d], pt_hi[:, t], pt_lo[:, t],
                                      start=(t == 0), stop=(t == CT - 1))
                m.then_inc(o_psum, 1)

            def block_work(s, h, half, first, last):
                i = NKV * s + h
                first = first and h == 0
                last = last and h == NKV - 1
                kuse = 0 if first else k_use(s, h, 0) - 2 - (CT if h % 2 == 0 else 0)
                scores(i, h, kuse, first)
                if not first:
                    prev_values(s, h)
                if h % 2 == 0:
                    values(s, h, half)
                nh, nhalf = ((h + 1), half) if h + 1 < NKV else (0, 1 - half)
                if not last:
                    if nh == 0:
                        pe.wait_ge(ctx_split, PIECES * (s + 2))
                    pe.wait_ge(kv_split, k_use(s, h, 0) - 1)
                    pe.wait_ge(scores_out, 4 * i + 4)
                    for k in range(KT):
                        project_keys(None, k_bank(h, 0), nhalf, nh, 0, k)
                    if not first:
                        turn_output(i - 1)
                    turn_probs(i, 0, first)
                    pe.wait_ge(kv_split, k_use(s, h, 1) - 1)
                    project_keys(None, k_bank(h, 1), nhalf, nh, 1, 0)
                    turn_probs(i, 1, first)
                    project_keys(None, k_bank(h, 1), nhalf, nh, 1, 1)
                    project_keys(None, k_bank(h, 1), nhalf, nh, 1, 2)
                    turn_probs(i, 2, False)
                    project_keys(None, k_bank(h, 1), nhalf, nh, 1, 3)
                    turn_probs(i, 3, False)
                else:
                    turn_output(i - 1)
                    for c in range(4):
                        turn_probs(i, c, False)

            pe.wait_ge(ctx_split, PIECES)
            for c in range(2):
                for k in range(KT):
                    project_keys(None, k_bank(NKV - 1, c), 0, 0, c, k)
            for h in range(NKV):
                block_work(0, h, 0, True, False)
            with pe.Fori(0, NCH // 2 - 1) as s2:
                for h in range(NKV):
                    block_work(2 * s2 + 1, h, 1, False, False)
                for h in range(NKV):
                    block_work(2 * s2 + 2, h, 0, False, False)
            for h in range(NKV):
                block_work(NCH - 2, h, 1, False, False)
            for h in range(NKV):
                block_work(NCH - 1, h, 0, False, True)
            prev_values(NCH, 0)
            turn_output(NB - 1)

        @block.scalar
        def _(act):
            def round_kv(use, dst, src, bias=None):
                act.wait_ge(kv_psum, use + 1)
                nc.scalar.activation(dst, src, ACT.Identity, bias=0.0 if bias is None else bias).then_inc(kv_rounded, 1)

            def round_keys(use, bank, nh, c):
                round_kv(use, k_hi[:, c * HALF:(c + 1) * HALF], p_kv[:, bank, 0:HALF], bk_sb[:, nh:nh + 1])

            def round_probs(i, c):
                act.wait_ge(pt_psum, 4 * i + c + 1)
                n = min(2, CT - 2 * c)
                nc.scalar.activation(pt_hi[:, 2 * c:2 * c + n, :].rearrange("p t q -> p (t q)"),
                                     p_t[:, c % 2, 0:n * ROWS], ACT.Copy).then_inc(pt_rounded, 1)

            def output_out(i):
                act.wait_ge(o_psum, i + 1)
                nc.scalar.activation(o_t[:], p_o[:, 0:ROWS], ACT.Copy).then_inc(o_out, 1)

            def block_work(s, h, first, last):
                i = NKV * s + h
                par = h % 4
                act.wait_ge(max_ready, i + 1)
                nc.scalar.activation(alpha[:, par, :], drop[:], ACT.Exp).then_inc(alpha_ready, 1)
                for r in range(RT):
                    nc.scalar.activation(probs[:, r, :], probs[:, r, :], ACT.Exp, bias=negmax[:, r:r + 1],
                                         accum_out=rowsum[:, par, r:r + 1]).then_inc(exp_ready, 1)
                if not (first and h == 0):
                    output_out(i - 1)
                if h % 2 == 0:
                    for t in range(CT):
                        round_kv(v_use(s, h, t), v_hi[:, t], p_kv[:, v_bank(h, t), 0:2 * D])
                if last and h == NKV - 1:
                    for c in range(4):
                        round_probs(i, c)
                    return
                nh = (h + 1) % NKV
                round_keys(k_use(s, h, 0), k_bank(h, 0), nh, 0)
                for c in range(3):
                    round_probs(i, c)
                round_keys(k_use(s, h, 1), k_bank(h, 1), nh, 1)
                round_probs(i, 3)

            for c in range(2):
                round_keys(c, k_bank(NKV - 1, c), 0, c)
            for h in range(NKV):
                block_work(0, h, True, False)
            with act.Fori(1, NCH - 1) as s:
                for h in range(NKV):
                    block_work(s, h, False, False)
            for h in range(NKV):
                block_work(NCH - 1, h, False, True)
            output_out(NB - 1)

        @block.vector
        def _(dve):
            def split_kv(use, dst, src, hi, bias=None):
                dve.wait_ge(kv_rounded, use + 1)
                if bias is None:
                    nc.vector.tensor_tensor(dst, src, hi.bitcast(F32), ALU.subtract).then_inc(kv_split, 1)
                else:
                    nc.vector.scalar_tensor_tensor(dst, src, bias, hi.bitcast(F32), ALU.add,
                                                   ALU.subtract).then_inc(kv_split, 1)

            def split_keys(use, bank, nh, c):
                keys = slice(c * HALF, (c + 1) * HALF)
                split_kv(use, k_lo[:, keys], p_kv[:, bank, 0:HALF], k_hi[:, keys], bk_sb[:, nh:nh + 1])

            def split_probs(i, c):
                dve.wait_ge(pt_rounded, 4 * i + c + 1)
                n = min(2, CT - 2 * c)
                nc.vector.tensor_tensor(pt_lo[:, 2 * c:2 * c + n, :].rearrange("p t q -> p (t q)"),
                                        p_t[:, c % 2, 0:n * ROWS],
                                        pt_hi[:, 2 * c:2 * c + n, :].rearrange("p t q -> p (t q)").bitcast(F32),
                                        ALU.subtract).then_inc(pt_split, 1)

            def add_output(i, h):
                dve.wait_ge(alpha_ready, i + 1)
                dve.wait_ge(ot_psum, i + 1)
                par = h % 4
                for r in range(RT):
                    nc.vector.scalar_tensor_tensor(denom[:, h, r:r + 1], denom[:, h, r:r + 1], alpha[:, par, r:r + 1],
                                                   rowsum[:, par, r:r + 1], ALU.mult, ALU.add)
                for r in range(RT):
                    m = nc.vector.scalar_tensor_tensor(acc[:, h, r, :], acc[:, h, r, :], alpha[:, par, r:r + 1],
                                                       p_ot[:, r * D:(r + 1) * D], ALU.mult, ALU.add)
                m.then_inc(ot_added, 1)

            def score_stats(i, h):
                for c in range(2):
                    for r in range(RT):
                        bank = p_s[:, r, 0:HALF] if c == 0 else p_kv[:, k_bank((h - 1) % NKV, r), 0:HALF]
                        dve.wait_ge(scores_psum, 4 * i + 2 * c + r + 1)
                        nc.vector.tensor_scalar(probs[:, r, c * HALF:(c + 1) * HALF], bank, SCALE, None,
                                                ALU.mult, ALU.max,
                                                accum_out=maxes[:, h, r, 1 + c:2 + c]).then_inc(scores_out, 1)
                dve.wait_ge(scores_out, 4 * i + 4)
                nc.vector.tensor_reduce(newmax[:], maxes[:, h], AX_X, ALU.max).then_inc(stat_step, 1)
                dve.wait_ge(stat_step, 2 * i + 1)
                nc.vector.tensor_scalar(negmax[:], newmax[:], -1.0, None, ALU.mult)
                nc.vector.tensor_tensor(drop[:], maxes[:, h, :, 0], newmax[:], ALU.subtract).then_inc(max_ready, 1)
                dve.wait_ge(max_ready, i + 1)
                nc.vector.tensor_copy(maxes[:, h, :, 0], newmax[:]).then_inc(stat_step, 1)

            def take_bits(n, first=False):
                dve.wait_ge(code_narrow, n + 1)
                if not (isinstance(n, int) and n == 0):
                    dve.wait_ge(chosen, 4 * n)
                for bit, dst in ((0, bit0), (1, bit1), (2, bit2), (3, bit3)):
                    m = nc.vector.tensor_scalar(dst[:], code16[:], 1 << bit, None, ALU.bitwise_and)
                m.then_inc(bits_ready, 1)

            def take(b, bit, slot, other):
                return nc.vector.copy_predicated(leaf[:, b, slot, :], bit[:, b * HW:(b + 1) * HW], leaf[:, b, other, :])

            def low_by_bit1(n, b):
                wait_apart(dve, leaves_ready, 4 * n + 1 + b, dve_passed)
                take(b, bit1, 0, 1)
                take(b, bit1, 2, 3).then_inc(choice, 1)

            def low_by_bit2(n, b):
                wait_apart(dve, choice, 6 * n + 1 + b, dve_passed)
                take(b, bit2, 0, 2).then_inc(chosen, 1)

            def high_by_bit1(n, b):
                wait_apart(dve, leaves_ready, 4 * n + 3 + b, dve_passed)
                take(b, bit1, 1, 2)
                take(b, bit1, 3, 4).then_inc(choice, 1)

            def high_by_bit2(n, b):
                wait_apart(dve, choice, 6 * n + 3 + b, dve_passed)
                take(b, bit2, 1, 3).then_inc(choice, 1)

            def all_by_bit3(n, b):
                wait_apart(dve, choice, 6 * n + 5 + b, dve_passed)
                take(b, bit3, 0, 1).then_inc(chosen, 1)

            def both_halves(n, *choices):
                for choose in choices:
                    for b in range(2):
                        choose(n, b)

            def block_work(s, h, first, last):
                i = NKV * s + h
                score_stats(i, h)
                if not (first and h < 2):
                    add_output(i - 2, (h - 2) % NKV)
                if h % 2 == 0:
                    if not (first and h == 0):
                        both_halves(i - 1, high_by_bit1, high_by_bit2, all_by_bit3)
                    for t in range(CT):
                        split_kv(v_use(s, h, t), v_lo[:, t], p_kv[:, v_bank(h, t), 0:2 * D], v_hi[:, t])
                        if t == 0:
                            take_bits(i)
                        if t in (2, 3):
                            low_by_bit1(i, t - 2)
                        if t == 4:
                            both_halves(i, low_by_bit2)
                        if t == 6:
                            both_halves(i, high_by_bit1, high_by_bit2, all_by_bit3)
                else:
                    both_halves(i, low_by_bit1, low_by_bit2)
                if last and h == NKV - 1:
                    add_output(i - 1, (h - 1) % NKV)
                    for c in range(4):
                        split_probs(i, c)
                    return
                nh = (h + 1) % NKV
                split_keys(k_use(s, h, 0), k_bank(h, 0), nh, 0)
                for c in range(3):
                    split_probs(i, c)
                    if c == 1 and h % 2 == 0:
                        take_bits(i + 1)
                split_keys(k_use(s, h, 1), k_bank(h, 1), nh, 1)
                split_probs(i, 3)

            for c in range(2):
                split_keys(c, k_bank(NKV - 1, c), 0, c)
            for h in range(NKV):
                block_work(0, h, True, False)
            with dve.Fori(1, NCH - 1) as s:
                for h in range(NKV):
                    block_work(s, h, False, False)
            for h in range(NKV):
                block_work(NCH - 1, h, False, True)
            both_halves(NB - 1, high_by_bit1, high_by_bit2, all_by_bit3)
            add_output(NB - 1, NKV - 1)


def tail(nc, wo, bo, weights, lora_a, lora_a_down, lora_b, lora_b_down, w_base, b_base, enc, out,
         ident, x, acc, denom, bv_sb, four_dram, sem, sb, psum):
    WB = 10
    with ExitStack() as st:
        wring = sb(st, "wring", [P, WB, TW], F32)
        o_n = sb(st, "o_n", [P, NKV, RT, D], F32)
        rden = sb(st, "rden", [P, NKV, RT], F32)
        ot = sb(st, "ot", [P, NKV, ROWS], F32)
        x_sb = sb(st, "x_sb", [TOK, HID], F32)
        w_four = sb(st, "w_four", [RR, HID], F32)
        bo_sb = sb(st, "bo_sb", [TOK, HID], F32)
        bb_sb = sb(st, "bb_sb", [TOK, HID], F32)
        la = sb(st, "la", [P, KT, 6 * RANK], F32)
        lad = sb(st, "lad", [P, FT, RANK], F32)
        lb_qkv = sb(st, "lb_qkv", [3 * RANK, HID], F32)
        lb_o = sb(st, "lb_o", [RANK, HID], F32)
        lb_gu = sb(st, "lb_gu", [RANK, 2 * FFN], F32)
        lb_d = sb(st, "lb_d", [RANK, HID], F32)
        wb = sb(st, "wb", [P, KT, HID], F32)
        en = sb(st, "en", [P, KT, RR], F32)
        xa = sb(st, "xa", [TOK, HID], F32)
        z = sb(st, "z", [TOK, HID], F32)
        y = sb(st, "y", [TOK, HID], F32)
        xb = sb(st, "xb", [TOK, HID], F32)
        z2 = sb(st, "z2", [TOK, HID], F32)
        av = sb(st, "av", [TOK, HID], F32)
        fin = sb(st, "fin", [TOK, HID], F32)
        res = sb(st, "res", [TOK, HID], F32)
        sums = sb(st, "sums", [TOK, HID], F32)
        zt = sb(st, "zt", [P, KT, TOK], F32)
        at = sb(st, "at", [P, KT, TOK], F32)
        yt = sb(st, "yt", [P, KT, TOK], F32)
        z2t = sb(st, "z2t", [P, KT, TOK], F32)
        gu = sb(st, "gu", [TOK, 2 * FFN], F32)
        eg = sb(st, "eg", [TOK, FFN], F32)
        rg = sb(st, "rg", [TOK, FFN], F32)
        ht = sb(st, "ht", [P, FT, TOK], F32)
        e_qkv = sb(st, "e_qkv", [3 * RANK, TOK], F32)
        e_small = sb(st, "e_small", [RANK, 4, TOK], F32)
        e_f = sb(st, "e_f", [RR, TOK], F32)
        stats = sb(st, "stats", [TOK, 2, 6], F32)
        mv = sb(st, "mv", [TOK, 2, 4], F32)

        pb = [psum(st, f"pb{i}", [P, 512]) for i in range(8)]

        small_in = sem("small_in")
        w_in = [sem(f"w_in{i}") for i in range(WB)]
        w_used = sem("w_used")
        PARTS = NH + NT
        block = st.enter_context(nc.Block())
        order = list(range(0, ATT_TILES))
        order += [ATT_TILES + k * GU_COLS + c for c in range(GU_COLS) for k in range(KT)]
        order += [ATT_TILES + GU_TILES + j for j in range(FT)]
        smalls = [(bo_sb[:], bo.partition_broadcast(TOK)), (bb_sb[:], b_base.partition_broadcast(TOK)),
                  (la[:], lora_a), (lad[:], lora_a_down), (lb_qkv[:], lora_b[0:3 * RANK, 0:HID]),
                  (lb_o[:], lora_b[3 * RANK:4 * RANK, 0:HID]), (lb_gu[:, 0:FFN], lora_b[4 * RANK:5 * RANK, :]),
                  (lb_gu[:, FFN:2 * FFN], lora_b[5 * RANK:6 * RANK, :]), (lb_d[:], lora_b_down),
                  (wb[:], w_base), (en[:], enc), (x_sb[:], x), (w_four[:], four_dram)]

        names = {}

        def step(name):
            if name not in names:
                names[name] = sem(name)
            return names[name]

        @block.scalar
        def _(act):
            for dst, src in smalls:
                act.dma_start(dst, src).then_inc(small_in, 16)

            def root(n):
                act.wait_ge(step(f"variance{n}"), 1)
                nc.scalar.activation(mv[:, n, 3:4], mv[:, n, 2:3], ACT.Sqrt).then_inc(step(f"deviation{n}"), 1)

            root(0)
            act.wait_ge(step("gu_out"), 1)
            nc.scalar.activation(eg[:], gu[:, 0:FFN], ACT.Exp, scale=-1.0).then_inc(step("exp_gate"), 1)
            root(1)

        @block.sync
        def _(sp):
            for n in range(PARTS):
                if n >= WB:
                    sp.wait_ge(w_used, n - WB + 1)
                src = wo[n] if n < NH else weights[order[n - NH]]
                sp.dma_start(wring[:, n % WB, :], src).then_inc(w_in[n % WB], 16)
            sp.wait_ge(step("final"), 1)
            sp.dma_start(out, res[:]).then_inc(step("stored"), 16)
            sp.wait_ge(step("stored"), 16)

        @block.vector
        def _(dve):
            nc.vector.reciprocal(rden[:], denom[:]).then_inc(step("reciprocals"), 1)
            dve.wait_ge(step("reciprocals"), 1)
            for h in range(NKV):
                for r in range(RT):
                    m = nc.vector.tensor_scalar(o_n[:, h, r, :], acc[:, h, r, :], rden[:, h, r:r + 1], None, ALU.mult)
                m.then_inc(step("divided"), 1)
            for h in range(NKV):
                dve.wait_ge(step("attn_turned"), h + 1)
                nc.vector.tensor_scalar(ot[:, h, :], pb[h % 2][:, 0:ROWS], bv_sb[:, h:h + 1], None,
                                        ALU.add).then_inc(step("attn_t"), 1)
            dve.wait_ge(step("attn_psum"), 1)
            dve.wait_ge(small_in, 16 * len(smalls))
            nc.vector.tensor_tensor(sums[:], pb[2][0:TOK, :], bo_sb[:], ALU.add).then_inc(step("with_bo"), 1)
            dve.wait_ge(step("with_bo"), 1)
            nc.vector.tensor_tensor(xa[:], sums[:], x_sb[:], ALU.add).then_inc(step("xa_ready"), 1)

            def norm(n, src, dst, ready):
                dve.wait_ge(step(ready), 1)
                nc.vector.bn_stats(stats[:, n], src[:]).then_inc(step(f"moments{n}"), 1)
                dve.wait_ge(step(f"moments{n}"), 1)
                nc.vector.bn_aggr(mv[:, n, 0:2], stats[:, n]).then_inc(step(f"mean{n}"), 1)
                dve.wait_ge(step(f"mean{n}"), 1)
                nc.vector.tensor_scalar(mv[:, n, 2:3], mv[:, n, 1:2], EPS, None, ALU.add).then_inc(step(f"variance{n}"), 1)
                dve.wait_ge(step(f"deviation{n}"), 1)
                nc.vector.reciprocal(mv[:, n, 2:3], mv[:, n, 3:4]).then_inc(step(f"inverse{n}"), 1)
                dve.wait_ge(step(f"inverse{n}"), 1)
                nc.vector.tensor_scalar(dst[:], src[:], mv[:, n, 0:1], mv[:, n, 2:3], ALU.subtract,
                                        ALU.mult).then_inc(step(f"normed{n}"), 1)

            def turned(name, dst, bank):
                dve.wait_ge(step(f"{name}_turned"), 1)
                nc.vector.tensor_copy(dst[:], bank[:, 0:KT * TOK].rearrange("p (k t) -> p k t", k=KT)).then_inc(
                    step(f"{name}_t"), 1)

            norm(0, xa, z, "xa_ready")
            turned("z", zt, pb[0])
            dve.wait_ge(step("low_qkv"), 1)
            nc.vector.tensor_copy(e_qkv[:], pb[3][0:3 * RANK, 0:TOK]).then_inc(step("e_qkv"), 1)
            dve.wait_ge(step("qkv_psum"), 1)
            nc.vector.tensor_scalar(av[:], pb[2][0:TOK, :], 1.0 / 3.0, None, ALU.mult).then_inc(step("av_ready"), 1)
            turned("a", at, pb[0])
            dve.wait_ge(step("low_o"), 1)
            nc.vector.tensor_copy(e_small[:, 0], pb[3][0:RANK, 0:TOK]).then_inc(step("e_o"), 1)
            dve.wait_ge(step("o_psum_t"), 1)
            nc.vector.tensor_tensor(y[:], pb[2][0:TOK, :], z[:], ALU.add).then_inc(step("y_ready"), 1)
            turned("y", yt, pb[0])
            for j in range(2):
                dve.wait_ge(step(f"low_gu{j}"), 1)
                nc.vector.tensor_copy(e_small[:, 1 + j], pb[0][0:RANK, 256 + j * TOK:256 + (j + 1) * TOK]).then_inc(
                    step(f"e_gu{j}"), 1)
            for c in range(GU_COLS):
                dve.wait_ge(step("gu_psum"), c + 1)
                m = nc.vector.tensor_copy(gu[:, c * TW:(c + 1) * TW], pb[1 + c][0:TOK, :])
            m.then_inc(step("gu_out"), 1)
            dve.wait_ge(step("exp_gate"), 1)
            nc.vector.tensor_scalar(rg[:], eg[:], 1.0, None, ALU.add).then_inc(step("one_plus"), 1)
            dve.wait_ge(step("one_plus"), 1)
            nc.vector.reciprocal(eg[:], rg[:]).then_inc(step("gate"), 1)
            dve.wait_ge(step("gate"), 1)
            nc.vector.tensor_tensor(rg[:], eg[:], gu[:, 0:FFN], ALU.mult).then_inc(step("silu"), 1)
            dve.wait_ge(step("silu"), 1)
            nc.vector.tensor_tensor(eg[:], rg[:], gu[:, FFN:2 * FFN], ALU.mult).then_inc(step("h_ready"), 1)
            for half in range(2):
                dve.wait_ge(step("h_turned"), half + 1)
                nc.vector.tensor_copy(ht[:, 7 * half:7 * half + 7, :],
                                      pb[half][:, 0:7 * TOK].rearrange("p (k t) -> p k t", k=7)).then_inc(step("h_t"), 1)
            dve.wait_ge(step("low_d"), 1)
            nc.vector.tensor_copy(e_small[:, 3], pb[3][0:RANK, 0:TOK]).then_inc(step("e_d"), 1)
            nc.vector.tensor_tensor(fin[:], y[:], xa[:], ALU.add).then_inc(step("y_plus_xa"), 1)
            dve.wait_ge(step("y_plus_xa"), 1)
            dve.wait_ge(step("d_psum"), 1)
            nc.vector.tensor_tensor(xb[:], pb[2][0:TOK, :], fin[:], ALU.add).then_inc(step("xb_ready"), 1)
            norm(1, xb, z2, "xb_ready")
            nc.vector.tensor_tensor(sums[:], xb[:], bb_sb[:], ALU.add).then_inc(step("with_bb"), 1)
            turned("z2", z2t, pb[0])
            dve.wait_ge(step("low_f"), 1)
            nc.vector.tensor_copy(e_f[:], pb[3][0:RR, 0:TOK]).then_inc(step("e_f"), 1)
            dve.wait_ge(step("f_psum"), 1)
            dve.wait_ge(step("with_bb"), 1)
            nc.vector.tensor_tensor(res[:], pb[4][0:TOK, :], sums[:], ALU.add).then_inc(step("final"), 1)

        @block.tensor
        def _(pe):
            used = [0]

            def product(dst, lhs, start, stop=False):
                n = used[0]
                pe.wait_ge(w_in[n % WB], 16 * (n // WB + 1))
                used[0] += 1
                return nc.tensor.matmul(dst, lhs, wring[:, n % WB, :], start=start, stop=stop)

            def turn(name, src, dst):
                for k in range(KT):
                    m = nc.tensor.transpose(dst[:, k * TOK:(k + 1) * TOK], src[:, k * P:(k + 1) * P],
                                            ident[0:TOK, 0:TOK])
                m.then_inc(step(f"{name}_turned"), 1)

            for h in range(NKV):
                pe.wait_ge(step("divided"), h + 1)
                if h >= 2:
                    pe.wait_ge(step("attn_t"), h - 1)
                for r in range(RT):
                    m = nc.tensor.transpose(pb[h % 2][:, r * P:(r + 1) * P], o_n[:, h, r, :], ident[:])
                m.then_inc(step("attn_turned"), 1)
            for h in range(NH):
                pe.wait_ge(step("attn_t"), h // G + 1)
                m = product(pb[2][0:TOK, :], ot[:, h // G, (h % G) * TOK:(h % G + 1) * TOK], h == 0, h == NH - 1)
                m.then_inc(w_used, 1)
            nc.tensor.matmul(pb[3][0:TOK, 0:2], ident[:, 0:TOK], ident[:, 0:2], start=True, stop=True).then_inc(
                step("attn_psum"), 1)

            pe.wait_ge(small_in, 16 * len(smalls))
            pe.wait_ge(step("normed0"), 1)
            pe.wait_ge(step("attn_t"), NKV)
            turn("z", z, pb[0])
            pe.wait_ge(step("z_t"), 1)
            for k in range(KT):
                m = nc.tensor.matmul(pb[3][0:3 * RANK, 0:TOK], la[:, k, 0:3 * RANK], zt[:, k], start=(k == 0),
                                     stop=(k == KT - 1))
            m.then_inc(step("low_qkv"), 1)
            for n in range(3 * KT):
                product(pb[2][0:TOK, :], zt[:, n % KT], n == 0).then_inc(w_used, 1)
            pe.wait_ge(step("e_qkv"), 1)
            nc.tensor.matmul(pb[2][0:TOK, :], e_qkv[:], lb_qkv[:], start=False, stop=True).then_inc(step("qkv_psum"), 1)
            pe.wait_ge(step("av_ready"), 1)
            turn("a", av, pb[0])
            pe.wait_ge(step("a_t"), 1)
            for k in range(KT):
                m = nc.tensor.matmul(pb[3][0:RANK, 0:TOK], la[:, k, 3 * RANK:4 * RANK], at[:, k], start=(k == 0),
                                     stop=(k == KT - 1))
            m.then_inc(step("low_o"), 1)
            for k in range(KT):
                product(pb[2][0:TOK, :], at[:, k], k == 0).then_inc(w_used, 1)
            pe.wait_ge(step("e_o"), 1)
            nc.tensor.matmul(pb[2][0:TOK, :], e_small[:, 0], lb_o[:], start=False, stop=True).then_inc(
                step("o_psum_t"), 1)
            pe.wait_ge(step("y_ready"), 1)
            turn("y", y, pb[0])
            pe.wait_ge(step("y_t"), 1)
            for j in range(2):
                for k in range(KT):
                    m = nc.tensor.matmul(pb[0][0:RANK, 256 + j * TOK:256 + (j + 1) * TOK],
                                         la[:, k, (4 + j) * RANK:(5 + j) * RANK], yt[:, k], start=(k == 0),
                                         stop=(k == KT - 1))
                m.then_inc(step(f"low_gu{j}"), 1)
                pe.wait_ge(step(f"e_gu{j}"), 1)
            for c in range(GU_COLS):
                for k in range(KT):
                    product(pb[1 + c][0:TOK, :], yt[:, k], k == 0).then_inc(w_used, 1)
                lo, hi = c * TW, (c + 1) * TW
                parts = [(0, lo, min(hi, FFN))] * (lo < FFN) + [(1, max(lo, FFN), hi)] * (hi > FFN)
                for n, (j, a, b) in enumerate(parts):
                    m = nc.tensor.matmul(pb[1 + c][0:TOK, a - lo:b - lo], e_small[:, 1 + j], lb_gu[:, a:b],
                                         start=False, stop=(n == len(parts) - 1))
                m.then_inc(step("gu_psum"), 1)
            pe.wait_ge(step("h_ready"), 1)
            for t in range(FT):
                m = nc.tensor.transpose(pb[t // 7][:, (t % 7) * TOK:(t % 7 + 1) * TOK], eg[:, t * P:(t + 1) * P],
                                        ident[0:TOK, 0:TOK])
                if t % 7 == 6:
                    m.then_inc(step("h_turned"), 1)
            pe.wait_ge(step("h_t"), 2)
            for t in range(FT):
                m = nc.tensor.matmul(pb[3][0:RANK, 0:TOK], lad[:, t], ht[:, t], start=(t == 0), stop=(t == FT - 1))
            m.then_inc(step("low_d"), 1)
            for t in range(FT):
                product(pb[2][0:TOK, :], ht[:, t], t == 0).then_inc(w_used, 1)
            pe.wait_ge(step("e_d"), 1)
            nc.tensor.matmul(pb[2][0:TOK, :], e_small[:, 3], lb_d[:], start=False, stop=True).then_inc(step("d_psum"), 1)
            pe.wait_ge(step("normed1"), 1)
            turn("z2", z2, pb[0])
            pe.wait_ge(step("z2_t"), 1)
            for k in range(KT):
                m = nc.tensor.matmul(pb[3][0:RR, 0:TOK], en[:, k], z2t[:, k], start=(k == 0), stop=(k == KT - 1))
            m.then_inc(step("low_f"), 1)
            for k in range(KT):
                nc.tensor.matmul(pb[4][0:TOK, :], z2t[:, k], wb[:, k], start=(k == 0), stop=False)
            pe.wait_ge(step("e_f"), 1)
            nc.tensor.matmul(pb[4][0:TOK, :], e_f[:], w_four[:], start=False, stop=True).then_inc(step("f_psum"), 1)


def fourier_matrix(n):
    t = np.arange(n)
    rows = np.zeros((n, n))
    rows[0] = 1.0 / np.sqrt(n)
    for f in range(1, (n - 1) // 2 + 1):
        rows[2 * f - 1] = np.sqrt(2.0 / n) * np.cos(2 * np.pi * f * t / n)
        rows[2 * f] = np.sqrt(2.0 / n) * np.sin(2 * np.pi * f * t / n)
    rows[n - 1] = (1.0 - 2.0 * (t % 2)) / np.sqrt(n)
    return rows.astype(np.float32)


def kernel(**inputs):
    import numpy as _np
    import concourse.bacc as _bacc
    from concourse import mybir as _mybir
    from concourse.bass_utils import run_bass_kernel_spmd as _run

    a = {k: _np.asarray(v) for k, v in inputs.items()}

    def k_tiles(m):
        return m.reshape(-1, P, m.shape[1]).transpose(1, 0, 2)

    def weight_tiles(m):
        o, i = m.shape
        return m.T.reshape(i // P, P, o // TW, TW).transpose(0, 2, 1, 3).reshape(-1, P, TW)

    def scale_tiles(m):
        o, b = m.shape
        return m.T.reshape(b // 2, 2, o // TW, TW).transpose(0, 2, 1, 3).reshape(-1, 2, TW)

    def all_tiles(f, att, gate_up, down):
        return _np.concatenate([f(m) for m in att] + [f(_np.concatenate([gate_up[0], gate_up[1]], 0)), f(down)])

    lb_gu = a["L0_attn_lora_B_gu"]
    lb = _np.zeros((6 * RANK, FFN), _np.float32)
    for m in range(4):
        lb[m * RANK:(m + 1) * RANK, 0:HID] = a["L0_attn_lora_B_attn"][m].T
    for m in range(2):
        lb[(4 + m) * RANK:(5 + m) * RANK] = lb_gu[m].T
    coefs = _np.concatenate([a["L0_ffn_coefs0"], a["L0_ffn_coefs1"]], 2)
    mask = _np.concatenate([a["L0_ffn_mask0"], a["L0_ffn_mask1"]], 2)
    laid = {
        "x": a["x"].reshape(TOK, HID),
        "ctx_t": a["ctx_4096"].reshape(NCH, CHUNK, KT, P).transpose(0, 2, 3, 1),
        "wq": k_tiles(a["L0_xattn_Wq"]),
        "bq": a["L0_xattn_bq"].reshape(NH, D).T,
        "wkv": k_tiles(a["L0_xattn_Wkv"]),
        "bk": a["L0_xattn_bkv"][:NKV * D].reshape(NKV, D).T,
        "bv": a["L0_xattn_bkv"][NKV * D:].reshape(NKV, D).T,
        "wo": a["L0_xattn_Wo"].reshape(NH, D, HID),
        "bo": a["L0_xattn_bo"],
        "codes": all_tiles(weight_tiles, a["L0_attn_codes_attn"], a["L0_attn_codes_gu"], a["L0_attn_codes_down"]),
        "scales": all_tiles(scale_tiles, a["L0_attn_scales_attn"], a["L0_attn_scales_gu"], a["L0_attn_scales_down"]),
        "lora_a": k_tiles(a["L0_attn_lora_A_h"].reshape(6 * RANK, HID).T),
        "lora_a_down": k_tiles(a["L0_attn_lora_A_down"].T),
        "lora_b": lb,
        "lora_b_down": a["L0_attn_lora_B_down"].T,
        "w_base": k_tiles(a["L0_ffn_W_base"].T),
        "b_base": a["L0_ffn_b_base"],
        "enc": k_tiles(_np.concatenate([a["L0_ffn_enc0"], a["L0_ffn_enc1"]], 0).T),
        "coefs": coefs.transpose(1, 0, 2).reshape(KT, P, NEXP, RR).transpose(1, 0, 2, 3),
        "mask": mask.transpose(1, 0, 2).reshape(KT, P, NEXP, RR).transpose(1, 0, 2, 3),
        "fourier": k_tiles(fourier_matrix(HID)),
        "ident": _np.eye(P, dtype=_np.float32),
    }
    nc = _bacc.Bacc("TRN2", target_bir_lowering=False, num_devices=1)
    arrays, args = {}, []
    for name, m in laid.items():
        m = _np.ascontiguousarray(m)
        arrays[f"in_{name}"] = m
        args.append(nc.dram_tensor(f"in_{name}", m.shape, _mybir.dt.from_np(m.dtype), kind="ExternalInput").ap())
    args.append(nc.dram_tensor("out_x", (TOK, HID), _mybir.dt.float32, kind="ExternalOutput").ap())
    perceiver_block(nc, *args)
    r = _run(nc, [arrays], core_ids=[0])
    return r.results[0]["out_x"].reshape(1, TOK, HID)
```

```python
from contextlib import ExitStack

import numpy as np

import concourse.bass as bass
from concourse import mybir

ALU = mybir.AluOpType
ACT = mybir.ActivationFunctionType
AX_X = mybir.AxisListType.X
F32 = mybir.dt.float32
F32R = mybir.dt.float32r
I32 = mybir.dt.int32
U16 = mybir.dt.uint16
U8 = mybir.dt.uint8

P = 128
HID = 512
KT = HID // P
TOK = 64
KEYS = 6272
D = 128
NKV = 8
G = 4
NH = NKV * G
ROWS = G * TOK
RT = ROWS // P
CT = 7
CHUNK = CT * P
NCH = KEYS // CHUNK
HALF = CHUNK // 2
SCALE = float(1.0 / np.sqrt(D))
FFN = 1792
FT = FFN // P
RANK = 16
R0, R1, NEXP = 32, 8, 3
RR = R0 + R1
QBLK = 64
NF4 = [-1.0, -0.6961928009986877, -0.5250730514526367, -0.39491748809814453, -0.28444138169288635,
       -0.18477343022823334, -0.09105003625154495, 0.0, 0.07958029955625534, 0.16093020141124725,
       0.24611230194568634, 0.33791524171829224, 0.44070982933044434, 0.5626170039176941,
       0.7229568362236023, 1.0]
TW = 512
ATT_TILES = 4 * KT
GU_COLS = 2 * FFN // TW
GU_TILES = KT * GU_COLS
NT = ATT_TILES + GU_TILES + FT
EXTRA = NT - NCH * NKV
HW = TW // 2
PIECE = CHUNK // 4
PIECES = KT * (CHUNK // PIECE)
PAIR_PIECES = (5, 5, 5, 1)
EPS = 1e-5
LOWEST = -3.0e38


def split_matmuls(nc, out, hi, lo, rhi, rlo, start=True, stop=True):
    nc.tensor.matmul(out, hi, rhi, start=start, stop=False)
    nc.tensor.matmul(out, hi, rlo, start=False, stop=False)
    return nc.tensor.matmul(out, lo, rhi, start=False, stop=stop)


def wait_apart(eng, sem, value, passed):
    eng.wait_ge(sem, value)
    eng.sem_inc(passed, 1)


def perceiver_block(nc, x, ctx_t, wq, bq, wkv, bk, bv, wo, bo, codes, scales, lora_a, lora_a_down, lora_b,
                    lora_b_down, w_base, b_base, enc, coefs, mask, fourier, ident_in, out):
    with ExitStack() as top:
        def sem(name):
            return top.enter_context(nc.semaphore(name))

        def sb(stack, name, shape, dt):
            return stack.enter_context(nc.sbuf_tensor(name, shape, dt))

        def psum(stack, name, shape):
            return stack.enter_context(nc.psum_tensor(name, shape, F32))

        weights = nc.dram_tensor("expanded_weights", [NT - EXTRA, P, TW], F32).ap()
        four_dram = nc.dram_tensor("folded_fourier", [RR, HID], F32).ap()

        ident = sb(top, "ident", [P, P], F32)
        acc = sb(top, "acc", [P, NKV, RT, D], F32)
        denom = sb(top, "denom", [P, NKV, RT], F32)
        maxes = sb(top, "maxes", [P, NKV, RT, 3], F32)
        bv_sb = sb(top, "bv_sb", [P, NKV], F32)

        phase1 = ExitStack()
        wkv_hi = sb(phase1, "wkv_hi", [P, KT, 2 * NKV * D], F32R)
        wkv_lo = sb(phase1, "wkv_lo", [P, KT, 2 * NKV * D], F32R)
        q_hi = sb(phase1, "q_hi", [P, NKV, ROWS], F32R)
        q_lo = sb(phase1, "q_lo", [P, NKV, ROWS], F32R)
        bk_sb = sb(phase1, "bk_sb", [P, NKV], F32)

        even_hi = sb(phase1, "ctx_even_hi", [P, KT, CHUNK], F32R)
        even_lo = sb(phase1, "ctx_even_lo", [P, KT, CHUNK], F32R)

        prologue(nc, ctx_t, x, wq, bq, wkv, bk, bv, coefs, mask, fourier, ident_in, ident, acc, denom, maxes,
                 bv_sb, bk_sb, four_dram, wkv_hi, wkv_lo, q_hi, q_lo, even_hi, even_lo, sem, sb, psum)
        attention(nc, ctx_t, codes, scales, weights, ident, acc, denom, maxes, bk_sb,
                  wkv_hi, wkv_lo, q_hi, q_lo, even_hi, even_lo, sem, sb, psum)
        phase1.close()
        tail(nc, codes, scales, wo, bo, weights, lora_a, lora_a_down, lora_b, lora_b_down, w_base, b_base, enc, out,
             ident, x, acc, denom, bv_sb, four_dram, sem, sb, psum)


def prologue(nc, ctx_t, x, wq, bq, wkv, bk, bv, coefs, mask, fourier, ident_in, ident, acc, denom, maxes, bv_sb,
             bk_sb, four_dram, wkv_hi, wkv_lo, q_hi, q_lo, ctx_hi, ctx_lo, sem, sb, psum):
    STAGES = 3
    WQ_SLOTS = 4
    NG = NH // 8
    CTX_LOADS = KT // 2
    with ExitStack() as st:
        x_sb = sb(st, "x_in_sb", [TOK, HID], F32)
        w_four = sb(st, "w_four_out", [RR, HID], F32)
        xhat = sb(st, "xhat0", [TOK, HID], F32)
        stats = sb(st, "stats0", [TOK, 6], F32)
        mv = sb(st, "mv0", [TOK, 4], F32)
        xt = sb(st, "xt0", [P, KT, TOK], F32)
        bq_sb = sb(st, "bq_sb", [P, NH], F32)
        wq_sb = sb(st, "wq_sb", [P, WQ_SLOTS, KT, TW], F32)
        stage = sb(st, "stage", [P, STAGES, 2 * NKV * D], F32)
        q_f = sb(st, "q_f", [P, 2, 8 * TOK], F32)
        co = sb(st, "co", [P, KT, NEXP, RR], F32)
        mk = sb(st, "mk", [P, KT, NEXP, RR], U8)
        cm = sb(st, "cm", [P, KT, NEXP, RR], F32)
        ws = sb(st, "ws", [P, KT, RR], F32)
        four = sb(st, "four", [P, KT, HID], F32)
        p_x = psum(st, "p_x", [P, KT, TOK])
        p_q = psum(st, "p_q", [P, 2, 8 * TOK])
        p_w = psum(st, "p_w", [RR, HID])

        x_in, vecs_in = sem("x_in"), sem("vecs_in")
        wq_in = [sem(f"wq_in{i}") for i in range(WQ_SLOTS)]
        stage_in = [sem(f"stage_in{i}") for i in range(STAGES)]
        coef_in, four_in = sem("coef_in"), sem("four_in")
        ln_step, var_ready, std_ready, xhat_ready = sem("ln_step0"), sem("var_ready0"), sem("std_ready0"), sem("xhat_ready0")
        xt_psum, xt_ready = sem("xt_psum0"), sem("xt_ready0")
        q_psum, q_biased, q_rounded = sem("q_psum"), sem("q_biased"), sem("q_rounded")
        stage_rounded, stage_split = sem("stage_rounded"), sem("stage_split")
        masked, summed, folded, folded_out, four_stored = sem("masked"), sem("summed"), sem("folded"), sem("folded_out"), sem("four_stored")

        def staged(n):
            slot = n % STAGES
            if n < KT:
                return wkv[:, n], stage[:, slot], wkv_hi[:, n], wkv_lo[:, n]
            k = 2 * (n - KT)
            place = stage[:, slot, 0:2 * CHUNK].rearrange("p (k c) -> p k c", k=2)
            return ctx_t[0, k:k + 2].rearrange("k p c -> p k c"), place, ctx_hi[:, k:k + 2], ctx_lo[:, k:k + 2]

        LOADS = KT + CTX_LOADS
        block = st.enter_context(nc.Block())

        @block.sync
        def _(sp):
            sp.dma_start(x_sb[:], x).then_inc(x_in, 16)
            sp.dma_start(ident[:], ident_in).then_inc(x_in, 16)
            for g in range(NG * 2):
                if g == 1:
                    for dst, src in ((bq_sb, bq), (bk_sb, bk), (bv_sb, bv)):
                        sp.dma_start(dst[:], src).then_inc(vecs_in, 16)
                if g >= WQ_SLOTS:
                    sp.wait_ge(q_psum, g - WQ_SLOTS + 1)
                sp.dma_start(wq_sb[:, g % WQ_SLOTS], wq[:, :, g * TW:(g + 1) * TW]).then_inc(
                    wq_in[g % WQ_SLOTS], 16)
            sp.wait_ge(folded_out, 1)
            sp.dma_start(four_dram, w_four[:]).then_inc(four_stored, 16)
            sp.wait_ge(four_stored, 16)

        @block.scalar
        def _(act):
            def load(n):
                src, place, _, _ = staged(n)
                act.dma_start(place, src).then_inc(stage_in[n % STAGES], 16)

            act.wait_ge(var_ready, 1)
            nc.scalar.activation(mv[:, 3:4], mv[:, 2:3], ACT.Sqrt).then_inc(std_ready, 1)
            for n in range(STAGES):
                load(n)
            for n in range(LOADS):
                _, place, hi, _ = staged(n)
                act.wait_ge(stage_in[n % STAGES], 16 * (n // STAGES + 1))
                nc.scalar.activation(hi, place, ACT.Copy).then_inc(stage_rounded, 1)
                if n >= 1 and n - 1 + STAGES < LOADS:
                    act.wait_ge(stage_split, n)
                    load(n - 1 + STAGES)

        @block.gpsimd
        def _(pool):
            pool.dma_start(co[:], coefs).then_inc(coef_in, 16)
            pool.dma_start(mk[:], mask).then_inc(coef_in, 16)
            pool.dma_start(four[:], fourier).then_inc(four_in, 16)
            pool.wait_ge(coef_in, 32)
            nc.gpsimd.tensor_copy(cm[:], mk[:]).then_inc(masked, 1)
            pool.wait_ge(masked, 1)
            nc.gpsimd.tensor_tensor(cm[:], cm[:], co[:], ALU.mult).then_inc(masked, 1)
            pool.wait_ge(masked, 2)
            nc.gpsimd.tensor_tensor(ws[:], cm[:, :, 0, :], cm[:, :, 1, :], ALU.add).then_inc(masked, 1)
            pool.wait_ge(masked, 3)
            nc.gpsimd.tensor_tensor(ws[:], ws[:], cm[:, :, 2, :], ALU.add).then_inc(summed, 1)
            nc.gpsimd.memset(acc[:], 0.0)
            nc.gpsimd.memset(denom[:], 0.0)
            nc.gpsimd.memset(maxes[:], LOWEST)

        @block.vector
        def _(dve):
            dve.wait_ge(x_in, 32)
            nc.vector.bn_stats(stats[:], x_sb[:]).then_inc(ln_step, 1)
            dve.wait_ge(ln_step, 1)
            nc.vector.bn_aggr(mv[:, 0:2], stats[:]).then_inc(ln_step, 1)
            dve.wait_ge(ln_step, 2)
            nc.vector.tensor_scalar(mv[:, 2:3], mv[:, 1:2], EPS, None, ALU.add).then_inc(var_ready, 1)
            dve.wait_ge(std_ready, 1)
            nc.vector.reciprocal(mv[:, 2:3], mv[:, 3:4]).then_inc(ln_step, 1)
            dve.wait_ge(ln_step, 3)
            nc.vector.tensor_scalar(xhat[:], x_sb[:], mv[:, 0:1], mv[:, 2:3], ALU.subtract,
                                    ALU.mult).then_inc(xhat_ready, 1)
            dve.wait_ge(xt_psum, 1)
            nc.vector.tensor_copy(xt[:], p_x[:]).then_inc(xt_ready, 1)
            dve.wait_ge(vecs_in, 48)

            def split_stage(n):
                _, place, hi, lo = staged(n)
                dve.wait_ge(stage_rounded, n + 1)
                nc.vector.tensor_tensor(lo, place, hi.bitcast(F32), ALU.subtract).then_inc(stage_split, 1)

            def finish_queries(g):
                dve.wait_ge(q_psum, 2 * g + 2)
                heads = q_f[:, g % 2].rearrange("p (h t) -> p h t", h=8)
                nc.vector.tensor_tensor(heads, p_q[:, g % 2].rearrange("p (h t) -> p h t", h=8),
                                        bq_sb[:, 8 * g:8 * g + 8].unsqueeze(2).broadcast_to([P, 8, TOK]),
                                        ALU.add).then_inc(q_biased, 1)
                dve.wait_ge(q_biased, g + 1)
                two = slice(2 * g, 2 * g + 2)
                q3 = q_f[:, g % 2].rearrange("p (h r) -> p h r", h=2)
                nc.vector.tensor_copy(q_hi[:, two], q3).then_inc(q_rounded, 1)
                dve.wait_ge(q_rounded, g + 1)
                nc.vector.tensor_tensor(q_lo[:, two], q3, q_hi[:, two].bitcast(F32), ALU.subtract)

            for n in range(LOADS):
                split_stage(n)
                if n == 2:
                    finish_queries(0)
                    dve.wait_ge(folded, 1)
                    nc.vector.tensor_scalar(w_four[:], p_w[:], 0.5, None, ALU.mult).then_inc(folded_out, 1)
                elif n > 2:
                    finish_queries(n - 2)

        @block.tensor
        def _(pe):
            pe.wait_ge(xhat_ready, 1)
            for k in range(KT):
                t = nc.tensor.transpose(p_x[:, k, :], xhat[:, k * P:(k + 1) * P], ident[0:TOK, 0:TOK])
            t.then_inc(xt_psum, 1)
            pe.wait_ge(xt_ready, 1)
            pe.wait_ge(summed, 1)
            pe.wait_ge(four_in, 16)
            pe.wait_ge(wq_in[3], 16)
            for k in range(KT):
                m = nc.tensor.matmul(p_w[:], ws[:, k, :], four[:, k, :], start=(k == 0), stop=(k == KT - 1))
            m.then_inc(folded, 1)
            for g in range(2 * NG):
                pe.wait_ge(wq_in[g % WQ_SLOTS], 16 * (g // WQ_SLOTS + 1))
                if g >= 4 and g % 2 == 0:
                    pe.wait_ge(q_biased, g // 2 - 1)
                for h in range(4):
                    col = (g % 2) * 4 * TOK + h * TOK
                    for k in range(KT):
                        m = nc.tensor.matmul(p_q[:, (g // 2) % 2, col:col + TOK],
                                             wq_sb[:, g % WQ_SLOTS, k, h * D:(h + 1) * D], xt[:, k, :],
                                             start=(k == 0), stop=(k == KT - 1))
                m.then_inc(q_psum, 1)


def attention(nc, ctx_t, codes, scales, weights, ident, acc, denom, maxes, bk_sb,
              wkv_hi, wkv_lo, q_hi, q_lo, even_hi, even_lo, sem, sb, psum):
    with ExitStack() as st:
        ctx_st = sb(st, "ctx_st", [P, PIECE], F32)
        ctx_hi = [even_hi, sb(st, "ctx_odd_hi", [P, KT, CHUNK], F32R)]
        ctx_lo = [even_lo, sb(st, "ctx_odd_lo", [P, KT, CHUNK], F32R)]
        v_hi = sb(st, "v_hi", [P, CT, 2 * D], F32R)
        v_lo = sb(st, "v_lo", [P, CT, 2 * D], F32R)
        k_hi = sb(st, "k_hi", [P, CHUNK], F32R)
        k_lo = sb(st, "k_lo", [P, CHUNK], F32R)
        probs = sb(st, "probs", [P, RT, CHUNK], F32)
        pt_hi = sb(st, "pt_hi", [P, CT, ROWS], F32R)
        pt_lo = sb(st, "pt_lo", [P, CT, ROWS], F32R)
        o_t = sb(st, "o_t", [P, ROWS], F32)
        newmax = sb(st, "newmax", [P, RT], F32)
        negmax = sb(st, "negmax", [P, RT], F32)
        drop = sb(st, "drop", [P, RT], F32)
        alpha = sb(st, "alpha", [P, 4, RT], F32)
        rowsum = sb(st, "rowsum", [P, 4, RT], F32)
        scale = sb(st, "scale", [P, TW], F32)
        code = sb(st, "code", [P, TW], I32)
        bit0 = sb(st, "bit0", [P, TW], U16)
        bit1 = sb(st, "bit1", [P, TW], U16)
        bit2 = sb(st, "bit2", [P, TW], U16)
        bit3 = sb(st, "bit3", [P, TW], U16)
        code16 = sb(st, "code16", [P, TW], U16)
        leaf = sb(st, "leaf", [P, 2, 5, HW], F32)

        p_kv = psum(st, "p_kv", [P, 2, 512])
        p_s = psum(st, "p_s", [P, 2, 512])
        p_t = psum(st, "p_t", [P, 2, 512])
        p_o = psum(st, "p_o", [P, 512])
        p_ot = psum(st, "p_ot", [P, 512])

        ctx_in, ctx_rounded, ctx_split = sem("ctx_in"), sem("ctx_rounded"), sem("ctx_split")
        kv_psum, kv_rounded, kv_split = sem("kv_psum"), sem("kv_rounded"), sem("kv_split")
        scores_psum, scores_out = sem("scores_psum"), sem("scores_out")
        stat_step, max_ready = sem("stat_step"), sem("max_ready")
        alpha_ready, exp_ready = sem("alpha_ready"), sem("exp_ready")
        pt_psum, pt_rounded, pt_split = sem("pt_psum"), sem("pt_rounded"), sem("pt_split")
        o_psum, o_out, ot_psum, ot_added = sem("o_psum"), sem("o_out"), sem("ot_psum"), sem("ot_added")
        code_in, scale_in = sem("code_in"), sem("scale_in")
        code_narrow, bit0_ready, bits_ready = sem("code_narrow"), sem("bit0_ready"), sem("bits_ready")
        leaves_ready, chosen, choice = sem("leaves_ready"), sem("chosen"), sem("choice")
        scaled = sem("scaled")
        weight_out = [sem(f"weight_out{b}") for b in range(2)]
        pool_passed, dve_passed = sem("pool_passed"), sem("dve_passed")

        NB = NCH * NKV
        KV_USES = CT + 4

        def v_use(s, h, t):
            return 2 + KV_USES * (4 * s + h // 2) + t

        def k_use(s, h, c):
            return 2 + KV_USES * (4 * s + h // 2) + CT + 2 * (h % 2) + c

        def v_bank(h, t):
            return (h // 2 + t) % 2

        def k_bank(h, c):
            return (h // 2 + 1 + c) % 2

        block = st.enter_context(nc.Block())

        @block.sync
        def _(sp):
            def load_ctx(s, piece, first=False):
                if not first:
                    sp.wait_ge(ctx_split, PIECES * (s - 1) + piece)
                k, q = piece // 4, piece % 4
                sp.dma_start(ctx_st[:], ctx_t[s, k, :, q * PIECE:(q + 1) * PIECE]).then_inc(ctx_in, 16)

            def codes_of(n, first=False):
                if not first:
                    sp.wait_ge(code_narrow, n)
                sp.dma_start(code[:], codes[n]).then_inc(code_in, 16)

            def scales_of(n, first=False):
                if not first:
                    sp.wait_ge(scaled, 2 * n)
                for b in range(2):
                    sp.dma_start(scale[b * QBLK:(b + 1) * QBLK, :],
                                 scales[n, b].partition_broadcast(QBLK)).then_inc(scale_in, 16)

            def tile_out(n):
                for b in range(2):
                    sp.wait_ge(scaled, 2 * n + b + 1)
                    sp.dma_start(weights[n, :, b * HW:(b + 1) * HW], leaf[:, b, 4, :]).then_inc(weight_out[b], 16)

            codes_of(0, True)
            scales_of(0, True)
            codes_of(1)

            def chunk(s, last):
                piece = 0
                for pair in range(NKV // 2):
                    n = NKV * s + 2 * pair
                    start = isinstance(n, int) and n == 0

                    def load(q):
                        if not last and q < PAIR_PIECES[pair]:
                            load_ctx(s + 1, piece + q, start and q == 0)

                    load(0)
                    if not start:
                        tile_out(n - 1)
                        scales_of(n)
                    load(1)
                    if not (last and pair == NKV // 2 - 1):
                        codes_of(n + 2)
                    load(2)
                    tile_out(n)
                    scales_of(n + 1)
                    load(3)
                    load(4)
                    if not (last and pair == NKV // 2 - 1):
                        codes_of(n + 3)
                    piece += PAIR_PIECES[pair]

            chunk(0, False)
            with sp.Fori(1, NCH - 1) as s:
                chunk(s, False)
            chunk(NCH - 1, True)
            tile_out(NB - 1)
            for b in range(2):
                sp.wait_ge(weight_out[b], 16 * NB)

        @block.gpsimd
        def _(pool):
            def split_ctx(s, piece, half):
                n, k = PIECES * (s - 1) + piece, piece // 4
                keys = slice(piece % 4 * PIECE, (piece % 4 + 1) * PIECE)
                wait_apart(pool, ctx_rounded, n + 1, pool_passed)
                nc.gpsimd.tensor_tensor(ctx_lo[half][:, k, keys], ctx_st[:], ctx_hi[half][:, k, keys].bitcast(F32),
                                        ALU.subtract).then_inc(ctx_split, 1)

            def narrow(n, first=False):
                wait_apart(pool, code_in, 16 * (n + 1), pool_passed)
                if not first:
                    wait_apart(pool, bits_ready, n, pool_passed)
                nc.gpsimd.tensor_copy(code16[:], code[:]).then_inc(code_narrow, 1)

            def leaves(b, first_leaf, slots):
                for k, slot in enumerate(slots):
                    j = first_leaf + k
                    m = nc.gpsimd.tensor_scalar(leaf[:, b, slot, :], bit0[:, b * HW:(b + 1) * HW],
                                                NF4[2 * j + 1] - NF4[2 * j], NF4[2 * j], ALU.mult, ALU.add)
                m.then_inc(leaves_ready, 1)

            def low_leaves(n):
                wait_apart(pool, bit0_ready, n + 1, pool_passed)
                if not (isinstance(n, int) and n == 0):
                    wait_apart(pool, scaled, 2 * n, pool_passed)
                for b in range(2):
                    leaves(b, 0, (0, 1, 2, 3))

            def high_leaves(n):
                for b in range(2):
                    wait_apart(pool, chosen, 4 * n + 1 + b, pool_passed)
                    if not (isinstance(n, int) and n == 0):
                        wait_apart(pool, weight_out[b], 16 * n, pool_passed)
                    leaves(b, 4, (1, 2, 3, 4))

            def apply_scales(n):
                wait_apart(pool, scale_in, 32 * (n + 1), pool_passed)
                for b in range(2):
                    wait_apart(pool, chosen, 4 * n + 3 + b, pool_passed)
                    nc.gpsimd.tensor_tensor(leaf[:, b, 4, :], leaf[:, b, 0, :], scale[:, b * HW:(b + 1) * HW],
                                            ALU.mult).then_inc(scaled, 1)

            narrow(0, True)

            def chunk(s, par, last):
                piece = 0
                for pair in range(NKV // 2):
                    n = NKV * s + 2 * pair

                    def split(q):
                        if not last and q < PAIR_PIECES[pair]:
                            split_ctx(s + 1, piece + q, 1 - par)

                    if not (isinstance(n, int) and n == 0):
                        apply_scales(n - 1)
                    low_leaves(n)
                    split(0)
                    high_leaves(n)
                    narrow(n + 1)
                    split(1)
                    apply_scales(n)
                    split(2)
                    low_leaves(n + 1)
                    split(3)
                    high_leaves(n + 1)
                    if not (last and pair == NKV // 2 - 1):
                        narrow(n + 2)
                    split(4)
                    piece += PAIR_PIECES[pair]

            chunk(0, 0, False)
            with pool.Fori(0, NCH // 2 - 1) as s2:
                chunk(2 * s2 + 1, 1, False)
                chunk(2 * s2 + 2, 0, False)
            chunk(NCH - 2, 1, False)
            chunk(NCH - 1, 0, True)
            apply_scales(NB - 1)

        @block.tensor
        def _(pe):
            def project_keys(bank, half, h, c, k):
                cols = slice(h * D, (h + 1) * D)
                keys = slice(c * HALF, (c + 1) * HALF)
                m = split_matmuls(nc, p_kv[:, bank, 0:HALF], wkv_hi[:, k, cols], wkv_lo[:, k, cols],
                                  ctx_hi[half][:, k, keys], ctx_lo[half][:, k, keys],
                                  start=(k == 0), stop=(k == KT - 1))
                if k == KT - 1:
                    m.then_inc(kv_psum, 1)

            def static_first(i):
                return isinstance(i, int) and i == 0

            def turn_output(i):
                pe.wait_ge(o_out, i + 1)
                if not static_first(i):
                    pe.wait_ge(ot_added, i)
                for r in range(RT):
                    m = nc.tensor.transpose(p_ot[:, r * D:(r + 1) * D], o_t[:, r * P:(r + 1) * P], ident[:])
                m.then_inc(ot_psum, 1)

            def turn_probs(i, c, skip):
                if c == 0:
                    pe.wait_ge(exp_ready, 2 * i + 2)
                if not skip:
                    pe.wait_ge(pt_split, 4 * i + c - 1)
                for t in range(2 * c, min(2 * c + 2, CT)):
                    for r in range(RT):
                        col = (t % 2) * ROWS + r * P
                        m = nc.tensor.transpose(p_t[:, c % 2, col:col + P], probs[:, r, t * P:(t + 1) * P], ident[:])
                m.then_inc(pt_psum, 1)

            def scores(i, h, kuse, static):
                for c in range(2):
                    pe.wait_ge(kv_split, kuse + c + 1)
                    for r in range(RT):
                        bank = p_s[:, r, 0:HALF] if c == 0 else p_kv[:, k_bank((h - 1) % NKV, r), 0:HALF]
                        if c == 0 and not static:
                            pe.wait_ge(scores_out, 4 * i - 3 + r)
                        m = split_matmuls(nc, bank, q_hi[:, h, r * P:(r + 1) * P],
                                          q_lo[:, h, r * P:(r + 1) * P], k_hi[:, c * HALF:(c + 1) * HALF],
                                          k_lo[:, c * HALF:(c + 1) * HALF])
                        m.then_inc(scores_psum, 1)

            def values(s, h, half):
                for t in range(CT):
                    if t < 2:
                        pe.wait_ge(scores_out, 4 * (NKV * s + h) + 4)
                    pe.wait_ge(kv_split, v_use(s, h, t) - 1)
                    cols = slice((NKV + h) * D, (NKV + h + 2) * D)
                    for k in range(KT):
                        keys = slice(t * P, (t + 1) * P)
                        m = split_matmuls(nc, p_kv[:, v_bank(h, t), 0:2 * D], ctx_hi[half][:, k, keys],
                                          ctx_lo[half][:, k, keys], wkv_hi[:, k, cols], wkv_lo[:, k, cols],
                                          start=(k == 0), stop=(k == KT - 1))
                    m.then_inc(kv_psum, 1)

            def prev_values(s, h):
                i = NKV * s + h - 1
                hp = (h - 1) % NKV
                pair = 4 * s + h // 2 - (1 if h % 2 == 0 else 0)
                pe.wait_ge(pt_split, 4 * i + 4)
                pe.wait_ge(kv_split, 2 + KV_USES * pair + CT)
                if not static_first(i):
                    pe.wait_ge(o_out, i)
                d = slice((hp % 2) * D, (hp % 2 + 1) * D)
                for t in range(CT):
                    m = split_matmuls(nc, p_o[:, 0:ROWS], v_hi[:, t, d], v_lo[:, t, d], pt_hi[:, t], pt_lo[:, t],
                                      start=(t == 0), stop=(t == CT - 1))
                m.then_inc(o_psum, 1)

            def block_work(s, h, half, first, last):
                i = NKV * s + h
                first = first and h == 0
                last = last and h == NKV - 1
                kuse = 0 if first else k_use(s, h, 0) - 2 - (CT if h % 2 == 0 else 0)
                scores(i, h, kuse, first)
                if not first:
                    prev_values(s, h)
                if h % 2 == 0:
                    values(s, h, half)
                nh, nhalf = ((h + 1), half) if h + 1 < NKV else (0, 1 - half)
                if not last:
                    if nh == 0:
                        pe.wait_ge(ctx_split, PIECES * (s + 1))
                    pe.wait_ge(kv_split, k_use(s, h, 0) - 1)
                    pe.wait_ge(scores_out, 4 * i + 4)
                    for k in range(KT):
                        project_keys(k_bank(h, 0), nhalf, nh, 0, k)
                    turn_probs(i, 0, first)
                    if not first:
                        turn_output(i - 1)
                    pe.wait_ge(kv_split, k_use(s, h, 1) - 1)
                    project_keys(k_bank(h, 1), nhalf, nh, 1, 0)
                    turn_probs(i, 1, first)
                    for k in range(1, KT):
                        project_keys(k_bank(h, 1), nhalf, nh, 1, k)
                    turn_probs(i, 2, False)
                    turn_probs(i, 3, False)
                else:
                    turn_output(i - 1)
                    for c in range(4):
                        turn_probs(i, c, False)

            for c in range(2):
                for k in range(KT):
                    project_keys(k_bank(NKV - 1, c), 0, 0, c, k)
            for h in range(NKV):
                block_work(0, h, 0, True, False)
            with pe.Fori(0, NCH // 2 - 1) as s2:
                for h in range(NKV):
                    block_work(2 * s2 + 1, h, 1, False, False)
                for h in range(NKV):
                    block_work(2 * s2 + 2, h, 0, False, False)
            for h in range(NKV):
                block_work(NCH - 2, h, 1, False, False)
            for h in range(NKV):
                block_work(NCH - 1, h, 0, False, True)
            prev_values(NCH, 0)
            turn_output(NB - 1)

        @block.scalar
        def _(act):
            def round_kv(use, dst, src, bias=None):
                act.wait_ge(kv_psum, use + 1)
                nc.scalar.activation(dst, src, ACT.Identity, bias=0.0 if bias is None else bias).then_inc(kv_rounded, 1)

            def round_keys(use, bank, nh, c):
                round_kv(use, k_hi[:, c * HALF:(c + 1) * HALF], p_kv[:, bank, 0:HALF], bk_sb[:, nh:nh + 1])

            def round_values(s, h, t):
                round_kv(v_use(s, h, t), v_hi[:, t], p_kv[:, v_bank(h, t), 0:2 * D])

            def round_probs(i, c):
                act.wait_ge(pt_psum, 4 * i + c + 1)
                n = min(2, CT - 2 * c)
                nc.scalar.activation(pt_hi[:, 2 * c:2 * c + n, :].rearrange("p t q -> p (t q)"),
                                     p_t[:, c % 2, 0:n * ROWS], ACT.Copy).then_inc(pt_rounded, 1)

            def output_out(i):
                act.wait_ge(o_psum, i + 1)
                nc.scalar.activation(o_t[:], p_o[:, 0:ROWS], ACT.Copy).then_inc(o_out, 1)

            def round_ctx(s, h, par, q, last):
                if last or q >= PAIR_PIECES[h // 2]:
                    return
                piece = sum(PAIR_PIECES[:h // 2]) + q
                act.wait_ge(ctx_in, 16 * (PIECES * s + piece + 1))
                keys = slice(piece % 4 * PIECE, (piece % 4 + 1) * PIECE)
                nc.scalar.activation(ctx_hi[1 - par][:, piece // 4, keys], ctx_st[:], ACT.Copy).then_inc(ctx_rounded, 1)

            def block_work(s, h, half, first, last):
                i = NKV * s + h
                par = h % 4
                act.wait_ge(max_ready, i + 1)
                nc.scalar.activation(alpha[:, par, :], drop[:], ACT.Exp).then_inc(alpha_ready, 1)
                for r in range(RT):
                    nc.scalar.activation(probs[:, r, :], probs[:, r, :], ACT.Exp, bias=negmax[:, r:r + 1],
                                         accum_out=rowsum[:, par, r:r + 1]).then_inc(exp_ready, 1)
                    if r == 0 and h % 2 == 0:
                        round_values(s, h, 0)
                if not (first and h == 0):
                    output_out(i - 1)
                if h % 2 == 0:
                    for t in range(1, CT):
                        round_values(s, h, t)
                        if t == 1:
                            round_ctx(s, h, half, 0, last)
                else:
                    round_ctx(s, h, half, 3, last)
                if last and h == NKV - 1:
                    for c in range(4):
                        round_probs(i, c)
                    return
                nh = (h + 1) % NKV
                round_keys(k_use(s, h, 0), k_bank(h, 0), nh, 0)
                for c in range(2):
                    round_probs(i, c)
                if h % 2 == 0:
                    round_ctx(s, h, half, 1, last)
                round_keys(k_use(s, h, 1), k_bank(h, 1), nh, 1)
                for c in range(2, 4):
                    round_probs(i, c)
                round_ctx(s, h, half, 2 if h % 2 == 0 else 4, last)

            for c in range(2):
                round_keys(c, k_bank(NKV - 1, c), 0, c)
            for h in range(NKV):
                block_work(0, h, 0, True, False)
            with act.Fori(0, NCH // 2 - 1) as s2:
                for h in range(NKV):
                    block_work(2 * s2 + 1, h, 1, False, False)
                for h in range(NKV):
                    block_work(2 * s2 + 2, h, 0, False, False)
            for h in range(NKV):
                block_work(NCH - 2, h, 1, False, False)
            for h in range(NKV):
                block_work(NCH - 1, h, 0, False, True)
            output_out(NB - 1)

        @block.vector
        def _(dve):
            def split_kv(use, dst, src, hi, bias=None):
                dve.wait_ge(kv_rounded, use + 1)
                if bias is None:
                    nc.vector.tensor_tensor(dst, src, hi.bitcast(F32), ALU.subtract).then_inc(kv_split, 1)
                else:
                    nc.vector.scalar_tensor_tensor(dst, src, bias, hi.bitcast(F32), ALU.add,
                                                   ALU.subtract).then_inc(kv_split, 1)

            def split_keys(use, bank, nh, c):
                keys = slice(c * HALF, (c + 1) * HALF)
                split_kv(use, k_lo[:, keys], p_kv[:, bank, 0:HALF], k_hi[:, keys], bk_sb[:, nh:nh + 1])

            def split_probs(i, c):
                dve.wait_ge(pt_rounded, 4 * i + c + 1)
                n = min(2, CT - 2 * c)
                nc.vector.tensor_tensor(pt_lo[:, 2 * c:2 * c + n, :].rearrange("p t q -> p (t q)"),
                                        p_t[:, c % 2, 0:n * ROWS],
                                        pt_hi[:, 2 * c:2 * c + n, :].rearrange("p t q -> p (t q)").bitcast(F32),
                                        ALU.subtract).then_inc(pt_split, 1)

            def add_output(i, h):
                dve.wait_ge(alpha_ready, i + 1)
                dve.wait_ge(ot_psum, i + 1)
                par = h % 4
                for r in range(RT):
                    nc.vector.scalar_tensor_tensor(denom[:, h, r:r + 1], denom[:, h, r:r + 1], alpha[:, par, r:r + 1],
                                                   rowsum[:, par, r:r + 1], ALU.mult, ALU.add)
                for r in range(RT):
                    m = nc.vector.scalar_tensor_tensor(acc[:, h, r, :], acc[:, h, r, :], alpha[:, par, r:r + 1],
                                                       p_ot[:, r * D:(r + 1) * D], ALU.mult, ALU.add)
                m.then_inc(ot_added, 1)

            def score_stats(i, h):
                for c in range(2):
                    for r in range(RT):
                        bank = p_s[:, r, 0:HALF] if c == 0 else p_kv[:, k_bank((h - 1) % NKV, r), 0:HALF]
                        dve.wait_ge(scores_psum, 4 * i + 2 * c + r + 1)
                        nc.vector.tensor_scalar(probs[:, r, c * HALF:(c + 1) * HALF], bank, SCALE, None,
                                                ALU.mult, ALU.max,
                                                accum_out=maxes[:, h, r, 1 + c:2 + c]).then_inc(scores_out, 1)
                dve.wait_ge(scores_out, 4 * i + 4)
                nc.vector.tensor_reduce(newmax[:], maxes[:, h], AX_X, ALU.max).then_inc(stat_step, 1)
                dve.wait_ge(stat_step, 2 * i + 1)
                nc.vector.tensor_scalar(negmax[:], newmax[:], -1.0, None, ALU.mult)
                nc.vector.tensor_tensor(drop[:], maxes[:, h, :, 0], newmax[:], ALU.subtract).then_inc(max_ready, 1)
                dve.wait_ge(max_ready, i + 1)
                nc.vector.tensor_copy(maxes[:, h, :, 0], newmax[:]).then_inc(stat_step, 1)

            def take_bit0(n):
                dve.wait_ge(code_narrow, n + 1)
                if not (isinstance(n, int) and n == 0):
                    dve.wait_ge(leaves_ready, 4 * n)
                nc.vector.tensor_scalar(bit0[:], code16[:], 1, None, ALU.bitwise_and).then_inc(bit0_ready, 1)

            def take_other_bits(n):
                dve.wait_ge(code_narrow, n + 1)
                if not (isinstance(n, int) and n == 0):
                    dve.wait_ge(chosen, 4 * n)
                for bit, dst in ((1, bit1), (2, bit2), (3, bit3)):
                    m = nc.vector.tensor_scalar(dst[:], code16[:], 1 << bit, None, ALU.bitwise_and)
                m.then_inc(bits_ready, 1)

            def take(b, bit, slot, other):
                return nc.vector.copy_predicated(leaf[:, b, slot, :], bit[:, b * HW:(b + 1) * HW], leaf[:, b, other, :])

            def low_by_bit1(n, b):
                wait_apart(dve, bits_ready, n + 1, dve_passed)
                wait_apart(dve, leaves_ready, 4 * n + 1 + b, dve_passed)
                take(b, bit1, 0, 1)
                take(b, bit1, 2, 3).then_inc(choice, 1)

            def low_by_bit2(n, b):
                wait_apart(dve, choice, 6 * n + 1 + b, dve_passed)
                take(b, bit2, 0, 2).then_inc(chosen, 1)

            def high_by_bit1(n, b):
                wait_apart(dve, leaves_ready, 4 * n + 3 + b, dve_passed)
                take(b, bit1, 1, 2)
                take(b, bit1, 3, 4).then_inc(choice, 1)

            def high_by_bit2(n, b):
                wait_apart(dve, choice, 6 * n + 3 + 2 * b, dve_passed)
                take(b, bit2, 1, 3).then_inc(choice, 1)

            def all_by_bit3(n, b):
                wait_apart(dve, choice, 6 * n + 4 + 2 * b, dve_passed)
                take(b, bit3, 0, 1).then_inc(chosen, 1)

            def block_work(s, h, first, last):
                i = NKV * s + h
                score_stats(i, h)
                if not (first and h < 2):
                    add_output(i - 2, (h - 2) % NKV)
                if h % 2 == 0:
                    if not (first and h == 0):
                        high_by_bit2(i - 1, 0)
                        high_by_bit1(i - 1, 1)
                        high_by_bit2(i - 1, 1)
                    for t in range(CT):
                        split_kv(v_use(s, h, t), v_lo[:, t], p_kv[:, v_bank(h, t), 0:2 * D], v_hi[:, t])
                        if t == 0 and not (first and h == 0):
                            for b in range(2):
                                all_by_bit3(i - 1, b)
                        if t == 1:
                            take_bit0(i)
                            take_other_bits(i)
                        if t in (3, 4):
                            low_by_bit1(i, t - 3)
                        if t in (3, 5):
                            low_by_bit2(i, 0 if t == 3 else 1)
                    high_by_bit1(i, 0)
                    high_by_bit2(i, 0)
                    all_by_bit3(i, 0)
                    high_by_bit1(i, 1)
                else:
                    take_other_bits(i)
                    low_by_bit1(i, 0)
                    low_by_bit2(i, 0)
                    low_by_bit1(i, 1)
                if last and h == NKV - 1:
                    split_probs(i, 0)
                    split_probs(i, 1)
                    low_by_bit2(i, 1)
                    add_output(i - 1, (h - 1) % NKV)
                    split_probs(i, 2)
                    split_probs(i, 3)
                    return
                nh = (h + 1) % NKV
                split_keys(k_use(s, h, 0), k_bank(h, 0), nh, 0)
                if h % 2 == 0:
                    split_probs(i, 0)
                    split_probs(i, 1)
                    high_by_bit2(i, 1)
                    all_by_bit3(i, 1)
                else:
                    low_by_bit2(i, 1)
                    split_probs(i, 0)
                    split_probs(i, 1)
                    high_by_bit1(i, 0)
                split_keys(k_use(s, h, 1), k_bank(h, 1), nh, 1)
                if h % 2 == 0:
                    take_bit0(i + 1)
                split_probs(i, 2)
                split_probs(i, 3)

            for c in range(2):
                split_keys(c, k_bank(NKV - 1, c), 0, c)
            for h in range(NKV):
                block_work(0, h, True, False)
            with dve.Fori(1, NCH - 1) as s:
                for h in range(NKV):
                    block_work(s, h, False, False)
            for h in range(NKV):
                block_work(NCH - 1, h, False, True)
            for b in range(2):
                high_by_bit1(NB - 1, b)
                high_by_bit2(NB - 1, b)
                all_by_bit3(NB - 1, b)
            add_output(NB - 1, NKV - 1)


def tail(nc, codes, scales, wo, bo, weights, lora_a, lora_a_down, lora_b, lora_b_down, w_base, b_base, enc, out,
         ident, x, acc, denom, bv_sb, four_dram, sem, sb, psum):
    PAIRS = (NH + NT - EXTRA) // 2
    WB = 13
    XW = EXTRA * TW
    with ExitStack() as st:
        wring = sb(st, "wring", [P, WB, 2, TW], F32)
        rden = sb(st, "rden", [P, NKV, RT], F32)
        ot = sb(st, "ot", [P, NKV, ROWS], F32)
        x_sb = sb(st, "x_sb", [TOK, HID], F32)
        x_bo = sb(st, "x_bo", [TOK, HID], F32)
        w_four = sb(st, "w_four", [RR, HID], F32)
        bo_sb = sb(st, "bo_sb", [TOK, HID], F32)
        bb_sb = sb(st, "bb_sb", [TOK, HID], F32)
        la = sb(st, "la", [P, KT, 6 * RANK], F32)
        lad = sb(st, "lad", [P, FT, RANK], F32)
        lb_qkv = sb(st, "lb_qkv", [3 * RANK, HID], F32)
        lb_o = sb(st, "lb_o", [RANK, HID], F32)
        lb_gu = sb(st, "lb_gu", [RANK, 2, FFN], F32)
        lb_d = sb(st, "lb_d", [RANK, HID], F32)
        wb = sb(st, "wb", [P, KT, HID], F32)
        en = sb(st, "en", [P, KT, RR], F32)
        qkv_sum = sb(st, "qkv_sum", [P, KT, TW], F32)
        xa = sb(st, "xa", [TOK, HID], F32)
        z = sb(st, "z", [TOK, HID], F32)
        av = sb(st, "av", [TOK, HID], F32)
        y = sb(st, "y", [TOK, HID], F32)
        y_xa = sb(st, "y_xa", [TOK, HID], F32)
        xb = sb(st, "xb", [TOK, HID], F32)
        z2 = sb(st, "z2", [TOK, HID], F32)
        sums = sb(st, "sums", [TOK, HID], F32)
        res = sb(st, "res", [TOK, HID], F32)
        zt = sb(st, "zt", [P, KT, TOK], F32)
        at = sb(st, "at", [P, KT, TOK], F32)
        yt = sb(st, "yt", [P, KT, TOK], F32)
        z2t = sb(st, "z2t", [P, KT, TOK], F32)
        gate = sb(st, "gate", [TOK, 2, 5, 2 * P], F32)
        ht = sb(st, "ht", [P, FT, TOK], F32)
        e_qkv = sb(st, "e_qkv", [3 * RANK, TOK], F32)
        e_small = sb(st, "e_small", [RANK, 4, TOK], F32)
        e_f = sb(st, "e_f", [RR, TOK], F32)
        stats = sb(st, "stats", [TOK, 2, 6], F32)
        mv = sb(st, "mv", [TOK, 2, 4], F32)
        spare = sb(st, "spare", [P, 3], F32)
        x_code = sb(st, "x_code", [P, XW], I32)
        x_code16 = sb(st, "x_code16", [P, XW], U16)
        x_scale = sb(st, "x_scale", [P, XW], F32)
        x_bits = sb(st, "x_bits", [P, 4, XW], U16)
        x_base = sb(st, "x_base", [P, 8], F32)
        x_leaf = sb(st, "x_leaf", [P, 8, XW], F32)

        pb = [psum(st, f"pb{i}", [P, 512]) for i in range(8)]
        WO_BANK, TURN_BANK, RANK_BANK, QKV_BANK, DOWN_BANK = 2, 3, 4, 5, 7
        GU_BANKS = (5, 6)

        w_in = [sem(f"w_in{i}") for i in range(WB)]
        w_used, small_in, late_in, x_in = sem("w_used"), sem("small_in"), sem("late_in"), sem("extra_in")
        smalls = [(bo_sb[:], bo.partition_broadcast(TOK)), (x_sb[:], x), (la[:], lora_a), (lb_qkv[:], lora_b[0:3 * RANK, 0:HID]),
                  (lb_o[:], lora_b[3 * RANK:4 * RANK, 0:HID]), (lb_gu[:, 0, :], lora_b[4 * RANK:5 * RANK, :]),
                  (lb_gu[:, 1, :], lora_b[5 * RANK:6 * RANK, :])]
        late = [(lad[:], lora_a_down), (lb_d[:], lora_b_down),
                  (bb_sb[:], b_base.partition_broadcast(TOK)), (en[:], enc), (w_four[:], four_dram), (wb[:], w_base)]
        SUMMED = range(NH // 2, NH // 2 + 3 * KT // 2)
        names = {}

        def step(name):
            if name not in names:
                names[name] = sem(name)
            return names[name]

        block = st.enter_context(nc.Block())

        @block.sync
        def _(sp):
            for n in range(PAIRS):
                if n >= WB:
                    old = n - WB
                    if old in SUMMED:
                        sp.wait_ge(step("qkv_summed"), max(1, old - SUMMED[0] - KT + 1))
                    else:
                        sp.wait_ge(w_used, old + 1 if old < SUMMED[0] else old + 1 - len(SUMMED))
                src = wo[2 * n:2 * n + 2] if 2 * n < NH else weights[2 * n - NH:2 * n - NH + 2]
                sp.dma_start(wring[:, n % WB], src.rearrange("t p c -> p t c")).then_inc(w_in[n % WB], 16)
            sp.wait_ge(step("final"), 1)
            sp.dma_start(out, res[:]).then_inc(step("stored"), 16)
            sp.wait_ge(step("stored"), 16)

        @block.gpsimd
        def _(pool):
            for e in range(EXTRA):
                tile = slice(e * TW, (e + 1) * TW)
                pool.dma_start(x_code[:, tile], codes[NT - EXTRA + e]).then_inc(x_in, 16)
                for b in range(2):
                    pool.dma_start(x_scale[b * QBLK:(b + 1) * QBLK, tile],
                                   scales[NT - EXTRA + e, b].partition_broadcast(QBLK)).then_inc(x_in, 16)
            for j in range(8):
                m = nc.gpsimd.memset(x_base[:, j:j + 1], NF4[2 * j])
            m.then_inc(step("leaf_bases"), 1)
            pool.wait_ge(x_in, 48 * EXTRA)
            nc.gpsimd.tensor_copy(x_code16[:], x_code[:]).then_inc(step("extra_narrow"), 1)
            pool.wait_ge(small_in, 16 * len(smalls))
            nc.gpsimd.tensor_tensor(x_bo[:], x_sb[:], bo_sb[:], ALU.add).then_inc(step("x_bo"), 1)
            pool.wait_ge(step("extra_chosen"), 1)
            nc.gpsimd.tensor_tensor(x_leaf[:, 1, :], x_leaf[:, 0, :], x_scale[:], ALU.mult).then_inc(
                step("extra_ready"), 1)

        @block.scalar
        def _(act):
            for dst, src in smalls:
                act.dma_start(dst, src).then_inc(small_in, 16)
            act.wait_ge(step("leaf_bases"), 1)
            act.wait_ge(step("extra_bits"), 1)
            for j in range(8):
                nc.scalar.activation(x_leaf[:, j, :], x_bits[:, 0, :], ACT.Identity, bias=x_base[:, j:j + 1],
                                     scale=NF4[2 * j + 1] - NF4[2 * j]).then_inc(step("extra_leaves"), 1)

            def load_table(function, place):
                nc.scalar.activation(spare[:, place:place + 1], ident[:, 0:1], function)

            def root(n):
                act.wait_ge(step(f"variance{n}"), 1)
                nc.scalar.activation(mv[:, n, 3:4], mv[:, n, 2:3], ACT.Sqrt).then_inc(step(f"deviation{n}"), 1)

            load_table(ACT.Sqrt, 0)
            root(0)
            load_table(ACT.Exp, 1)
            for dst, src in late:
                act.dma_start(dst, src).then_inc(late_in, 16)
            for c in range(GU_COLS):
                act.wait_ge(step("gu_psum"), c + 1)
                if c >= 2:
                    act.wait_ge(step("one_plus"), c - 1)
                nc.scalar.activation(gate[:, c % 2, 0], pb[GU_BANKS[c % 2]][0:TOK, 0:2 * P], ACT.Exp,
                                     scale=-1.0).then_inc(step("exp_gate"), 1)
            load_table(ACT.Sqrt, 2)
            root(1)

        @block.vector
        def _(dve):
            nc.vector.reciprocal(rden[:], denom[:]).then_inc(step("reciprocals"), 1)
            dve.wait_ge(step("reciprocals"), 1)
            def divide(h):
                for r in range(RT):
                    m = nc.vector.tensor_scalar(acc[:, h, r, :], acc[:, h, r, :], rden[:, h, r:r + 1], None, ALU.mult)
                m.then_inc(step("divided"), 1)

            def attention_t(h):
                dve.wait_ge(step("attn_turned"), h + 1)
                nc.vector.tensor_scalar(ot[:, h, :], pb[h % 2][:, 0:ROWS], bv_sb[:, h:h + 1], None,
                                        ALU.add).then_inc(step("attn_t"), 1)

            divide(0)
            for h in range(NKV):
                if h + 1 < NKV:
                    divide(h + 1)
                attention_t(h)
                if h == NKV // 2:
                    dve.wait_ge(step("extra_narrow"), 1)
                    for bit in range(4):
                        m = nc.vector.tensor_scalar(x_bits[:, bit, :], x_code16[:], 1 << bit, None, ALU.bitwise_and)
                    m.then_inc(step("extra_bits"), 1)

            half = KT // 2

            def sum_q_k(n):
                q, k = NH // 2 + n, NH // 2 + half + n
                for p in (q, k):
                    dve.wait_ge(w_in[p % WB], 16 * (p // WB + 1))
                nc.vector.tensor_tensor(qkv_sum[:, 2 * n:2 * n + 2], wring[:, q % WB], wring[:, k % WB],
                                        ALU.add).then_inc(step("q_k_summed"), 1)

            def sum_v(n):
                p = NH // 2 + 2 * half + n
                dst = qkv_sum[:, 2 * n:2 * n + 2]
                dve.wait_ge(step("q_k_summed"), n + 1)
                dve.wait_ge(w_in[p % WB], 16 * (p // WB + 1))
                nc.vector.tensor_tensor(dst, dst, wring[:, p % WB], ALU.add).then_inc(step("qkv_summed"), 1)

            sum_q_k(0)

            def take(bit, slot, other):
                return nc.vector.copy_predicated(x_leaf[:, slot, :], x_bits[:, bit, :], x_leaf[:, other, :])

            def extra_by_bit1():
                for j in range(0, 8, 2):
                    dve.wait_ge(step("extra_leaves"), j + 2)
                    m = take(1, j, j + 1)
                m.then_inc(step("by_bit1"), 1)

            def extra_by_bit2():
                dve.wait_ge(step("by_bit1"), 1)
                for j in range(0, 8, 4):
                    m = take(2, j, j + 2)
                m.then_inc(step("by_bit2"), 1)

            def extra_by_bit3():
                dve.wait_ge(step("by_bit2"), 1)
                take(3, 0, 4).then_inc(step("extra_chosen"), 1)

            dve.wait_ge(step("x_bo"), 1)
            dve.wait_ge(w_used, NH // 2)
            nc.vector.tensor_tensor(xa[:], pb[WO_BANK][0:TOK, :], x_bo[:], ALU.add).then_inc(step("rows0"), 1)

            def norm(n, rows, dst, meanwhile=None):
                dve.wait_ge(step(f"rows{n}"), 1)
                nc.vector.bn_stats(stats[:, n], rows).then_inc(step(f"moments{n}"), 1)
                dve.wait_ge(step(f"moments{n}"), 1)
                nc.vector.bn_aggr(mv[:, n, 0:2], stats[:, n]).then_inc(step(f"mean{n}"), 1)
                dve.wait_ge(step(f"mean{n}"), 1)
                nc.vector.tensor_scalar(mv[:, n, 2:3], mv[:, n, 1:2], EPS, None, ALU.add).then_inc(step(f"variance{n}"), 1)
                if meanwhile:
                    meanwhile()
                dve.wait_ge(step(f"deviation{n}"), 1)
                nc.vector.reciprocal(mv[:, n, 2:3], mv[:, n, 3:4]).then_inc(step(f"inverse{n}"), 1)
                dve.wait_ge(step(f"inverse{n}"), 1)
                nc.vector.tensor_scalar(dst, rows, mv[:, n, 0:1], mv[:, n, 2:3], ALU.subtract,
                                        ALU.mult).then_inc(step(f"normed{n}"), 1)

            def turned(name, dst, bank):
                dve.wait_ge(step(f"{name}_turned"), 1)
                nc.vector.tensor_copy(dst[:], bank[:, 0:KT * TOK].rearrange("p (k t) -> p k t", k=KT)).then_inc(
                    step(f"{name}_t"), 1)

            norm(0, xa[:], z[:], lambda: sum_q_k(1))
            turned("z", zt, pb[TURN_BANK])
            sum_v(0)
            sum_v(1)
            dve.wait_ge(step("low_qkv"), 1)
            nc.vector.tensor_copy(e_qkv[:], pb[RANK_BANK][0:3 * RANK, 0:TOK]).then_inc(step("e_qkv"), 1)
            extra_by_bit1()
            dve.wait_ge(step("qkv_psum"), 1)
            nc.vector.tensor_scalar(av[:], pb[QKV_BANK][0:TOK, :], 1.0 / 3.0, None, ALU.mult).then_inc(step("av"), 1)
            turned("a", at, pb[TURN_BANK])
            dve.wait_ge(step("low_o"), 1)
            nc.vector.tensor_copy(e_small[:, 0], pb[RANK_BANK][0:RANK, 0:TOK]).then_inc(step("e_o"), 1)
            extra_by_bit2()
            dve.wait_ge(step("o_psum_t"), 1)
            nc.vector.tensor_tensor(y[:], pb[WO_BANK][0:TOK, :], z[:], ALU.add).then_inc(step("y"), 1)
            turned("y", yt, pb[TURN_BANK])
            dve.wait_ge(step("low_gu"), 2)
            nc.vector.tensor_copy(e_small[:, 1:3], pb[RANK_BANK][0:RANK, 0:2 * TOK].rearrange(
                "p (j t) -> p j t", j=2)).then_inc(step("e_gu"), 1)
            nc.vector.tensor_tensor(y_xa[:], y[:], xa[:], ALU.add).then_inc(step("y_plus_xa"), 1)
            extra_by_bit3()

            def gated_t(c):
                dve.wait_ge(step("h_turned"), c + 1)
                nc.vector.tensor_copy(ht[:, 2 * c:2 * c + 2, :],
                                      pb[c % 2][:, 0:2 * TOK].rearrange("p (k t) -> p k t", k=2)).then_inc(
                    step("h_t"), 1)

            for c in range(GU_COLS):
                bank = pb[GU_BANKS[c % 2]]
                dve.wait_ge(step("exp_gate"), c + 1)
                nc.vector.tensor_scalar(gate[:, c % 2, 1], gate[:, c % 2, 0], 1.0, None, ALU.add).then_inc(
                    step("one_plus"), 1)
                dve.wait_ge(step("one_plus"), c + 1)
                nc.vector.reciprocal(gate[:, c % 2, 2], gate[:, c % 2, 1]).then_inc(step("sigmoid"), 1)
                dve.wait_ge(step("sigmoid"), c + 1)
                nc.vector.tensor_tensor(gate[:, c % 2, 3], gate[:, c % 2, 2], bank[0:TOK, 0:2 * P],
                                        ALU.mult).then_inc(step("silu"), 1)
                dve.wait_ge(step("silu"), c + 1)
                if c >= 2:
                    dve.wait_ge(step("h_turned"), c - 1)
                nc.vector.tensor_tensor(gate[:, c % 2, 4], gate[:, c % 2, 3], bank[0:TOK, 2 * P:4 * P],
                                        ALU.mult).then_inc(step("h_ready"), 1)
                if c >= 1:
                    gated_t(c - 1)
            gated_t(GU_COLS - 1)
            dve.wait_ge(step("low_d"), 1)
            nc.vector.tensor_copy(e_small[:, 3], pb[RANK_BANK][0:RANK, 0:TOK]).then_inc(step("e_d"), 1)
            dve.wait_ge(step("y_plus_xa"), 1)
            dve.wait_ge(step("d_psum"), 1)
            nc.vector.tensor_tensor(xb[:], pb[DOWN_BANK][0:TOK, :], y_xa[:], ALU.add).then_inc(step("rows1"), 1)
            norm(1, xb[:], z2[:])
            dve.wait_ge(late_in, 16 * len(late))
            nc.vector.tensor_tensor(sums[:], xb[:], bb_sb[:], ALU.add).then_inc(step("with_bb"), 1)
            turned("z2", z2t, pb[TURN_BANK])
            dve.wait_ge(step("low_f"), 1)
            nc.vector.tensor_copy(e_f[:], pb[RANK_BANK][0:RR, 0:TOK]).then_inc(step("e_f"), 1)
            dve.wait_ge(step("f_psum"), 1)
            dve.wait_ge(step("with_bb"), 1)
            nc.vector.tensor_tensor(res[:], pb[WO_BANK][0:TOK, :], sums[:], ALU.add).then_inc(step("final"), 1)

        @block.tensor
        def _(pe):
            used = [0]

            def stream(dst, lhs, first, last=False):
                n = used[0]
                used[0] += 1
                pe.wait_ge(w_in[n % WB], 16 * (n // WB + 1))
                for j in range(2):
                    m = nc.tensor.matmul(dst, lhs[j], wring[:, n % WB, j], start=(first and j == 0),
                                         stop=(last and j == 1))
                m.then_inc(w_used, 1)

            def turn(name, src, dst):
                for k in range(KT):
                    m = nc.tensor.transpose(dst[:, k * TOK:(k + 1) * TOK], src[:, k * P:(k + 1) * P],
                                            ident[0:TOK, 0:TOK])
                m.then_inc(step(f"{name}_turned"), 1)

            def into_rank(dst, lhs, rhs, name):
                for k in range(len(lhs)):
                    m = nc.tensor.matmul(dst, lhs[k], rhs[k], start=(k == 0), stop=(k == len(lhs) - 1))
                m.then_inc(step(name), 1)

            wo_psum, qkv_psum = pb[WO_BANK][0:TOK, :], pb[QKV_BANK][0:TOK, :]
            down_psum = pb[DOWN_BANK][0:TOK, :]
            def turn_attention(h):
                pe.wait_ge(step("divided"), h + 1)
                if h >= 2:
                    pe.wait_ge(step("attn_t"), h - 1)
                for r in range(RT):
                    m = nc.tensor.transpose(pb[h % 2][:, r * P:(r + 1) * P], acc[:, h, r, :], ident[:])
                m.then_inc(step("attn_turned"), 1)

            turn_attention(0)
            for h in range(NKV):
                if h + 1 < NKV:
                    turn_attention(h + 1)
                pe.wait_ge(step("attn_t"), h + 1)
                for g in range(0, G, 2):
                    stream(wo_psum, [ot[:, h, (g + j) * TOK:(g + j + 1) * TOK] for j in range(2)], h + g == 0,
                           h == NKV - 1 and g == G - 2)
            used[0] += 3 * KT // 2
            pe.wait_ge(step("normed0"), 1)
            turn("z", z, pb[TURN_BANK])
            pe.wait_ge(small_in, 16 * len(smalls))
            pe.wait_ge(step("z_t"), 1)
            into_rank(pb[RANK_BANK][0:3 * RANK, 0:TOK], [la[:, k, 0:3 * RANK] for k in range(KT)],
                      [zt[:, k] for k in range(KT)], "low_qkv")
            for k in range(KT):
                pe.wait_ge(step("qkv_summed"), k // 2 + 1)
                nc.tensor.matmul(qkv_psum, zt[:, k], qkv_sum[:, k], start=(k == 0), stop=False)
            pe.wait_ge(step("e_qkv"), 1)
            nc.tensor.matmul(qkv_psum, e_qkv[:], lb_qkv[:], start=False, stop=True).then_inc(step("qkv_psum"), 1)
            pe.wait_ge(step("av"), 1)
            turn("a", av, pb[TURN_BANK])
            pe.wait_ge(step("a_t"), 1)
            into_rank(pb[RANK_BANK][0:RANK, 0:TOK], [la[:, k, 3 * RANK:4 * RANK] for k in range(KT)],
                      [at[:, k] for k in range(KT)], "low_o")
            for n in range(KT // 2):
                stream(wo_psum, [at[:, 2 * n + j] for j in range(2)], n == 0)
            pe.wait_ge(step("e_o"), 1)
            nc.tensor.matmul(wo_psum, e_small[:, 0], lb_o[:], start=False, stop=True).then_inc(step("o_psum_t"), 1)
            pe.wait_ge(step("y"), 1)
            turn("y", y, pb[TURN_BANK])
            pe.wait_ge(step("y_t"), 1)
            yts = [yt[:, k] for k in range(KT)]
            for j in range(2):
                into_rank(pb[RANK_BANK][0:RANK, j * TOK:(j + 1) * TOK],
                          [la[:, k, (4 + j) * RANK:(5 + j) * RANK] for k in range(KT)], yts, "low_gu")

            def turn_gated(c):
                pe.wait_ge(step("h_ready"), c + 1)
                if c >= 2:
                    pe.wait_ge(step("h_t"), c - 1)
                for j in range(2):
                    m = nc.tensor.transpose(pb[c % 2][:, j * TOK:(j + 1) * TOK], gate[:, c % 2, 4, j * P:(j + 1) * P],
                                            ident[0:TOK, 0:TOK])
                m.then_inc(step("h_turned"), 1)

            for c in range(GU_COLS):
                bank = pb[GU_BANKS[c % 2]]
                if c >= 2:
                    pe.wait_ge(step("h_ready"), c - 1)
                for n in range(KT // 2):
                    stream(bank[0:TOK, :], yts[2 * n:2 * n + 2], n == 0)
                pe.wait_ge(step("e_gu"), 1)
                for j in range(2):
                    m = nc.tensor.matmul(bank[0:TOK, j * 2 * P:(j + 1) * 2 * P], e_small[:, 1 + j],
                                         lb_gu[:, j, c * 2 * P:(c + 1) * 2 * P], start=False, stop=(j == 1))
                m.then_inc(step("gu_psum"), 1)
                if c >= 1:
                    turn_gated(c - 1)
            for n in range((FT - EXTRA) // 2):
                pe.wait_ge(step("h_t"), n + 1)
                stream(down_psum, [ht[:, 2 * n + j] for j in range(2)], n == 0)
                if n == 2:
                    turn_gated(GU_COLS - 1)
            pe.wait_ge(step("h_t"), GU_COLS)
            pe.wait_ge(late_in, 16 * len(late))
            into_rank(pb[RANK_BANK][0:RANK, 0:TOK], [lad[:, t] for t in range(FT)], [ht[:, t] for t in range(FT)],
                      "low_d")
            pe.wait_ge(step("extra_ready"), 1)
            for e in range(EXTRA):
                nc.tensor.matmul(down_psum, ht[:, FT - EXTRA + e], x_leaf[:, 1, e * TW:(e + 1) * TW], start=False,
                                 stop=False)
            pe.wait_ge(step("e_d"), 1)
            nc.tensor.matmul(down_psum, e_small[:, 3], lb_d[:], start=False, stop=True).then_inc(step("d_psum"), 1)
            pe.wait_ge(step("normed1"), 1)
            turn("z2", z2, pb[TURN_BANK])
            pe.wait_ge(step("z2_t"), 1)
            into_rank(pb[RANK_BANK][0:RR, 0:TOK], [en[:, k] for k in range(KT)], [z2t[:, k] for k in range(KT)],
                      "low_f")
            for k in range(KT):
                nc.tensor.matmul(wo_psum, z2t[:, k], wb[:, k], start=(k == 0), stop=False)
            pe.wait_ge(step("e_f"), 1)
            nc.tensor.matmul(wo_psum, e_f[:], w_four[:], start=False, stop=True).then_inc(step("f_psum"), 1)


def fourier_matrix(n):
    t = np.arange(n)
    rows = np.zeros((n, n))
    rows[0] = 1.0 / np.sqrt(n)
    for f in range(1, (n - 1) // 2 + 1):
        rows[2 * f - 1] = np.sqrt(2.0 / n) * np.cos(2 * np.pi * f * t / n)
        rows[2 * f] = np.sqrt(2.0 / n) * np.sin(2 * np.pi * f * t / n)
    rows[n - 1] = (1.0 - 2.0 * (t % 2)) / np.sqrt(n)
    return rows.astype(np.float32)


def kernel(**inputs):
    import numpy as _np
    import concourse.bacc as _bacc
    from concourse import mybir as _mybir
    from concourse.bass_utils import run_bass_kernel_spmd as _run

    a = {k: _np.asarray(v) for k, v in inputs.items()}

    def k_tiles(m):
        return m.reshape(-1, P, m.shape[1]).transpose(1, 0, 2)

    def weight_tiles(m):
        o, i = m.shape
        return m.T.reshape(i // P, P, o // TW, TW).transpose(0, 2, 1, 3).reshape(-1, P, TW)

    def scale_tiles(m):
        o, b = m.shape
        return m.T.reshape(b // 2, 2, o // TW, TW).transpose(0, 2, 1, 3).reshape(-1, 2, TW)

    def all_tiles(f, att, gate_up, down):
        both = gate_up.reshape(2, GU_COLS, TW // 2, -1).transpose(1, 0, 2, 3).reshape(GU_COLS, TW, -1)
        return _np.concatenate([f(m) for m in att] + [f(m) for m in both] + [f(down)])

    lb_gu = a["L0_attn_lora_B_gu"]
    lb = _np.zeros((6 * RANK, FFN), _np.float32)
    for m in range(4):
        lb[m * RANK:(m + 1) * RANK, 0:HID] = a["L0_attn_lora_B_attn"][m].T
    for m in range(2):
        lb[(4 + m) * RANK:(5 + m) * RANK] = lb_gu[m].T
    coefs = _np.concatenate([a["L0_ffn_coefs0"], a["L0_ffn_coefs1"]], 2)
    mask = _np.concatenate([a["L0_ffn_mask0"], a["L0_ffn_mask1"]], 2)
    laid = {
        "x": a["x"].reshape(TOK, HID),
        "ctx_t": a["ctx_4096"].reshape(NCH, CHUNK, KT, P).transpose(0, 2, 3, 1),
        "wq": k_tiles(a["L0_xattn_Wq"]),
        "bq": a["L0_xattn_bq"].reshape(NH, D).T,
        "wkv": k_tiles(a["L0_xattn_Wkv"]),
        "bk": a["L0_xattn_bkv"][:NKV * D].reshape(NKV, D).T,
        "bv": a["L0_xattn_bkv"][NKV * D:].reshape(NKV, D).T,
        "wo": a["L0_xattn_Wo"].reshape(NH, D, HID),
        "bo": a["L0_xattn_bo"],
        "codes": all_tiles(weight_tiles, a["L0_attn_codes_attn"], a["L0_attn_codes_gu"], a["L0_attn_codes_down"]),
        "scales": all_tiles(scale_tiles, a["L0_attn_scales_attn"], a["L0_attn_scales_gu"], a["L0_attn_scales_down"]),
        "lora_a": k_tiles(a["L0_attn_lora_A_h"].reshape(6 * RANK, HID).T),
        "lora_a_down": k_tiles(a["L0_attn_lora_A_down"].T),
        "lora_b": lb,
        "lora_b_down": a["L0_attn_lora_B_down"].T,
        "w_base": k_tiles(a["L0_ffn_W_base"].T),
        "b_base": a["L0_ffn_b_base"],
        "enc": k_tiles(_np.concatenate([a["L0_ffn_enc0"], a["L0_ffn_enc1"]], 0).T),
        "coefs": coefs.transpose(1, 0, 2).reshape(KT, P, NEXP, RR).transpose(1, 0, 2, 3),
        "mask": mask.transpose(1, 0, 2).reshape(KT, P, NEXP, RR).transpose(1, 0, 2, 3),
        "fourier": k_tiles(fourier_matrix(HID)),
        "ident": _np.eye(P, dtype=_np.float32),
    }
    nc = _bacc.Bacc("TRN2", target_bir_lowering=False, num_devices=1)
    arrays, args = {}, []
    for name, m in laid.items():
        m = _np.ascontiguousarray(m)
        arrays[f"in_{name}"] = m
        args.append(nc.dram_tensor(f"in_{name}", m.shape, _mybir.dt.from_np(m.dtype), kind="ExternalInput").ap())
    args.append(nc.dram_tensor("out_x", (TOK, HID), _mybir.dt.float32, kind="ExternalOutput").ap())
    perceiver_block(nc, *args)
    r = _run(nc, [arrays], core_ids=[0])
    return r.results[0]["out_x"].reshape(1, TOK, HID)
```
